# Optimizing a Trainium2 kernel written in Bass

```python
import numpy as np
import jax
import jax.numpy as jnp

def _softmax(x, axis=-1):
    return jax.nn.softmax(x, axis=axis)

def _gelu(x):
    return jax.nn.gelu(x, approximate=True)

def _silu(x):
    return jax.nn.silu(x)

def _sigmoid(x):
    return jax.nn.sigmoid(x)

def _layernorm(x, axis=-1, eps=1e-05):
    m = jnp.mean(x, axis=axis, keepdims=True)
    v = jnp.var(x, axis=axis, keepdims=True)
    return (x - m) / jnp.sqrt(v + eps)

def _scatter_add(tgt, idx, src, axis=0):
    return tgt.at[idx].add(src)

def _segment_sum(src, seg, n):
    return jax.ops.segment_sum(src, seg, n)
kernel_name = 'mk_prb_d1_jaxref_r8_63bb06'

def setup_inputs(seed: int=0):
    np.random.seed(seed)
    _w = jnp.asarray

    def _L0_attn_setup():
        import jax, jax.numpy as jnp
        import numpy as np
        HIDDEN = 256
        INTER = 512
        HEADS = 32
        HEAD_DIM = INTER // HEADS
        STATE = 128
        GROUPS = 1
        CONV_K = 4
        CHUNK = 32
        EPS = 1e-05
        CONV_DIM = INTER + 2 * GROUPS * STATE
        DT_MIN, DT_MAX = (0.0, 100.0)
        BATCH, SEQ = (2, 512)

        def _segment_sum(x):
            T = x.shape[-1]
            xx = jnp.broadcast_to(x[..., None], x.shape + (T,))
            mask_lower = jnp.tril(jnp.ones((T, T), bool), -1)
            xx = jnp.where(mask_lower, xx, 0.0)
            seg = jnp.cumsum(xx, axis=-2)
            mask_incl = jnp.tril(jnp.ones((T, T), bool), 0)
            return jnp.where(mask_incl, seg, -jnp.inf)
        key = jax.random.key(seed)
        ks = jax.random.split(key, 8)
        std = 0.02
        return {'hidden_states': jax.random.normal(ks[0], (BATCH, SEQ, HIDDEN), jnp.float32), 'in_proj_w': jax.random.normal(ks[1], (INTER + CONV_DIM + HEADS, HIDDEN), jnp.float32) * std, 'conv_w': jax.random.normal(ks[2], (CONV_DIM, 1, CONV_K), jnp.float32) * std, 'conv_b': jnp.zeros((CONV_DIM,), jnp.float32), 'A_log': jnp.log(jax.random.uniform(ks[3], (HEADS,), jnp.float32, 1.0, 16.0)), 'dt_bias': jax.random.normal(ks[4], (HEADS,), jnp.float32) * 0.1, 'D': jnp.ones((HEADS,), jnp.float32), 'norm_w': jnp.ones((INTER,), jnp.float32), 'out_proj_w': jax.random.normal(ks[5], (HIDDEN, INTER), jnp.float32) * (std / np.sqrt(48.0))}
    _L0_attn_in = _L0_attn_setup()

    def _L0_ffn_setup():
        import jax, jax.numpy as jnp
        import numpy as np
        HIDDEN = 256
        INTER = 1024
        COMPRESSION = 128.9

        def _n_ctrl(out_size, in_size):
            return max(16, int(out_size * in_size / COMPRESSION))

        def _catmull_rom_grid(n_ctrl, n_samples):
            t = np.linspace(0.0, n_ctrl - 1.0, n_samples, dtype=np.float64)
            i = np.clip(np.floor(t).astype(np.int64), 0, n_ctrl - 2)
            f = (t - i).astype(np.float32)
            idx = np.stack([np.clip(i + k, 0, n_ctrl - 1) for k in (-1, 0, 1, 2)], axis=0)
            return (jnp.asarray(idx.astype(np.int32)), jnp.asarray(f))

        def spline_reconstruct(control_points, out_size, in_size):
            n = out_size * in_size
            idx, f = _catmull_rom_grid(control_points.shape[0], n)
            p0, p1, p2, p3 = (control_points[idx[0]], control_points[idx[1]], control_points[idx[2]], control_points[idx[3]])
            f2 = f * f
            f3 = f2 * f
            w = 0.5 * (2.0 * p1 + (p2 - p0) * f + (2.0 * p0 - 5.0 * p1 + 4.0 * p2 - p3) * f2 + (3.0 * p1 - p0 - 3.0 * p2 + p3) * f3)
            return w.reshape(out_size, in_size)
        key = jax.random.key(seed)
        k0, k1, k2, k3 = jax.random.split(key, 4)
        hidden_states = jax.random.normal(k0, (4, 256, HIDDEN), dtype=jnp.float32)
        gate_cp = jax.random.normal(k1, (_n_ctrl(INTER, HIDDEN),), dtype=jnp.float32) * 0.02
        up_cp = jax.random.normal(k2, (_n_ctrl(INTER, HIDDEN),), dtype=jnp.float32) * 0.02
        down_cp = jax.random.normal(k3, (_n_ctrl(HIDDEN, INTER),), dtype=jnp.float32) * 0.02
        return {'hidden_states': hidden_states, 'gate_cp': gate_cp, 'up_cp': up_cp, 'down_cp': down_cp}
    _L0_ffn_in = _L0_ffn_setup()
    _d = {'L0_attn_hidden_states': _L0_attn_in['hidden_states'], 'L0_attn_in_proj_w': _L0_attn_in['in_proj_w'], 'L0_attn_conv_w': _L0_attn_in['conv_w'], 'L0_attn_conv_b': _L0_attn_in['conv_b'], 'L0_attn_A_log': _L0_attn_in['A_log'], 'L0_attn_dt_bias': _L0_attn_in['dt_bias'], 'L0_attn_D': _L0_attn_in['D'], 'L0_attn_norm_w': _L0_attn_in['norm_w'], 'L0_attn_out_proj_w': _L0_attn_in['out_proj_w'], 'L0_ffn_gate_cp': _L0_ffn_in['gate_cp'], 'L0_ffn_up_cp': _L0_ffn_in['up_cp'], 'L0_ffn_down_cp': _L0_ffn_in['down_cp']}
    _x0 = _d['L0_attn_hidden_states']
    _d['L0_attn_hidden_states'] = jax.random.normal(jax.random.fold_in(jax.random.key(seed), 1), (2, 2048, 256), dtype=_x0.dtype)
    del _x0
    return _d

def reference(L0_attn_hidden_states, L0_attn_in_proj_w, L0_attn_conv_w, L0_attn_conv_b, L0_attn_A_log, L0_attn_dt_bias, L0_attn_D, L0_attn_norm_w, L0_attn_out_proj_w, L0_ffn_gate_cp, L0_ffn_up_cp, L0_ffn_down_cp):

    def _L0_attn_ref(hidden_states, in_proj_w, conv_w, conv_b, A_log, dt_bias, D, norm_w, out_proj_w):
        import jax, jax.numpy as jnp
        import numpy as np
        HIDDEN = 256
        INTER = 512
        HEADS = 32
        HEAD_DIM = INTER // HEADS
        STATE = 128
        GROUPS = 1
        CONV_K = 4
        CHUNK = 32
        EPS = 1e-05
        CONV_DIM = INTER + 2 * GROUPS * STATE
        DT_MIN, DT_MAX = (0.0, 100.0)
        BATCH, SEQ = (2, 512)

        def _segment_sum(x):
            T = x.shape[-1]
            xx = jnp.broadcast_to(x[..., None], x.shape + (T,))
            mask_lower = jnp.tril(jnp.ones((T, T), bool), -1)
            xx = jnp.where(mask_lower, xx, 0.0)
            seg = jnp.cumsum(xx, axis=-2)
            mask_incl = jnp.tril(jnp.ones((T, T), bool), 0)
            return jnp.where(mask_incl, seg, -jnp.inf)
        b, s, _ = hidden_states.shape
        proj = hidden_states @ in_proj_w.T
        gate, hBC, dt = jnp.split(proj, [INTER, INTER + CONV_DIM], axis=-1)
        x = jnp.transpose(hBC, (0, 2, 1))
        x = jax.lax.conv_general_dilated(x, conv_w, window_strides=(1,), padding=[(CONV_K - 1, 0)], dimension_numbers=('NCH', 'OIH', 'NCH'), feature_group_count=CONV_DIM)
        x = x + conv_b[None, :, None]
        hBC = jax.nn.silu(jnp.transpose(x, (0, 2, 1)))
        xs, B, C = jnp.split(hBC, [INTER, INTER + GROUPS * STATE], axis=-1)
        A = -jnp.exp(A_log)
        dt = jnp.clip(jax.nn.softplus(dt + dt_bias), DT_MIN, DT_MAX)
        xs = xs.reshape(b, s, HEADS, HEAD_DIM)
        rep = HEADS // GROUPS
        Bm = jnp.repeat(B.reshape(b, s, GROUPS, STATE), rep, axis=2)
        Cm = jnp.repeat(C.reshape(b, s, GROUPS, STATE), rep, axis=2)
        pad = -s % CHUNK

        def padseq(t):
            return jnp.pad(t, ((0, 0), (0, pad)) + ((0, 0),) * (t.ndim - 2))
        D_res = D[None, None, :, None] * padseq(xs)
        xdt = padseq(xs * dt[..., None])
        Ad = padseq(A[None, None, :] * dt)
        Bm, Cm = (padseq(Bm), padseq(Cm))
        nc = (s + pad) // CHUNK
        xdt = xdt.reshape(b, nc, CHUNK, HEADS, HEAD_DIM)
        Ad = jnp.transpose(Ad.reshape(b, nc, CHUNK, HEADS), (0, 3, 1, 2))
        Bm = Bm.reshape(b, nc, CHUNK, HEADS, STATE)
        Cm = Cm.reshape(b, nc, CHUNK, HEADS, STATE)
        A_cum = jnp.cumsum(Ad, axis=-1)
        L = jnp.exp(_segment_sum(Ad))
        G = jnp.einsum('bclhn,bcshn->bclsh', Cm, Bm)
        M = G * jnp.transpose(L, (0, 2, 3, 4, 1))
        Y_diag = jnp.einsum('bclsh,bcshp->bclhp', M, xdt)
        decay_states = jnp.exp(A_cum[:, :, :, -1:] - A_cum)
        B_decay = Bm * jnp.transpose(decay_states, (0, 2, 3, 1))[..., None]
        states = jnp.einsum('bclhn,bclhp->bchpn', B_decay, xdt)
        states = jnp.concatenate([jnp.zeros_like(states[:, :1]), states], axis=1)
        chunk_sums = jnp.pad(A_cum[:, :, :, -1], ((0, 0), (0, 0), (1, 0)))
        decay_chunk = jnp.exp(_segment_sum(chunk_sums))
        decay_chunk = jnp.transpose(decay_chunk, (0, 2, 3, 1))
        new_states = jnp.einsum('bczh,bchpn->bzhpn', decay_chunk, states)
        states = new_states[:, :-1]
        state_decay = jnp.exp(A_cum)
        Y_off = jnp.einsum('bclhn,bchpn->bclhp', Cm, states) * jnp.transpose(state_decay, (0, 2, 3, 1))[..., None]
        y = (Y_diag + Y_off).reshape(b, nc * CHUNK, HEADS, HEAD_DIM) + D_res
        y = y[:, :s].reshape(b, s, INTER)
        y = y * jax.nn.silu(gate)
        var = jnp.mean(y * y, axis=-1, keepdims=True)
        y = y * jax.lax.rsqrt(var + EPS) * norm_w
        return y @ out_proj_w.T

    def _L0_ffn_ref(hidden_states, gate_cp, up_cp, down_cp):
        import jax, jax.numpy as jnp
        import numpy as np
        HIDDEN = 256
        INTER = 1024
        COMPRESSION = 128.9

        def _n_ctrl(out_size, in_size):
            return max(16, int(out_size * in_size / COMPRESSION))

        def _catmull_rom_grid(n_ctrl, n_samples):
            t = np.linspace(0.0, n_ctrl - 1.0, n_samples, dtype=np.float64)
            i = np.clip(np.floor(t).astype(np.int64), 0, n_ctrl - 2)
            f = (t - i).astype(np.float32)
            idx = np.stack([np.clip(i + k, 0, n_ctrl - 1) for k in (-1, 0, 1, 2)], axis=0)
            return (jnp.asarray(idx.astype(np.int32)), jnp.asarray(f))

        def spline_reconstruct(control_points, out_size, in_size):
            n = out_size * in_size
            idx, f = _catmull_rom_grid(control_points.shape[0], n)
            p0, p1, p2, p3 = (control_points[idx[0]], control_points[idx[1]], control_points[idx[2]], control_points[idx[3]])
            f2 = f * f
            f3 = f2 * f
            w = 0.5 * (2.0 * p1 + (p2 - p0) * f + (2.0 * p0 - 5.0 * p1 + 4.0 * p2 - p3) * f2 + (3.0 * p1 - p0 - 3.0 * p2 + p3) * f3)
            return w.reshape(out_size, in_size)
        gate_w = spline_reconstruct(gate_cp, INTER, HIDDEN)
        up_w = spline_reconstruct(up_cp, INTER, HIDDEN)
        down_w = spline_reconstruct(down_cp, HIDDEN, INTER)
        gate = jnp.einsum('bsh,ih->bsi', hidden_states, gate_w)
        up = jnp.einsum('bsh,ih->bsi', hidden_states, up_w)
        inter = jax.nn.silu(gate) * up
        return jnp.einsum('bsi,hi->bsh', inter, down_w)
    x = L0_attn_hidden_states
    xn = _layernorm(x, axis=-1)
    x = x + _L0_attn_ref(xn, L0_attn_in_proj_w, L0_attn_conv_w, L0_attn_conv_b, L0_attn_A_log, L0_attn_dt_bias, L0_attn_D, L0_attn_norm_w, L0_attn_out_proj_w) + _L0_ffn_ref(xn, L0_ffn_gate_cp, L0_ffn_up_cp, L0_ffn_down_cp)
    return x

_drawn_inputs = setup_inputs


def setup_inputs(seed=0):
    import zlib

    import numpy as np

    out = dict(_drawn_inputs(seed))
    spreads = {'L0_attn_conv_b': (0.0, 0.1), 'L0_attn_D': (1.0, 0.6), 'L0_attn_norm_w': (1.0, 0.6)}
    factors = {'L0_attn_conv_w': 6.514,
     'L0_attn_A_log': 8.0,
     'L0_attn_dt_bias': 8.0,
     'L0_ffn_up_cp': 3.12,
     'L0_ffn_down_cp': 3.294}
    for name, (base, spread) in spreads.items():
        noise = np.random.default_rng([zlib.crc32(name.encode()), seed]).standard_normal(out[name].shape)
        drawn = base * np.exp(spread * noise) if base else spread * noise
        out[name] = jnp.asarray(drawn.astype(out[name].dtype))
    for name, factor in factors.items():
        out[name] = (out[name] * factor).astype(out[name].dtype)
    return out
```

```python
from contextlib import ExitStack

import concourse.bass as bass
from concourse import mybir

ALU = mybir.AluOpType
ACT = mybir.ActivationFunctionType
F32 = mybir.dt.float32
F32R = mybir.dt.float32r
BF16 = mybir.dt.bfloat16

P = 128
BATCH, SEQ, HID = 2, 2048, 256
INTER, STATE, HEADS, CONV_K = 512, 128, 32, 4
HDIM = INTER // HEADS
FFN = 1024
EPS = 1e-5
DT_MAX = 100.0

ST_B = 256
ST = BATCH * ST_B
NST = SEQ // ST_B
NQ = ST // P
KT = HID // P
ZB = INTER // P
XB = INTER // P
CB = XB + 2
FB = FFN // P
G = 8
REP = 3
R3 = REP * HEADS

NCP = int(FFN * HID / 128.9)
NSAMP = FFN * HID
SEG = (NSAMP - 1) // (NCP - 1)
RPP = -(-(-(-NSAMP // SEG)) // P)
WROW = RPP * SEG

PJ = [("T", 0), ("T", 1), ("DT", 0), ("X", 0)]
for _j in range(FB):
    PJ += [("GATE", _j), ("UP", _j)]
    if _j + 1 < CB:
        PJ += [("X", _j + 1)]
PJ += [("Z", _j) for _j in range(ZB)]
NPJ = len(PJ)
BY_ACT = ("DT", "X")

FILL = {1: ("T", 0), 3: ("DT", 0), 4: ("X", 0), 6: ("GU", 0), 8: ("X", 1), 10: ("GU", 1), 12: ("DN", 0),
        13: ("X", 2), 15: ("GU", 2), 17: ("DN", 1), 18: ("X", 3), 20: ("GU", 3), 22: ("DN", 2), 23: ("X", 4),
        25: ("GU", 4), 27: ("DN", 3), 28: ("X", 5), 30: ("GU", 5), 31: ("DN", 4)}
SCAN_SLOT, DECAY_SLOT = 14, 17


def pj_index(kind, j):
    return PJ.index((kind, j))


def pj_bank(kind, j):
    return pj_index(kind, j) % 2


def pj_freed(upto, by_act):
    return sum((k in BY_ACT) == by_act for k, _ in PJ[:upto + 1])


N_ACT, N_DVE = pj_freed(NPJ - 1, True), pj_freed(NPJ - 1, False)


def cols(q):
    c = (q % BATCH) * ST_B + (q // BATCH) * P
    return slice(c, c + P)


def head(g, j):
    return 8 * (g // 2) + 2 * j + g % 2


def w_groups():
    out = []
    for kind in ("gate", "up"):
        for k in range(KT):
            for a in range(0, FB, 4):
                out.append((kind, [(a + i, k) for i in range(4)]))
    for a in range(0, FB, 2):
        out.append(("down", [(a + i, b) for i in range(2) for b in range(KT)]))
    return out


W_GROUPS = w_groups()
W_FIRST = {k: [g[0] for g in W_GROUPS].index(k) for k in ("gate", "up", "down")}
N_CONST = 9 + 2 * REP
OPN = FB + XB


class Steps:

    def __init__(self, eng, sem):
        self.eng, self.sem, self.n, self.seen = eng, sem, 0, 0

    def did(self, ins):
        self.n += 1
        ins.then_inc(self.sem, 1)
        return self.n

    def wait(self, n=None):
        n = self.n if n is None else n
        if n > self.seen:
            self.eng.wait_ge(self.sem, n)
            self.seen = n

    def restart(self):
        self.wait()
        if self.n:
            self.eng.sem_clear(self.sem)
        self.n = self.seen = 0


def mamba_ffn_kernel(nc, x, in_w, conv_w, conv_b, a_log, dt_bias, d_skip, norm_w, out_w, gate_cp, up_cp, down_cp,
                     frac, prev_mask, ident_c, ident_bc, future_c, head_c, feature_c, out):
    with ExitStack() as ctx:
        def sb(name, shape, dt=F32, c=ctx):
            return c.enter_context(nc.sbuf_tensor(name, shape, dt))

        def sem(name):
            return ctx.enter_context(nc.semaphore(name))

        NIN = INTER + CB * P + R3
        win_h, win_l = sb("win_h", [P, KT, NIN], F32R), sb("win_l", [P, KT, NIN], F32R)
        wgu_h, wgu_l = sb("wgu_h", [P, KT, 2 * FFN], F32R), sb("wgu_l", [P, KT, 2 * FFN], F32R)
        wdn_h, wdn_l = sb("wdn_h", [P, FB, HID], F32R), sb("wdn_l", [P, FB, HID], F32R)
        wo_h, wo_l = sb("wo_h", [P, XB, HID], F32R), sb("wo_l", [P, XB, HID], F32R)
        ident = sb("ident", [P, P])
        ident_b = sb("ident_b", [P, P], BF16)
        future = sb("future", [P, P], BF16)
        sel = sb("sel", [R3, HEADS], BF16)
        selq = sb("selq", [R3, INTER], BF16)
        ones = sb("ones", [P, P])
        half_neg = sb("half_neg", [P, NQ])
        eps_1 = sb("eps_1", [P, NQ])
        eps_n = sb("eps_n", [P, NQ])
        cw = sb("cw", [P, CB, CONV_K])
        cb = sb("cb", [P, CB])
        dtb = sb("dtb", [R3, 1])
        alog = sb("alog", [R3, 1])
        a_neg = sb("a_neg", [R3, 1])
        dsk = sb("dsk", [P, XB])
        nw = sb("nw", [P, XB])
        xin = sb("xin", [P, NQ, HID])
        stats = sb("stats", [P, NQ, 6])
        mv = sb("mv", [P, NQ, 2])
        rstd = sb("rstd", [P, NQ])
        xnt_h, xnt_l = sb("xnt_h", [P, KT, ST], F32R), sb("xnt_l", [P, KT, ST], F32R)
        pre = sb("pre", [P, 2, BATCH, CONV_K - 1 + ST_B])
        halo = sb("halo", [P, CB, BATCH, CONV_K - 1])
        acc = sb("acc", [P, CB, ST])
        u = sb("u", [P, CB, ST])
        th = sb("th", [P, 2, ST])
        gz = sb("gz", [P, ZB, ST])
        dz = sb("dz", [R3, ST])
        de = sb("de", [R3, ST])
        dl = sb("dl", [R3, ST])
        dw = sb("dw", [R3, ST])
        acum = sb("acum", [R3, ST])
        a3 = sb("a3", [R3, ST], BF16)
        a3n = sb("a3n", [R3, ST], BF16)
        e3 = sb("e3", [R3, ST], BF16)
        tt_f = sb("tt_f", [2 * HEADS, ST])
        res = sb("res", [P, NQ, HID])
        opn_h, opn_l = sb("opn_h", [P, 2, ST], F32R), sb("opn_l", [P, 2, ST], F32R)
        inter = sb("inter", [P, 2, ST])
        state = [sb(f"state{b}", [P, INTER]) for b in range(BATCH)]
        with ExitStack() as early:
            raw_in = sb("raw_in", [P, KT, NIN], c=early)
            raw_out = sb("raw_out", [P, XB, HID], c=early)
            fr = sb("fr", [P, RPP, SEG], c=early)
            mk = sb("mk", [P, RPP, 16], c=early)
            cpw = sb("cpw", [P, 3, RPP + 4], c=early)
            coef = sb("coef", [P, 4, RPP + 1], c=early)
            ctmp = sb("ctmp", [P, RPP + 1], c=early)
            wv = sb("wv", [P, RPP, SEG], c=early)
            wp = sb("wp", [P, RPP, 16], c=early)
        tt = sb("tt", [P, NQ, 2 * HEADS])
        gm = sb("gm", [P, NQ, P])
        e_sb = sb("e_sb", [P, XB, P])
        xpad = sb("xpad", [P, 2, HEADS, 2 * HDIM])
        xdec = sb("xdec", [P, 2, INTER])
        b_tok = sb("b_tok", [P, NQ, STATE])
        etot = sb("etot", [P, NQ, HEADS])
        lm = sb("lm", [P, 4, 4 * P])
        y = sb("y", [P, XB, ST])
        sqs = sb("sqs", [P, ST])
        ss_sb = sb("ss_sb", [P, NQ])
        rms = sb("rms", [P, NQ])
        raw_w = acc[:, :, :].rearrange("p a b -> p (a b)")[:, 0:FB * HID].rearrange("p (n h) -> p n h", h=HID)

        def weight_parts(kind, parts, ps):
            a0, b0 = parts[0]
            n = len(parts) * P
            if kind == "down":
                w = slice(a0, a0 + 2)
                return wdn_h[:, w, :], wdn_l[:, w, :], ps[:, :].rearrange("p (a h) -> p a h", a=2), 0.5
            o = (kind == "up") * FFN
            c = slice(o + a0 * P, o + a0 * P + n)
            return wgu_h[:, b0, c], wgu_l[:, b0, c], ps[:, 0:n], 1.0

        w_dram = [nc.dram_tensor(f"spline_w{i}", [P * WROW], F32, kind="Internal").ap() for i in range(3)]

        psum = [ctx.enter_context(nc.psum_tensor(f"ps{i}", [P, 512], F32)) for i in range(8)]
        pd = [psum[0][:].rearrange("p (t h) -> p t h", t=2), psum[1][:].rearrange("p (t h) -> p t h", t=2)]
        pj = [psum[2], psum[3]]
        pseg = [psum[4], psum[5]]
        py = psum[6]
        pm = psum[7]
        po = [psum[6][:].rearrange("p (t h) -> p t h", t=2), psum[7][:].rearrange("p (t h) -> p t h", t=2)]

        names = """ld_const ld_w0 ld_w1 ld_w2 ld_w3 ld_w4 ld_w5 ld_w6 st_w0 st_w1 st_w2 ld_x ld_res st_out
        set_w set_dve set_pool set_act w_trans in_high w_high w_low spline
        xn_ready var_ready rstd_ready xnt_high pj_done pj_act pj_dve
        pre_ready tap_done silu_tanh u_ready gate_tanh opn_high opn_low f_used o_used
        z_act dt_log ad_ready scan_done dt_ready decay_ready exp_acum a3_ready e3_ready
        tt_psum tt_ready g_psum gm_ready b_psum b_ready et_psum et_ready
        xt_psum xpad_ready xdec_ready seg_psum l_ready m_ready m_used
        e_psum e_ready o_psum y_off s_psum s_decayed s_ready y_psum y_sum
        y_gated sq_ready sqs_ready ss_psum ss_ready rms_ready evac_done final_done gz_ready
        pe_step act_step dve_step pool_step""".split()
        sm = {n: sem(n) for n in names}

        def rep(ap, n):
            return ap.unsqueeze(len(ap.shape)).broadcast_to(list(ap.shape) + [n])

        x_st = x.rearrange("b (s h p) c -> b s p h c", p=P, h=ST_B // P)
        out_st = out.rearrange("b (s h p) c -> b s p h c", p=P, h=ST_B // P)
        HB = ST_B // P
        WGRP = 20

        block = ctx.enter_context(nc.Block())

        @block.sync
        def _(sp):
            n = 0
            for i, cp in enumerate((gate_cp, up_cp, down_cp)):
                window = bass.AP(cp.tensor, 0, [[RPP, P], [1, RPP + 4]])
                sp.dma_start(cpw[:, i, :], window).then_inc(sm["ld_w6"], 16)
            sp.dma_start(fr[:], frac.rearrange("p (j r) -> p j r", r=SEG)).then_inc(sm["ld_w6"], 16)
            sp.dma_start(mk[:], prev_mask.rearrange("p (j r) -> p j r", r=16)).then_inc(sm["ld_w6"], 16)
            for dst, src in ((ident[:], ident_c), (ident_b[:], ident_bc), (future[:], future_c), (sel[:], head_c), (selq[:], feature_c),
                             (cw[:], conv_w.rearrange("p (j k) -> p j k", k=CONV_K)), (cb[:], conv_b),
                             (nw[:], norm_w), (dsk[:], d_skip)):
                sp.dma_start(dst, src).then_inc(sm["ld_const"], 16)
                n += 1
            for c in range(REP):
                rr = slice(c * HEADS, (c + 1) * HEADS)
                sp.dma_start(dtb[rr, :], dt_bias).then_inc(sm["ld_const"], 16)
                sp.dma_start(alog[rr, :], a_log).then_inc(sm["ld_const"], 16)
                n += 2
            assert n == N_CONST
            sp.dma_start(raw_in[:], in_w.rearrange("(k p) f -> p k f", p=P)).then_inc(sm["ld_w0"], 16)
            sp.dma_start(raw_out[:], out_w.rearrange("(j p) h -> p j h", p=P)).then_inc(sm["ld_w1"], 16)
            for b in range(BATCH):
                sp.dma_start(xin[:, b * HB:(b + 1) * HB, :], x_st[b, 0]).then_inc(sm["ld_x"], 16)
                sp.dma_start(res[:, b * HB:(b + 1) * HB, :], x_st[b, 0]).then_inc(sm["ld_res"], 16)
            for i in range(3):
                sp.wait_ge(sm["spline"], i + 1)
                sp.dma_start(w_dram[i].rearrange("(p n) -> p n", p=P),
                             wv[:].rearrange("p a b -> p (a b)")).then_inc(sm[f"st_w{i}"], 16)
                sp.wait_ge(sm[f"st_w{i}"], 16)
                if i:
                    sp.wait_ge(sm["w_trans"], W_FIRST[('gate', 'up', 'down')[i]])
                wide = HID if i < 2 else FFN
                src = w_dram[i][0:NSAMP].rearrange("(b p h) -> p b h", p=P, h=wide)
                dst = raw_w.rearrange("p n h -> p (n h)").rearrange("p (n h) -> p n h", h=wide)
                sp.dma_start(dst, src).then_inc(sm[f"ld_w{2 + i}"], 16)

            def load_x(s):
                sp.wait_ge(sm["pj_done"], NPJ * (s - 1) + KT)
                for b in range(BATCH):
                    sp.dma_start(xin[:, b * HB:(b + 1) * HB, :], x_st[b, s]).then_inc(sm["ld_x"], 16)

            def store(r):
                sp.wait_ge(sm["final_done"], r + 1)
                for b in range(BATCH):
                    sp.dma_start(out_st[b, r], res[:, b * HB:(b + 1) * HB, :]).then_inc(sm["st_out"], 16)
                sp.wait_ge(sm["st_out"], 32 * (r + 1))

            def load_res(s):
                for b in range(BATCH):
                    sp.dma_start(res[:, b * HB:(b + 1) * HB, :], x_st[b, s]).then_inc(sm["ld_res"], 16)

            load_x(1)
            with sp.Fori(1, NST - 1) as s:
                load_x(s + 1)
                store(s - 1)
                load_res(s)
            store(NST - 2)
            load_res(NST - 1)
            store(NST - 1)

        @block.tensor
        def _(pe):
            pe.wait_ge(sm["ld_const"], 16 * N_CONST)
            for n, (kind, parts) in enumerate(W_GROUPS):
                if n >= 8:
                    pe.wait_ge(sm["w_low"], n - 7)
                pe.wait_ge(sm[f"ld_w{2 + ('gate', 'up', 'down').index(kind)}"], 16)
                for i, (a, b) in enumerate(parts):
                    if kind == "down":
                        src = raw_w.rearrange("p n h -> p (n h)")[:, b * FFN + a * P:b * FFN + (a + 1) * P]
                    else:
                        src = raw_w[:, a, b * P:(b + 1) * P]
                    last = nc.tensor.transpose(psum[n % 8][:, i * P:(i + 1) * P], src, ident[:])
                last.then_inc(sm["w_trans"], 1)

            def pj_free(s, B, kind, j):
                n = pj_index(kind, j)
                if n >= 2:
                    k = PJ[n - 2][0] in BY_ACT
                    pe.wait_ge(sm["pj_act" if k else "pj_dve"], (N_ACT if k else N_DVE) * s + pj_freed(n - 2, k))
                elif B:
                    pe.wait_ge(sm["pj_dve"], N_DVE * s)
                else:
                    pe.wait_ge(sm["w_low"], len(W_GROUPS))

            def project(s, B, kind, j, w_h, w_l, c0, m):
                pj_free(s, B, kind, j)
                bank = pj[pj_bank(kind, j)]
                n = 0
                for k in range(KT):
                    for w, a in ((w_h, xnt_h), (w_h, xnt_l), (w_l, xnt_h)):
                        last = nc.tensor.matmul(bank[0:m, :], w[:, k, c0:c0 + m], a[:, k, :],
                                                start=(n == 0), stop=(n == 3 * KT - 1))
                        n += 1
                last.then_inc(sm["pj_done"], 1)

            def fill(s, B, kind, j):
                if kind == "T":
                    pe.wait_ge(sm["xn_ready"], s * NQ + NQ)
                    for k in range(KT):
                        pj_free(s, B, "T", k)
                        for t in range(NQ):
                            last = nc.tensor.transpose(pj[k][:, t * P:(t + 1) * P],
                                                       xin[:, t, k * P:(k + 1) * P], ident[:])
                        last.then_inc(sm["pj_done"], 1)
                elif kind == "DT":
                    pe.wait_ge(sm["pj_dve"], N_DVE * s + KT)
                    project(s, B, "DT", 0, win_h, win_l, INTER + CB * P, R3)
                elif kind == "X":
                    project(s, B, "X", j, win_h, win_l, INTER + j * P, P)
                elif kind == "Z":
                    project(s, B, "Z", j, win_h, win_l, j * P, P)
                elif kind == "GU":
                    project(s, B, "GATE", j, wgu_h, wgu_l, j * P, P)
                    project(s, B, "UP", j, wgu_h, wgu_l, FFN + j * P, P)
                elif kind == "DN":
                    pe.wait_ge(sm["opn_low"], OPN * s + j + 1 - (0 if not B else XB))
                    if j == 0:
                        if B:
                            pe.wait_ge(sm["evac_done"], s)
                    down(j, j, wdn_h, wdn_l, pd, j == 0, j == FB - 1, "f_used")

            def down(slot, j, w_h, w_l, banks, first, final, used):
                for t in range(NQ):
                    tc = slice(t * P, (t + 1) * P)
                    for n, (a, w) in enumerate(((opn_h, w_h), (opn_h, w_l), (opn_l, w_h))):
                        last = nc.tensor.matmul(banks[t // 2][:, t % 2, :], a[:, slot % 2, tc], w[:, j, :],
                                                start=(first and t % 2 == 0 and n == 0), stop=(final and n == 2),
                                                skip_group_check=True)
                last.then_inc(sm[used], 1)

            def seg(r, k):
                q, g = divmod(k, G)
                bank = pseg[k % 2]
                if k == 0:
                    pe.wait_ge(sm["a3_ready"], r + 1)
                if k >= 2:
                    pe.wait_ge(sm["l_ready"], 32 * r + k - 1)
                c = cols(q)
                heads = sel[:, 8 * (g // 2) + g % 2:8 * (g // 2) + 8:2]
                nc.tensor.matmul(bank[:, :].rearrange("p (h l) -> p h l", h=4), a3n[:, c], rep(heads, P),
                                 start=True, stop=False, skip_group_check=True)
                nc.tensor.matmul(bank[:, :].rearrange("p (h l) -> p h l", h=4), ident_b[:],
                                 future[:].unsqueeze(1).broadcast_to([P, 4, P]),
                                 start=False, stop=False, skip_group_check=True)
                for j in range(4):
                    h = head(g, j)
                    last = nc.tensor.matmul(bank[:, j * P:(j + 1) * P], sel[:, h:h + 1].broadcast_to([R3, P]), a3[:, c],
                                            start=False, stop=True, skip_group_check=True)
                last.then_inc(sm["seg_psum"], 1)

            def yd(r, k):
                q, g = divmod(k, G)
                pe.wait_ge(sm["m_ready"], 32 * r + k + 1)
                if g == 0:
                    pe.wait_ge(sm["xpad_ready"], NQ * r + q + 1)
                    if q:
                        pe.wait_ge(sm["y_sum"], NQ * r + q)
                for j in range(4):
                    last = nc.tensor.matmul(py[32 * j:32 * j + 32, (g // 2) * P:(g // 2 + 1) * P],
                                            xpad[:, q % 2, head(g, j), :], lm[:, k % 4, j * P:(j + 1) * P],
                                            start=(g % 2 == 0), stop=(g % 2 == 1), skip_group_check=True)
                last.then_inc(sm["m_used"], 1)

            def x_tok(s, q):
                for j in range(XB):
                    last = nc.tensor.transpose(pm[:, j * P:(j + 1) * P], u[:, j, cols(q)], ident[:])
                last.then_inc(sm["xt_psum"], 1)

            def a2(s, B):
                pe.wait_ge(sm["u_ready"], CB * s + CB)
                if B:
                    pe.wait_ge(sm["final_done"], s)
                for q in range(NQ):
                    last = nc.tensor.matmul(pm[:, q * P:(q + 1) * P], u[:, XB, cols(q)], u[:, XB + 1, cols(q)],
                                            start=True, stop=True)
                last.then_inc(sm["g_psum"], 1)
                pe.wait_ge(sm["gm_ready"], s + 1)
                for q in range(NQ):
                    last = nc.tensor.transpose(pm[:, q * P:(q + 1) * P], u[:, XB, cols(q)], ident[:])
                last.then_inc(sm["b_psum"], 1)
                pe.wait_ge(sm["b_ready"], s + 1)
                pe.wait_ge(sm["dt_ready"], s + 1)
                pe.wait_ge(sm["decay_ready"], s + 1)
                for q in range(NQ):
                    last = nc.tensor.matmul(pm[:, q * 2 * HEADS:(q + 1) * 2 * HEADS], tt_f[:, cols(q)],
                                            ident[0:2 * HEADS, 0:2 * HEADS], start=True, stop=True)
                last.then_inc(sm["tt_psum"], 1)
                pe.wait_ge(sm["tt_ready"], s + 1)
                pe.wait_ge(sm["e3_ready"], s + 1)
                for q in range(NQ):
                    last = nc.tensor.matmul(pm[:, q * HEADS:(q + 1) * HEADS], e3[:, cols(q).stop - 1:cols(q).stop].broadcast_to([R3, P]),
                                            sel[:, :], start=True, stop=True)
                last.then_inc(sm["et_psum"], 1)
                pe.wait_ge(sm["et_ready"], s + 1)
                x_tok(s, 0)

            def body(s, A, B):
                r = s - 1
                for k in range(NQ * G):
                    q, g = divmod(k, G)
                    if B:
                        seg(r, k)
                    if A and k in FILL:
                        fill(s, B, *FILL[k])
                    if B:
                        if k:
                            yd(r, k - 1)
                        if g == 1:
                            pe.wait_ge(sm["xpad_ready"], NQ * r + q + 1)
                            for j in range(XB):
                                last = nc.tensor.matmul(pm[:, j * P:(j + 1) * P], selq[:, j * P:(j + 1) * P],
                                                        e3[:, cols(q)], start=True, stop=True)
                            last.then_inc(sm["e_psum"], 1)
                        if g == 3:
                            pe.wait_ge(sm["e_ready"], NQ * r + q + 1)
                            if q >= 2:
                                pe.wait_ge(sm["s_ready"], NQ * r + q - 1)
                            for j in range(XB):
                                last = nc.tensor.matmul(pm[:, j * P:(j + 1) * P],
                                                        state[q % BATCH][:, j * P:(j + 1) * P],
                                                        u[:, XB + 1, cols(q)], start=True, stop=True)
                            last.then_inc(sm["o_psum"], 1)
                        if g == 5:
                            pe.wait_ge(sm["y_off"], NQ * r + q + 1)
                            pe.wait_ge(sm["xdec_ready"], NQ * r + q + 1)
                            nc.tensor.matmul(pm[:, :], b_tok[:, q, :], xdec[:, q % 2, :],
                                             start=True, stop=True).then_inc(sm["s_psum"], 1)
                        if g == 7 and q < NQ - 1:
                            pe.wait_ge(sm["s_ready"], NQ * r + q + 1)
                            x_tok(r, q + 1)
                if B:
                    yd(r, NQ * G - 1)
                if A:
                    for it in (("GU", 6), ("DN", 5), ("GU", 7), ("DN", 6), ("DN", 7)):
                        fill(s, B, *it)
                if B:
                    pe.wait_ge(sm["y_sum"], NQ * r + NQ)
                    pe.wait_ge(sm["s_ready"], NQ * r + NQ)
                    for j in range(XB):
                        pe.wait_ge(sm["opn_low"], OPN * (r + 1) + FB * A - XB + j + 1)
                        down(j, j, wo_h, wo_l, po, j == 0, j == XB - 1, "o_used")
                    pe.wait_ge(sm["sqs_ready"], r + 1)
                    pe.wait_ge(sm["l_ready"], 32 * (r + 1))
                    for t in range(NQ):
                        last = nc.tensor.matmul(pseg[0][:, t:t + 1], sqs[:, t * P:(t + 1) * P], ones[:, 0:1],
                                                start=True, stop=True)
                    last.then_inc(sm["ss_psum"], 1)
                if A:
                    for j in range(ZB):
                        fill(s, B, "Z", j)
                    a2(s, B)

            body(0, True, False)
            with pe.Fori(1, NST) as s:
                body(s, True, True)
            body(NST, False, True)

        @block.scalar
        def _(act):
            st = Steps(act, sm["act_step"])
            act.wait_ge(sm["ld_const"], 16 * N_CONST)
            nc.scalar.activation(a_neg[:], alog[:], ACT.Exp).then_inc(sm["set_act"], 1)
            act.wait_ge(sm["ld_w0"], 16)
            nc.scalar.activation(win_h[:], raw_in[:], ACT.Copy).then_inc(sm["in_high"], 1)
            act.wait_ge(sm["ld_w1"], 16)
            for j in range(XB):
                nc.scalar.activation(wo_h[:, j, :], raw_out[:, j, :], ACT.Identity,
                                     scale=nw[:, j:j + 1]).then_inc(sm["in_high"], 1)
            for n, (kind, parts) in enumerate(W_GROUPS):
                act.wait_ge(sm["w_trans"], n + 1)
                w_h, w_l, ps, scale = weight_parts(kind, parts, psum[n % 8])
                nc.scalar.activation(w_h, ps, ACT.Copy, scale=scale).then_inc(sm["w_high"], 1)

            def t_free(s, B, i):
                if i < 2:
                    if B:
                        act.wait_ge(sm["u_ready"], CB * s)
                elif i - 2 < FB + ZB:
                    kind, j = ("GATE", i - 2) if i - 2 < FB else ("Z", i - 2 - FB)
                    act.wait_ge(sm["pj_dve"], N_DVE * s + pj_freed(pj_index(kind, j), False))
                else:
                    act.wait_ge(sm["u_ready"], CB * s + i - 1 - FB - ZB)

            def operand_free(s, B, i, f):
                if f and i >= 2:
                    act.wait_ge(sm["f_used"], FB * s + i - 1)
                if not f:
                    if i >= 2:
                        act.wait_ge(sm["o_used"], XB * s + i - 1)

            def early(s, B, kind, j):
                if kind == "T":
                    for k in range(KT):
                        act.wait_ge(sm["pj_done"], NPJ * s + k + 1)
                        nc.scalar.activation(xnt_h[:, k, :], pj[k][:], ACT.Copy).then_inc(sm["xnt_high"], 1)
                elif kind == "DT":
                    act.wait_ge(sm["pj_done"], NPJ * s + pj_index("DT", 0) + 1)
                    nc.scalar.activation(dz[:], pj[pj_bank("DT", 0)][0:R3, :], ACT.Identity,
                                         bias=dtb[:]).then_inc(sm["pj_act"], 1)
                    act.wait_ge(sm["pj_act"], N_ACT * s + 1)
                    st.did(nc.scalar.activation(dw[:], dz[:], ACT.Abs))
                    st.wait()
                    st.did(nc.scalar.activation(de[:], dw[:], ACT.Exp, scale=-1.0))
                    st.wait()
                    nc.scalar.activation(dl[:], de[:], ACT.Ln, bias=1.0).then_inc(sm["dt_log"], 1)
                elif kind == "X":
                    act.wait_ge(sm["pj_done"], NPJ * s + pj_index("X", j) + 1)
                    if j >= 2 or B:
                        act.wait_ge(sm["tap_done"], CB * s + j - 1)
                    bank = pj[pj_bank("X", j)]
                    nc.scalar.activation(pre[:, j % 2, :, CONV_K - 1:],
                                         bank[:].rearrange("p (b t) -> p b t", b=BATCH),
                                         ACT.Copy).then_inc(sm["pre_ready"], 1)
                    nc.scalar.activation(acc[:, j, :], bank[:], ACT.Identity, bias=cb[:, j:j + 1],
                                         scale=cw[:, j, CONV_K - 1:CONV_K]).then_inc(sm["pj_act"], 1)
                elif kind == "GU":
                    act.wait_ge(sm["pj_done"], NPJ * s + pj_index("GATE", j) + 1)
                    t_free(s, B, j)
                    nc.scalar.activation(th[:, j % 2, :], pj[pj_bank("GATE", j)][:], ACT.Tanh,
                                         scale=0.5).then_inc(sm["gate_tanh"], 1)
                elif kind == "Z":
                    act.wait_ge(sm["pj_done"], NPJ * s + pj_index("Z", j) + 1)
                    t_free(s, B, FB + j)
                    nc.scalar.activation(th[:, (FB + j) % 2, :], pj[pj_bank("Z", j)][:], ACT.Tanh,
                                         scale=0.5).then_inc(sm["gate_tanh"], 1)

            def late(s, B, kind, j):
                if kind == "GU":
                    act.wait_ge(sm["pj_dve"], N_DVE * s + pj_freed(pj_index("UP", j), False))
                    operand_free(s, B, j, True)
                    nc.scalar.activation(opn_h[:, j % 2, :], inter[:, j % 2, :],
                                         ACT.Copy).then_inc(sm["opn_high"], 1)

            def body(s, A, B):
                r = s - 1
                for k in range(NQ * G + 2):
                    q, g = divmod(k, G)
                    if B and k < NQ * G:
                        act.wait_ge(sm["seg_psum"], 32 * r + k + 1)
                        if k >= 4:
                            act.wait_ge(sm["m_used"], 32 * r + k - 3)
                        nc.scalar.activation(lm[:, k % 4, :], pseg[k % 2][:], ACT.Exp).then_inc(sm["l_ready"], 1)
                        if g == 2:
                            act.wait_ge(sm["e_psum"], NQ * r + q + 1)
                            if q:
                                act.wait_ge(sm["y_off"], NQ * r + q)
                            nc.scalar.activation(e_sb[:].rearrange("p a b -> p (a b)"), pm[:],
                                                 ACT.Copy).then_inc(sm["e_ready"], 1)
                    if A and k - 2 in FILL:
                        late(s, B, *FILL[k - 2])
                    if A and k in FILL:
                        early(s, B, *FILL[k])
                    if A and k == DECAY_SLOT:
                        act.wait_ge(sm["scan_done"], s + 1)
                        for t in range(NQ):
                            c = slice(t * P, (t + 1) * P)
                            last = nc.scalar.activation(tt_f[HEADS:2 * HEADS, c], acum[HEADS:2 * HEADS, c], ACT.Exp,
                                                        scale=-1.0,
                                                        bias=acum[HEADS:2 * HEADS, c.stop - 1:c.stop])
                        last.then_inc(sm["decay_ready"], 1)
                        nc.scalar.activation(dl[:], acum[:], ACT.Exp).then_inc(sm["exp_acum"], 1)
                if A:
                    early(s, B, "GU", 6)
                    early(s, B, "GU", 7)
                    late(s, B, "GU", 6)
                    late(s, B, "GU", 7)
                if B:
                    for j in range(XB):
                        act.wait_ge(sm["y_gated"], XB * r + j + 1)
                        if j < 2:
                            if A:
                                act.wait_ge(sm["f_used"], FB * s + FB - 1 + j)
                        else:
                            act.wait_ge(sm["o_used"], XB * r + j - 1)
                        nc.scalar.activation(opn_h[:, j % 2, :], y[:, j, :], ACT.Copy).then_inc(sm["opn_high"], 1)
                        nc.scalar.activation(gz[:, j, :], y[:, j, :], ACT.Square,
                                             scale=0.5).then_inc(sm["sq_ready"], 1)
                    act.wait_ge(sm["ss_psum"], r + 1)
                    nc.scalar.activation(ss_sb[:], pseg[0][:, 0:NQ], ACT.Copy).then_inc(sm["ss_ready"], 1)
                if A:
                    for j in range(ZB):
                        early(s, B, "Z", j)
                    for j in range(CB):
                        act.wait_ge(sm["pj_act"], N_ACT * s + N_ACT)
                        act.wait_ge(sm["tap_done"], CB * s + CB)
                        t_free(s, B, FB + ZB + j)
                        nc.scalar.activation(th[:, (FB + ZB + j) % 2, :], acc[:, j, :], ACT.Tanh,
                                             scale=0.5).then_inc(sm["silu_tanh"], 1)
                    act.wait_ge(sm["g_psum"], s + 1)
                    nc.scalar.activation(gm[:].rearrange("p q l -> p (q l)"), pm[:], ACT.Copy,
                                         scale=0.25).then_inc(sm["gm_ready"], 1)
                    act.wait_ge(sm["b_psum"], s + 1)
                    nc.scalar.activation(b_tok[:].rearrange("p a b -> p (a b)"), pm[:],
                                         ACT.Copy).then_inc(sm["b_ready"], 1)
                    act.wait_ge(sm["tt_psum"], s + 1)
                    nc.scalar.activation(tt[:].rearrange("p a b -> p (a b)"), pm[:, 0:NQ * 2 * HEADS],
                                         ACT.Copy).then_inc(sm["tt_ready"], 1)
                    act.wait_ge(sm["et_psum"], s + 1)
                    nc.scalar.activation(etot[:].rearrange("p a b -> p (a b)"), pm[:, 0:NQ * HEADS],
                                         ACT.Copy).then_inc(sm["et_ready"], 1)
                st.restart()

            body(0, True, False)
            with act.Fori(1, NST) as s:
                body(s, True, True)
            body(NST, False, True)

        @block.vector
        def _(dve):
            st = Steps(dve, sm["dve_step"])

            def link(ins):
                st.did(ins)
                st.wait()

            V = nc.vector
            V.memset(ones[:], 1.0).then_inc(sm["set_dve"], 1)
            V.memset(halo[:].rearrange("p a b c -> p (a b c)"), 0.0).then_inc(sm["set_dve"], 1)
            for b in range(BATCH):
                V.memset(state[b][:], 0.0).then_inc(sm["set_dve"], 1)
            for t, v in ((half_neg, -0.5), (eps_1, EPS), (eps_n, EPS * INTER)):
                V.memset(t[:], v).then_inc(sm["set_dve"], 1)
            dve.wait_ge(sm["ld_const"], 16 * N_CONST)
            link(V.tensor_scalar(dsk[:], dsk[:], 0.5, None, ALU.mult))

            def spline(i):
                p0, p1, p2, p3 = (cpw[:, i, k:k + RPP + 1] for k in range(4))
                c0, c1, c2, c3 = (coef[:, k, :] for k in range(4))
                tmp = ctmp[:]
                link(V.tensor_copy(c0, p1))
                link(V.tensor_tensor(tmp, p2, p0, ALU.subtract))
                link(V.tensor_scalar(c1, tmp, 0.5, None, ALU.mult))
                link(V.scalar_tensor_tensor(tmp, p0, 2.0, p3, ALU.mult, ALU.subtract))
                link(V.scalar_tensor_tensor(tmp, p1, -5.0, tmp, ALU.mult, ALU.add))
                link(V.scalar_tensor_tensor(tmp, p2, 4.0, tmp, ALU.mult, ALU.add))
                link(V.tensor_scalar(c2, tmp, 0.5, None, ALU.mult))
                link(V.tensor_tensor(tmp, p3, p0, ALU.subtract))
                link(V.scalar_tensor_tensor(tmp, p1, 3.0, tmp, ALU.mult, ALU.add))
                link(V.scalar_tensor_tensor(tmp, p2, -3.0, tmp, ALU.mult, ALU.add))
                link(V.tensor_scalar(c3, tmp, 0.5, None, ALU.mult))

                def horner(dst, f, m0, n):
                    c = [rep(coef[:, k, m0:m0 + RPP], n) for k in range(4)]
                    link(V.tensor_tensor(dst, f, c[3], ALU.mult))
                    link(V.tensor_tensor(dst, dst, c[2], ALU.add))
                    link(V.tensor_tensor(dst, dst, f, ALU.mult))
                    link(V.tensor_tensor(dst, dst, c[1], ALU.add))
                    link(V.tensor_tensor(dst, dst, f, ALU.mult))
                    link(V.tensor_tensor(dst, dst, c[0], ALU.add))

                if i:
                    dve.wait_ge(sm[f"st_w{i - 1}"], 16)
                horner(wv[:], fr[:], 1, SEG)
                horner(wp[:], fr[:, :, 0:16], 0, 16)
                link(V.tensor_tensor(wp[:], wp[:], wv[:, :, 0:16], ALU.subtract))
                link(V.tensor_tensor(wp[:], wp[:], mk[:], ALU.mult))
                V.tensor_tensor(wv[:, :, 0:16], wv[:, :, 0:16], wp[:], ALU.add).then_inc(sm["spline"], 1)
                dve.wait_ge(sm["spline"], i + 1)

            def weights(n0, n1):
                for n in range(n0, n1):
                    kind, parts = W_GROUPS[n]
                    dve.wait_ge(sm["w_high"], n + 1)
                    w_h, w_l, ps, scale = weight_parts(kind, parts, psum[n % 8])
                    V.scalar_tensor_tensor(w_l, ps, scale, w_h.bitcast(F32), ALU.mult,
                                           ALU.subtract).then_inc(sm["w_low"], 1)

            dve.wait_ge(sm["ld_w6"], 16 * 5)
            spline(0)
            dve.wait_ge(sm["in_high"], 1 + XB)
            link(V.tensor_tensor(win_l[:], raw_in[:], win_h[:].bitcast(F32), ALU.subtract))
            for j in range(XB):
                V.scalar_tensor_tensor(wo_l[:, j, :], raw_out[:, j, :], nw[:, j:j + 1], wo_h[:, j, :].bitcast(F32),
                                       ALU.mult, ALU.subtract)
            spline(1)
            weights(W_FIRST["gate"], W_FIRST["up"])
            spline(2)
            weights(W_FIRST["up"], len(W_GROUPS))
            dve.wait_ge(sm["w_low"], len(W_GROUPS))

            V.memset(xpad[:].rearrange("p a b c -> p (a b c)"), 0.0).then_inc(sm["set_dve"], 1)
            dve.wait_ge(sm["set_dve"], 8)
            st.restart()

            def layer_norm(s):
                dve.wait_ge(sm["ld_x"], 32 * s + 32)
                for t in range(NQ):
                    st.did(V.bn_stats(stats[:, t, :], xin[:, t, :]))
                st.wait()
                for t in range(NQ):
                    last = V.bn_aggr(mv[:, t, :], stats[:, t, :])
                last.then_inc(sm["var_ready"], 1)

            def normalize(s):
                dve.wait_ge(sm["rstd_ready"], s + 1)
                for t in range(NQ):
                    V.tensor_scalar(xin[:, t, :], xin[:, t, :], mv[:, t, 0:1], rstd[:, t:t + 1],
                                    ALU.subtract, ALU.mult).then_inc(sm["xn_ready"], 1)

            def early(s, B, kind, j):
                if kind == "T":
                    for k in range(KT):
                        dve.wait_ge(sm["xnt_high"], KT * s + k + 1)
                        V.tensor_tensor(xnt_l[:, k, :], pj[k][:], xnt_h[:, k, :].bitcast(F32),
                                        ALU.subtract).then_inc(sm["pj_dve"], 1)
                elif kind == "X":
                    dve.wait_ge(sm["pre_ready"], CB * s + j + 1)
                    sl = pre[:, j % 2]
                    link(V.tensor_copy(sl[:, :, 0:CONV_K - 1], halo[:, j]))
                    dve.wait_ge(sm["pj_act"], N_ACT * s + pj_freed(pj_index("X", j), True))
                    a = acc[:, j, :].rearrange("p (b t) -> p b t", b=BATCH)
                    for k in range(CONV_K - 2, -1, -1):
                        ins = V.scalar_tensor_tensor(a, sl[:, :, k:k + ST_B], cw[:, j, k:k + 1], a, ALU.mult, ALU.add)
                        link(ins)
                    V.tensor_copy(halo[:, j], sl[:, :, ST_B:]).then_inc(sm["tap_done"], 1)
                elif kind == "GU":
                    dve.wait_ge(sm["gate_tanh"], (FB + ZB) * s + j + 1)
                    st.wait()
                    V.scalar_tensor_tensor(inter[:, j % 2, :], th[:, j % 2, :], 1.0,
                                           pj[pj_bank("GATE", j)][:], ALU.add,
                                           ALU.mult).then_inc(sm["pj_dve"], 1)
                    dve.wait_ge(sm["pj_dve"], N_DVE * s + pj_freed(pj_index("GATE", j), False))
                    dve.wait_ge(sm["pj_done"], NPJ * s + pj_index("UP", j) + 1)
                    V.tensor_tensor(inter[:, j % 2, :], inter[:, j % 2, :], pj[pj_bank("UP", j)][:],
                                    ALU.mult).then_inc(sm["pj_dve"], 1)
                elif kind == "Z":
                    dve.wait_ge(sm["gate_tanh"], (FB + ZB) * s + FB + j + 1)
                    V.scalar_tensor_tensor(gz[:, j, :], th[:, (FB + j) % 2, :], 1.0, pj[pj_bank("Z", j)][:],
                                           ALU.add, ALU.mult).then_inc(sm["pj_dve"], 1)

            def late(s, B, kind, j):
                if kind == "GU":
                    dve.wait_ge(sm["opn_high"], OPN * s + j + 1 - (XB if B else 0))
                    V.tensor_tensor(opn_l[:, j % 2, :], inter[:, j % 2, :], opn_h[:, j % 2, :].bitcast(F32),
                                    ALU.subtract).then_inc(sm["opn_low"], 1)

            def pad_x(s, q):
                dve.wait_ge(sm["xt_psum"], NQ * s + q + 1)
                if q == 0:
                    dve.wait_ge(sm["tt_ready"], s + 1)
                dst = bass.AP(xpad, (q % 2) * 2 * INTER,
                              [[4 * INTER, P], [4 * HDIM, HEADS // 2], [3 * HDIM, 2], [1, HDIM]])
                V.tensor_tensor(dst, pm[:].rearrange("p (a b c) -> p a b c", a=HEADS // 2, b=2),
                                rep(tt[:, q, 0:HEADS], HDIM).rearrange("p (a b) c -> p a b c", b=2),
                                ALU.mult).then_inc(sm["xpad_ready"], 1)

            def y_sum(r, q):
                dve.wait_ge(sm["m_used"], 32 * r + G * q + G)
                dve.wait_ge(sm["y_off"], NQ * r + q + 1)
                V.tensor_tensor(y[:, :, cols(q)], y[:, :, cols(q)], py[:].rearrange("p (a l) -> p a l", a=XB),
                                ALU.add).then_inc(sm["y_sum"], 1)

            def body(s, A, B):
                r = s - 1
                if A:
                    layer_norm(s)
                for k in range(NQ * G + 3):
                    q, g = divmod(k, G)
                    if B and k < NQ * G:
                        dve.wait_ge(sm["l_ready"], 32 * r + k + 1)
                        slot = lm[:, k % 4, :].rearrange("p (h l) -> p h l", h=4)
                        V.tensor_tensor(slot, slot, gm[:, q, :].unsqueeze(1).broadcast_to([P, 4, P]),
                                        ALU.mult).then_inc(sm["m_ready"], 1)
                        if g == 0 and q:
                            y_sum(r, q - 1)
                        if g == 4:
                            dve.wait_ge(sm["o_psum"], NQ * r + q + 1)
                            dve.wait_ge(sm["e_ready"], NQ * r + q + 1)
                            V.tensor_tensor(y[:, :, cols(q)], pm[:].rearrange("p (a l) -> p a l", a=XB), e_sb[:],
                                            ALU.mult).then_inc(sm["y_off"], 1)
                        if g == 6:
                            dve.wait_ge(sm["s_psum"], NQ * r + q + 1)
                            dve.wait_ge(sm["s_decayed"], NQ * r + q + 1)
                            V.tensor_tensor(state[q % 2][:], state[q % 2][:], pm[:],
                                            ALU.add).then_inc(sm["s_ready"], 1)
                        if g == 7 and q < NQ - 1:
                            pad_x(r, q + 1)
                        if k == 2:
                            dve.wait_ge(sm["ld_res"], 32 * r + 32)
                            dve.wait_ge(sm["f_used"], FB * r + FB)
                            for t in range(2):
                                last = V.tensor_tensor(res[:, 2 * t:2 * t + 2, :], res[:, 2 * t:2 * t + 2, :], pd[t],
                                                       ALU.add)
                            last.then_inc(sm["evac_done"], 1)
                    if A and k == 0:
                        normalize(s)
                    if A and k - 3 in FILL:
                        late(s, B, *FILL[k - 3])
                    if A and k - 1 in FILL:
                        early(s, B, *FILL[k - 1])
                    if A and k == SCAN_SLOT:
                        dve.wait_ge(sm["ad_ready"], s + 1)
                        for t in range(NQ):
                            c = slice(t * P, (t + 1) * P)
                            last = V.tensor_tensor_scan(acum[:, c], ones[0:R3, :], de[:, c], 0.0, ALU.mult, ALU.add)
                        last.then_inc(sm["scan_done"], 1)
                if A:
                    early(s, B, "GU", 6)
                if B:
                    y_sum(r, NQ - 1)
                    dve.wait_ge(sm["y_sum"], NQ * r + NQ)
                    for j in range(XB):
                        link(V.scalar_tensor_tensor(y[:, j, :], u[:, j, :], dsk[:, j:j + 1], y[:, j, :],
                                                    ALU.mult, ALU.add))
                        V.tensor_tensor(y[:, j, :], y[:, j, :], gz[:, j, :], ALU.mult).then_inc(sm["y_gated"], 1)
                if A:
                    late(s, B, "GU", 6)
                    early(s, B, "GU", 7)
                    late(s, B, "GU", 7)
                if B:
                    for j in range(XB):
                        dve.wait_ge(sm["opn_high"], OPN * (r + 1) + FB * A - XB + j + 1)
                        V.tensor_tensor(opn_l[:, j % 2, :], y[:, j, :], opn_h[:, j % 2, :].bitcast(F32),
                                        ALU.subtract).then_inc(sm["opn_low"], 1)
                    dve.wait_ge(sm["evac_done"], r + 1)
                    dve.wait_ge(sm["rms_ready"], r + 1)
                    dve.wait_ge(sm["o_used"], XB * r + XB)
                    for t in range(NQ):
                        last = V.scalar_tensor_tensor(res[:, t, :], po[t // 2][:, t % 2, :], rms[:, t:t + 1],
                                                      res[:, t, :], ALU.mult, ALU.add)
                    last.then_inc(sm["final_done"], 1)
                if A:
                    for j in range(ZB):
                        early(s, B, "Z", j)
                    for j in range(CB):
                        i = FB + ZB + j
                        dve.wait_ge(sm["silu_tanh"], CB * s + j + 1)
                        V.scalar_tensor_tensor(u[:, j, :], th[:, i % 2, :], 1.0, acc[:, j, :],
                                               ALU.add, ALU.mult).then_inc(sm["u_ready"], 1)
                    pad_x(s, 0)
                st.restart()

            body(0, True, False)
            with dve.Fori(1, NST) as s:
                body(s, True, True)
            body(NST, False, True)

        @block.gpsimd
        def _(pool):
            st = Steps(pool, sm["pool_step"])
            Gp = nc.gpsimd

            def link(ins):
                st.did(ins)
                st.wait()

            pool.wait_ge(sm["set_act"], 1)
            pool.wait_ge(sm["set_dve"], 7)
            link(Gp.tensor_scalar(a_neg[:], a_neg[:], -1.0, None, ALU.mult))

            def split3(dst, src, tmp):
                link(Gp.tensor_tensor(dst[:], src[:], ones[0:R3, 0:1].broadcast_to([R3, ST]), ALU.mult))
                m = 2 * HEADS
                link(Gp.tensor_tensor(tmp[0:m, :], src[0:m, :], dst[0:m, :], ALU.subtract))
                link(Gp.tensor_scalar(dst[0:m, :], tmp[0:m, :], 1.0, None, ALU.mult))
                m = HEADS
                link(Gp.tensor_tensor(tmp[0:m, :], tmp[0:m, :], dst[0:m, :], ALU.subtract))
                return Gp.tensor_scalar(dst[0:m, :], tmp[0:m, :], 1.0, None, ALU.mult)

            def ssd_tile(r, q):
                pool.wait_ge(sm["xpad_ready"], NQ * r + q + 1)
                if q >= 2:
                    pool.wait_ge(sm["s_psum"], NQ * r + q - 1)
                src = bass.AP(xpad, (q % 2) * 2 * INTER,
                              [[4 * INTER, P], [4 * HDIM, HEADS // 2], [3 * HDIM, 2], [1, HDIM]])
                Gp.tensor_tensor(xdec[:, q % 2, :].rearrange("p (a b c) -> p a b c", b=2, c=HDIM), src,
                                 rep(tt[:, q, HEADS:], HDIM).rearrange("p (a b) c -> p a b c", b=2),
                                 ALU.mult).then_inc(sm["xdec_ready"], 1)
                pool.wait_ge(sm["o_psum"], NQ * r + q + 1)
                b = q % BATCH
                Gp.tensor_tensor(state[b][:].rearrange("p (h c) -> p h c", c=HDIM),
                                 state[b][:].rearrange("p (h c) -> p h c", c=HDIM),
                                 rep(etot[:, q, :], HDIM), ALU.mult).then_inc(sm["s_decayed"], 1)

            def body(s, A, B):
                r = s - 1
                if A:
                    pool.wait_ge(sm["var_ready"], s + 1)
                    link(Gp.tensor_tensor(rstd[:], mv[:, :, 1], eps_1[:], ALU.add))
                    Gp.tensor_tensor(rstd[:], rstd[:], half_neg[:], ALU.pow).then_inc(sm["rstd_ready"], 1)
                if B:
                    ssd_tile(r, 0)
                if A:
                    pool.wait_ge(sm["dt_log"], s + 1)
                    one = ones[0:R3, 0:1].broadcast_to([R3, ST])
                    link(Gp.tensor_tensor(dw[:], de[:], one, ALU.add))
                    link(Gp.tensor_scalar(dw[:], dw[:], 1.0, None, ALU.subtract))
                    link(Gp.tensor_tensor(dw[:], de[:], dw[:], ALU.subtract))
                    link(Gp.tensor_scalar(dz[:], dz[:], 0.0, None, ALU.max))
                    link(Gp.tensor_tensor(dw[:], dw[:], dl[:], ALU.add))
                    link(Gp.tensor_tensor(dz[:], dz[:], dw[:], ALU.add))
                    link(Gp.tensor_scalar(dz[:], dz[:], 0.0, DT_MAX, ALU.max, ALU.min))
                    Gp.tensor_scalar(de[:], dz[:], a_neg[:], None, ALU.mult).then_inc(sm["ad_ready"], 1)
                    Gp.tensor_scalar(tt_f[0:HEADS, :], dz[0:HEADS, :], 0.5, None, ALU.mult).then_inc(sm["dt_ready"], 1)
                if B:
                    for q in range(1, NQ):
                        ssd_tile(r, q)
                if A:
                    pool.wait_ge(sm["exp_acum"], s + 1)
                    if B:
                        pool.wait_ge(sm["seg_psum"], 32 * s)
                        pool.wait_ge(sm["e_psum"], NQ * s)
                    link(split3(a3, acum, dw))
                    Gp.tensor_scalar(a3n[:], a3[:], -1.0, None, ALU.mult).then_inc(sm["a3_ready"], 1)
                if B:
                    for j in range(XB):
                        pool.wait_ge(sm["sq_ready"], XB * r + j + 1)
                        if j == 1:
                            link(Gp.tensor_tensor(sqs[:], gz[:, 0, :], gz[:, 1, :], ALU.add))
                        if j == 2:
                            link(Gp.tensor_tensor(sqs[:], sqs[:], gz[:, 2, :], ALU.add))
                        if j == 3:
                            Gp.tensor_tensor(sqs[:], sqs[:], gz[:, 3, :], ALU.add).then_inc(sm["sqs_ready"], 1)
                    pool.wait_ge(sm["ss_ready"], r + 1)
                    link(Gp.tensor_tensor(rms[:], ss_sb[:], eps_n[:], ALU.add))
                    link(Gp.tensor_tensor(rms[:], rms[:], half_neg[:], ALU.pow))
                    Gp.tensor_scalar(rms[:], rms[:], 0.5 * INTER ** 0.5, None, ALU.mult).then_inc(sm["rms_ready"], 1)
                if A:
                    split3(e3, dl, dw).then_inc(sm["e3_ready"], 1)
                st.restart()

            body(0, True, False)
            with pool.Fori(1, NST) as s:
                body(s, True, True)
            body(NST, False, True)


def _constants():
    import numpy as np

    t = np.linspace(0.0, NCP - 1.0, NSAMP, dtype=np.float64)
    seg = np.clip(np.floor(t).astype(np.int64), 0, NCP - 2)
    f = (t - seg).astype(np.float32)
    n = np.arange(P * WROW)
    row, r = n // SEG, n % SEG
    real = n < NSAMP
    n = np.minimum(n, NSAMP - 1)
    prev = row - seg[n]
    assert np.isin(prev[real], (0, 1)).all() and (r[real & (prev == 1)] < 16).all()
    frac = np.where(real, f[n], np.float32(0)).astype(np.float32).reshape(P, WROW)
    mask = (real & (prev == 1)).astype(np.float32).reshape(P, RPP, SEG)[:, :, :16].reshape(P, RPP * 16)
    ident = np.eye(P, dtype=np.float32)
    bf16 = np.dtype("bfloat16")
    future = np.tril(np.full((P, P), -1e38, np.float32), -1).astype(bf16)
    row_of = np.tile(np.eye(HEADS, dtype=np.float32), (REP, 1))
    feature = np.repeat(row_of * np.float32(0.25), HDIM, axis=1).astype(bf16)
    return {"frac": frac, "prev_mask": np.ascontiguousarray(mask), "ident": ident,
            "ident_b": ident.astype(bf16), "future": future,
            "head": row_of.astype(bf16), "feature": feature}


def _layouts(w):
    import numpy as np

    def by_block(v):
        return np.ascontiguousarray(v.reshape(-1, P).T)

    in_w = w["in_proj_w"].T
    dt_w = in_w[:, -HEADS:]
    return {
        "hidden_states": w["hidden_states"],
        "in_proj_w": np.ascontiguousarray(np.concatenate([in_w[:, :-HEADS]] + [dt_w] * REP, axis=1)),
        "conv_w": np.ascontiguousarray(w["conv_w"].reshape(-1, P, CONV_K).transpose(1, 0, 2).reshape(P, -1)),
        "conv_b": by_block(w["conv_b"]),
        "A_log": w["A_log"].reshape(-1, 1),
        "dt_bias": w["dt_bias"].reshape(-1, 1),
        "D": by_block(np.repeat(w["D"], HDIM)),
        "norm_w": by_block(w["norm_w"]),
        "out_proj_w": np.ascontiguousarray(w["out_proj_w"].T),
    }


_INS = ["hidden_states", "in_proj_w", "conv_w", "conv_b", "A_log", "dt_bias", "D", "norm_w", "out_proj_w"]


def kernel(**inputs):
    import numpy as np
    import concourse.bacc as bacc
    from concourse.bass_utils import run_bass_kernel_spmd as run

    nc = bacc.Bacc("TRN2", target_bir_lowering=False, num_devices=1)
    arrays = _layouts({n: np.asarray(inputs[f"L0_attn_{n}"]) for n in _INS})
    for n in ("gate_cp", "up_cp", "down_cp"):
        cp = np.asarray(inputs[f"L0_ffn_{n}"])
        arrays[n] = np.concatenate([cp[:1]] * 2 + [cp] + [cp[-1:]] * (RPP * P + 4 - 2 - NCP))
    arrays.update(_constants())
    args = [nc.dram_tensor(f"in_{n}", a.shape, mybir.dt.from_np(a.dtype), kind="ExternalInput").ap()
            for n, a in arrays.items()]
    out = nc.dram_tensor("out_0", (BATCH, SEQ, HID), F32, kind="ExternalOutput").ap()
    mamba_ffn_kernel(nc, *args, out)
    r = run(nc, [{f"in_{n}": a for n, a in arrays.items()}], core_ids=[0])
    return r.results[0]["out_0"]
```

```python
from contextlib import ExitStack

import concourse.bass as bass
from concourse import mybir

ALU = mybir.AluOpType
ACT = mybir.ActivationFunctionType
F32 = mybir.dt.float32
F32R = mybir.dt.float32r
BF16 = mybir.dt.bfloat16

P = 128
BATCH, SEQ, HID = 2, 2048, 256
INTER, STATE, HEADS, CONV_K = 512, 128, 32, 4
HDIM = INTER // HEADS
FFN = 1024
EPS = 1e-5
DT_MAX = 100.0

ST_B = 256
ST = BATCH * ST_B
NST = SEQ // ST_B
NQ = ST // P
KT = HID // P
ZB = INTER // P
XB = INTER // P
CB = XB + 2
FB = FFN // P
G = 8
REP = 3
R3 = REP * HEADS

NCP = int(FFN * HID / 128.9)
NSAMP = FFN * HID
SEG = (NSAMP - 1) // (NCP - 1)
RPP = -(-(-(-NSAMP // SEG)) // P)
WROW = RPP * SEG

FILL_SSD = {0: ("T", 0), 1: ("DT", 0), 2: ("X", 0), 4: ("GU", 0), 6: ("X", 1), 8: ("GU", 1), 9: ("DN", 0),
            11: ("X", 2), 13: ("GU", 2), 15: ("DN", 1), 16: ("X", 3), 18: ("GU", 3), 20: ("DN", 2), 21: ("X", 4),
            23: ("GU", 4), 25: ("DN", 3), 26: ("X", 5), 28: ("GU", 5), 30: ("DN", 4)}
FILL_ALONE = dict(enumerate([
    ("T", 0), ("DT", 0), ("X", 0), ("X", 1), ("X", 2), ("X", 3), ("W", "gate"), ("X", 4), ("X", 5), ("Z", 0),
    ("C", 4), ("W", "up"), ("C", 5), ("GU", 0), ("C", 0), ("Z", 1), ("GU", 1), ("C", 1), ("Z", 2), ("W", "down"),
    ("GU", 2), ("DN", 0), ("C", 2), ("Z", 3), ("GU", 3), ("DN", 1), ("C", 3), ("GU", 4), ("DN", 2), ("GU", 5),
    ("DN", 3), ("GU", 6), ("DN", 4), ("GU", 7), ("DN", 5), ("DN", 6), ("DN", 7)]))
FILL = {True: FILL_SSD, False: FILL_ALONE}
SLOTS = {b: max(f) + 1 for b, f in FILL.items()}
SLOTS[True] = NQ * G
NOTHING = (None, 0)
DT_SLOT = {True: 1, False: 1}
SCAN_SLOT = {True: 13, False: 12}
DECAY_SLOT = {True: 16, False: 14}
STAT_SLOT = {True: 9, False: 20}
NORM_SLOT = {True: 15, False: 22}
RESIDUAL_SLOT = 7
DOWN_SPLINE_SLOT = 4

PE_TAIL = [("GU", 6), ("YD", 0), ("DN", 5), ("Z", 0), ("GU", 7), ("CB", 0), ("BT", 0), ("OUT", 0), ("DN", 6),
           ("OUT", 1), ("Z", 1), ("OUT", 2), ("DD", 0), ("ET", 0), ("DN", 7), ("Z", 2), ("OUT", 3), ("SS", 0),
           ("XT", 0), ("Z", 3)]
ACT_TAIL = [("GT", 6), ("CT", 4), ("CT", 5), ("ZT", 0), ("YH", 0), ("GT", 7), ("GH", 6), ("SQ", 0), ("YH", 1),
            ("CB", 0), ("SQ", 1), ("YH", 2), ("BT", 0), ("ZT", 1), ("GH", 7), ("SQ", 2), ("DD", 0), ("YH", 3),
            ("ZT", 2), ("SQ", 3), ("ET", 0), ("CT", 0), ("CT", 1), ("CT", 2), ("CT", 3), ("SS", 0), ("ZT", 3)]
DVE_TAIL = [("GM", 6), ("C", 4), ("C", 5), ("YS", 0), ("Y", 0), ("Z", 0), ("Y", 1), ("GM", 7), ("YL", 0),
            ("GL", 6), ("Y", 2), ("YL", 1), ("Z", 1), ("Y", 3), ("YL", 2), ("GL", 7), ("Z", 2), ("YL", 3),
            ("C", 0), ("C", 1), ("C", 2), ("C", 3), ("Z", 3), ("XT", 0), ("FIN", 0)]
SSD_PART = ("YD", "YS", "Y", "YH", "YL", "SQ", "OUT", "SS", "FIN")
START_PART = ("CB", "BT", "DD", "ET", "XT")


def tail(steps, A, B):
    if A and B:
        return steps
    return [t for t in steps if t[0] in (SSD_PART if B else START_PART)]


def pj_order(B):
    out = []
    for kind, j in [FILL[B][k] for k in sorted(FILL[B])] + tail(PE_TAIL, True, B):
        out += {"T": [("T", 0), ("T", 1)], "GU": [("GATE", j), ("UP", j)], "DT": [("DT", 0)], "X": [("X", j)],
                "Z": [("Z", j)]}.get(kind, [])
    return out


def tanh_order(B):
    names = {"GU": "GATE", "GT": "GATE", "Z": "Z", "ZT": "Z", "C": "C", "CT": "C"}
    steps = [FILL[B][k] for k in sorted(FILL[B])] + tail(ACT_TAIL, True, B)
    return [(names[kind], j) for kind, j in steps if kind in names]


PJ = {b: pj_order(b) for b in FILL}
TANH = {b: tanh_order(b) for b in FILL}
NPJ = len(PJ[True])
CONV_ORDER = [j for kind, j in TANH[True] if kind == "C"]
assert NPJ == len(PJ[False]) and CONV_ORDER == [j for kind, j in TANH[False] if kind == "C"]
BY_ACT = ("DT", "X")
RING = [("F", j) for j in range(FB - 2)] + [("F" if k == "GH" else "O", j) for k, j in ACT_TAIL if k in ("GH", "YH")]


def pj_index(B, kind, j):
    return PJ[B].index((kind, j))


def pj_bank(B, kind, j):
    return pj_index(B, kind, j) % 2


def pj_freed(B, upto, by_act):
    return sum((k in BY_ACT) == by_act for k, _ in PJ[B][:upto + 1])


N_ACT, N_DVE = pj_freed(True, NPJ - 1, True), pj_freed(True, NPJ - 1, False)


def pj_count(s, B, kind, j):
    by_act = kind in BY_ACT
    return (N_ACT if by_act else N_DVE) * s + pj_freed(B, pj_index(B, kind, j), by_act)


def pj_made(s, B, kind, j):
    return NPJ * s + pj_index(B, kind, j) + 1


def tanh_made(s, B, kind, j):
    order = [t for t in TANH[B] if t[0] != "C"]
    return len(order) * s + order.index((kind, j)) + 1


def u_made(s, j):
    return CB * s + CONV_ORDER.index(j) + 1


def ring_slot(kind, j):
    return RING.index((kind, j)) % 2


def ring_count(s, A, B, kind, j):
    here = [t for t in RING if (A and t[0] == "F") or (B and t[0] == "O")]
    return OPN * s - (XB if B else 0) + here.index((kind, j)) + 1


def ring_before(A, B, kind, j):
    here = [t for t in RING if (A and t[0] == "F") or (B and t[0] == "O")]
    same = [t for t in here[:here.index((kind, j))] if ring_slot(*t) == ring_slot(kind, j)]
    return same[-1] if same else None


def cols(q):
    c = (q % BATCH) * ST_B + (q // BATCH) * P
    return slice(c, c + P)


def head(g, j):
    return 8 * (g // 2) + 2 * j + g % 2


def w_groups():
    out = []
    for kind in ("gate", "up"):
        for k in range(KT):
            for a in range(0, FB, 4):
                out.append((kind, [(a + i, k) for i in range(4)]))
    for a in range(0, FB, 2):
        out.append(("down", [(a + i, b) for i in range(2) for b in range(KT)]))
    return out


W_GROUPS = w_groups()
W_FIRST = {k: [g[0] for g in W_GROUPS].index(k) for k in ("gate", "up", "down")}
N_CONST = 9 + 2 * REP
OPN = FB + XB


class Steps:

    def __init__(self, eng, sem):
        self.eng, self.sem, self.n, self.seen = eng, sem, 0, 0

    def did(self, ins):
        self.n += 1
        ins.then_inc(self.sem, 1)
        return self.n

    def wait(self, n=None):
        n = self.n if n is None else n
        if n > self.seen:
            self.eng.wait_ge(self.sem, n)
            self.seen = n

    def restart(self):
        self.wait()
        if self.n:
            self.eng.sem_clear(self.sem)
        self.n = self.seen = 0


def mamba_ffn_kernel(nc, x, in_w, conv_w, conv_b, a_log, dt_bias, d_skip, norm_w, out_w, gate_cp, up_cp, down_cp,
                     frac, prev_mask, ident_c, ident_bc, future_c, head_c, feature_c, out):
    with ExitStack() as ctx:
        def sb(name, shape, dt=F32, c=ctx):
            return c.enter_context(nc.sbuf_tensor(name, shape, dt))

        def sem(name):
            return ctx.enter_context(nc.semaphore(name))

        NIN = INTER + CB * P + R3
        win_h, win_l = sb("win_h", [P, KT, NIN], F32R), sb("win_l", [P, KT, NIN], F32R)
        wgu_h, wgu_l = sb("wgu_h", [P, KT, 2 * FFN], F32R), sb("wgu_l", [P, KT, 2 * FFN], F32R)
        wdn_h, wdn_l = sb("wdn_h", [P, FB, HID], F32R), sb("wdn_l", [P, FB, HID], F32R)
        wo_h, wo_l = sb("wo_h", [P, XB, HID], F32R), sb("wo_l", [P, XB, HID], F32R)
        ident = sb("ident", [P, P])
        ident_b = sb("ident_b", [P, P], BF16)
        future = sb("future", [P, P], BF16)
        sel = sb("sel", [R3, HEADS], BF16)
        selq = sb("selq", [R3, INTER], BF16)
        ones = sb("ones", [P, P])
        half_neg = sb("half_neg", [P, NQ])
        eps_1 = sb("eps_1", [P, NQ])
        eps_n = sb("eps_n", [P, NQ])
        cw = sb("cw", [P, CB, CONV_K])
        cb = sb("cb", [P, CB])
        dtb = sb("dtb", [R3, 1])
        alog = sb("alog", [R3, 1])
        a_neg = sb("a_neg", [R3, 1])
        dsk = sb("dsk", [P, XB])
        nw = sb("nw", [P, XB])
        xin = sb("xin", [P, NQ, HID])
        stats = sb("stats", [P, NQ, 6])
        mv = sb("mv", [P, NQ, 2])
        rstd = sb("rstd", [P, NQ])
        xnt_h, xnt_l = sb("xnt_h", [P, KT, ST], F32R), sb("xnt_l", [P, KT, ST], F32R)
        pre = sb("pre", [P, 2, BATCH, CONV_K - 1 + ST_B])
        halo = sb("halo", [P, CB, BATCH, CONV_K - 1])
        acc = sb("acc", [P, CB, ST])
        u = sb("u", [P, CB, ST])
        th = sb("th", [P, 2, ST])
        gz = sb("gz", [P, ZB, ST])
        dz = sb("dz", [R3, ST])
        de = sb("de", [R3, ST])
        dl = sb("dl", [R3, ST])
        dw = sb("dw", [R3, ST])
        acum = sb("acum", [R3, ST])
        a3 = sb("a3", [R3, ST], BF16)
        a3n = sb("a3n", [R3, ST], BF16)
        e3 = sb("e3", [R3, ST], BF16)
        tt_f = sb("tt_f", [2 * HEADS, ST])
        res = sb("res", [P, NQ, HID])
        opn_h, opn_l = sb("opn_h", [P, 2, ST], F32R), sb("opn_l", [P, 2, ST], F32R)
        inter = sb("inter", [P, 2, ST])
        state = [sb(f"state{b}", [P, INTER]) for b in range(BATCH)]
        with ExitStack() as early:
            raw_in = sb("raw_in", [P, KT, NIN], c=early)
            raw_out = sb("raw_out", [P, XB, HID], c=early)
            fr = sb("fr", [P, RPP, SEG], c=early)
            mk = sb("mk", [P, RPP, 16], c=early)
            cpw = sb("cpw", [P, 3, RPP + 4], c=early)
            coef = sb("coef", [P, 4, 3, RPP + 1], c=early)
            ctmp = sb("ctmp", [P, 3, RPP + 1], c=early)
            wv = sb("wv", [P, RPP, SEG], c=early)
            wp = sb("wp", [P, RPP, 16], c=early)
        tt = sb("tt", [P, NQ, 2 * HEADS])
        gm = sb("gm", [P, NQ, P])
        e_sb = sb("e_sb", [P, XB, P])
        xpad = sb("xpad", [P, 2, HEADS, 2 * HDIM])
        xdec = sb("xdec", [P, 2, INTER])
        b_tok = sb("b_tok", [P, NQ, STATE])
        etot = sb("etot", [P, NQ, HEADS])
        lm = sb("lm", [P, 4, 4 * P])
        y = sb("y", [P, XB, ST])
        sqs = sb("sqs", [P, ST])
        ss_sb = sb("ss_sb", [P, NQ])
        rms = sb("rms", [P, NQ])
        u_flat = u[:, :, :].rearrange("p a b -> p (a b)")
        wv_up = u_flat[:, 0:WROW].rearrange("p (j r) -> p j r", r=SEG)
        wp_up = u_flat[:, WROW:WROW + RPP * 16].rearrange("p (j r) -> p j r", r=16)
        raw_w = {"gate": gz[:, :, :].rearrange("p a b -> p (a b)"),
                 "up": raw_in[:, :, :].rearrange("p a b -> p (a b)")[:, 0:NSAMP // P],
                 "down": fr[:, :, :].rearrange("p a b -> p (a b)")[:, 0:NSAMP // P]}
        KINDS = ("gate", "up", "down")
        W_BANKS = (4, 5, 6, 7, 0, 1)

        def weight_parts(kind, parts, ps):
            a0, b0 = parts[0]
            n = len(parts) * P
            if kind == "down":
                w = slice(a0, a0 + 2)
                return wdn_h[:, w, :], wdn_l[:, w, :], ps[:, :].rearrange("p (a h) -> p a h", a=2), 0.5
            o = (kind == "up") * FFN
            c = slice(o + a0 * P, o + a0 * P + n)
            return wgu_h[:, b0, c], wgu_l[:, b0, c], ps[:, 0:n], 1.0

        w_dram = [nc.dram_tensor(f"spline_w{i}", [P * WROW], F32, kind="Internal").ap() for i in range(3)]

        psum = [ctx.enter_context(nc.psum_tensor(f"ps{i}", [P, 512], F32)) for i in range(8)]
        pd = [psum[0][:].rearrange("p (t h) -> p t h", t=2), psum[1][:].rearrange("p (t h) -> p t h", t=2)]
        pj = [psum[2], psum[3]]
        pseg = [psum[4], psum[5]]
        py = psum[6]
        pm = psum[7]
        po = [psum[6][:].rearrange("p (t h) -> p t h", t=2), psum[7][:].rearrange("p (t h) -> p t h", t=2)]

        names = """ld_const ld_spline ld_in ld_out ld_x ld_res st_out
        st_gate st_up st_down ld_gate ld_up ld_down
        set_dve set_act in_high in_low out_high w_trans w_high w_low
        coef_ready spline_gate spline_up spline_down
        xn_ready var_ready rstd_ready xnt_high pj_done pj_act pj_dve
        tap_done silu_tanh u_ready gate_tanh opn_high opn_low f_used o_used
        dt_log ad_ready scan_done dt_ready decay_ready exp_acum a3_ready e3_ready
        tt_psum tt_ready g_psum gm_ready b_psum b_ready et_psum et_ready
        xt_psum xpad_ready xdec_ready seg_psum l_ready m_ready m_used
        e_psum e_ready o_psum y_off s_psum s_decayed s_ready y_sum
        y_gated sq_ready sq_used sqs_ready ss_psum ss_ready rms_ready evac_done final_done
        act_step dve_step pool_step""".split()
        sm = {n: sem(n) for n in names}

        def rep(ap, n):
            return ap.unsqueeze(len(ap.shape)).broadcast_to(list(ap.shape) + [n])

        x_st = x.rearrange("b (s h p) c -> b s p h c", p=P, h=ST_B // P)
        out_st = out.rearrange("b (s h p) c -> b s p h c", p=P, h=ST_B // P)
        HB = ST_B // P

        block = ctx.enter_context(nc.Block())

        def spline_rows(eng, link, i, dst, first):
            def horner(dst, f, m0, n):
                c = [rep(coef[:, k, i, m0:m0 + RPP], n) for k in range(4)]
                link(eng.tensor_tensor(dst, f, c[3], ALU.mult))
                link(eng.tensor_tensor(dst, dst, c[2], ALU.add))
                link(eng.tensor_tensor(dst, dst, f, ALU.mult))
                link(eng.tensor_tensor(dst, dst, c[1], ALU.add))
                link(eng.tensor_tensor(dst, dst, f, ALU.mult))
                link(eng.tensor_tensor(dst, dst, c[0], ALU.add))

            horner(dst, fr[:], 1, SEG)
            horner(first, fr[:, :, 0:16], 0, 16)
            link(eng.tensor_tensor(first, first, dst[:, :, 0:16], ALU.subtract))
            link(eng.tensor_tensor(first, first, mk[:], ALU.mult))
            return eng.tensor_tensor(dst[:, :, 0:16], dst[:, :, 0:16], first, ALU.add)

        @block.sync
        def _(sp):
            for b in range(BATCH):
                sp.dma_start(xin[:, b * HB:(b + 1) * HB, :], x_st[b, 0]).then_inc(sm["ld_x"], 16)
            for i, cp in enumerate((gate_cp, up_cp, down_cp)):
                window = bass.AP(cp.tensor, 0, [[RPP, P], [1, RPP + 4]])
                sp.dma_start(cpw[:, i, :], window).then_inc(sm["ld_spline"], 16)
            sp.dma_start(fr[:], frac.rearrange("p (j r) -> p j r", r=SEG)).then_inc(sm["ld_spline"], 16)
            sp.dma_start(mk[:], prev_mask.rearrange("p (j r) -> p j r", r=16)).then_inc(sm["ld_spline"], 16)
            sp.dma_start(raw_in[:], in_w.rearrange("(k p) f -> p k f", p=P)).then_inc(sm["ld_in"], 16)
            n = 0
            for dst, src in ((ident[:], ident_c), (ident_b[:], ident_bc), (future[:], future_c), (sel[:], head_c),
                             (selq[:], feature_c), (cw[:], conv_w.rearrange("p (j k) -> p j k", k=CONV_K)),
                             (cb[:], conv_b), (nw[:], norm_w), (dsk[:], d_skip)):
                sp.dma_start(dst, src).then_inc(sm["ld_const"], 16)
                n += 1
            for c in range(REP):
                rr = slice(c * HEADS, (c + 1) * HEADS)
                sp.dma_start(dtb[rr, :], dt_bias).then_inc(sm["ld_const"], 16)
                sp.dma_start(alog[rr, :], a_log).then_inc(sm["ld_const"], 16)
                n += 2
            assert n == N_CONST
            sp.dma_start(raw_out[:], out_w.rearrange("(j p) h -> p j h", p=P)).then_inc(sm["ld_out"], 16)
            for b in range(BATCH):
                sp.dma_start(res[:, b * HB:(b + 1) * HB, :], x_st[b, 0]).then_inc(sm["ld_res"], 16)
            for i, kind in enumerate(KINDS):
                sp.wait_ge(sm[f"spline_{kind}"], 1)
                src = wv_up if kind == "up" else wv[:]
                sp.dma_start(w_dram[i].rearrange("(p j r) -> p j r", p=P, r=SEG), src).then_inc(sm[f"st_{kind}"], 16)
                sp.wait_ge(sm[f"st_{kind}"], 16)
                if kind == "up":
                    sp.wait_ge(sm["in_low"], 1)
                wide = FFN if kind == "down" else HID
                sp.dma_start(raw_w[kind].rearrange("p (n h) -> p n h", h=wide),
                             w_dram[i][0:NSAMP].rearrange("(b p h) -> p b h", p=P, h=wide)).then_inc(sm[f"ld_{kind}"], 16)

            def load_x(s):
                sp.wait_ge(sm["pj_done"], NPJ * (s - 1) + KT)
                for b in range(BATCH):
                    sp.dma_start(xin[:, b * HB:(b + 1) * HB, :], x_st[b, s]).then_inc(sm["ld_x"], 16)

            def store(r):
                sp.wait_ge(sm["final_done"], r + 1)
                for b in range(BATCH):
                    sp.dma_start(out_st[b, r], res[:, b * HB:(b + 1) * HB, :]).then_inc(sm["st_out"], 16)
                sp.wait_ge(sm["st_out"], 32 * (r + 1))

            def load_res(s):
                for b in range(BATCH):
                    sp.dma_start(res[:, b * HB:(b + 1) * HB, :], x_st[b, s]).then_inc(sm["ld_res"], 16)

            load_x(1)
            with sp.Fori(1, NST - 1) as s:
                load_x(s + 1)
                store(s - 1)
                load_res(s)
            store(NST - 2)
            load_res(NST - 1)
            store(NST - 1)

        @block.tensor
        def _(pe):
            pe.wait_ge(sm["ld_const"], 16 * N_CONST)

            def weights(kind):
                pe.wait_ge(sm[f"ld_{kind}"], 16)
                raw = raw_w[kind]
                for n, (k, parts) in enumerate(W_GROUPS):
                    if k != kind:
                        continue
                    nb = len(W_BANKS)
                    if n >= nb:
                        pe.wait_ge(sm["w_low"], n - nb + 1)
                    for i, (a, b) in enumerate(parts):
                        c = b * FFN + a * P if kind == "down" else a * HID + b * P
                        last = nc.tensor.transpose(psum[W_BANKS[n % nb]][:, i * P:(i + 1) * P], raw[:, c:c + P],
                                                   ident[:])
                    last.then_inc(sm["w_trans"], 1)

            def pj_free(s, B, kind, j):
                n = pj_index(B, kind, j)
                if n >= 2:
                    before = PJ[B][n - 2]
                    pe.wait_ge(sm["pj_act" if before[0] in BY_ACT else "pj_dve"], pj_count(s, B, *before))
                elif B:
                    pe.wait_ge(sm["pj_dve"], N_DVE * s)

            def project(s, B, kind, j, w_h, w_l, c0, m):
                pj_free(s, B, kind, j)
                bank = pj[pj_bank(B, kind, j)]
                n = 0
                for k in range(KT):
                    for w, a in ((w_h, xnt_h), (w_h, xnt_l), (w_l, xnt_h)):
                        last = nc.tensor.matmul(bank[0:m, :], w[:, k, c0:c0 + m], a[:, k, :],
                                                start=(n == 0), stop=(n == 3 * KT - 1))
                        n += 1
                last.then_inc(sm["pj_done"], 1)

            def down(s, A, B, kind, j, w_h, w_l, banks, n_blocks, used):
                pe.wait_ge(sm["opn_low"], ring_count(s, A, B, kind, j))
                for t in range(NQ):
                    tc = slice(t * P, (t + 1) * P)
                    for n, (a, w) in enumerate(((opn_h, w_h), (opn_h, w_l), (opn_l, w_h))):
                        last = nc.tensor.matmul(banks[t // 2][:, t % 2, :], a[:, ring_slot(kind, j), tc], w[:, j, :],
                                                start=(j == 0 and t % 2 == 0 and n == 0),
                                                stop=(j == n_blocks - 1 and n == 2), skip_group_check=True)
                last.then_inc(sm[used], 1)

            def seg(r, k):
                q, g = divmod(k, G)
                bank = pseg[k % 2]
                if k == 0:
                    pe.wait_ge(sm["a3_ready"], r + 1)
                    pe.wait_ge(sm["ss_ready"], r)
                    pe.wait_ge(sm["tt_ready"], r + 1)
                if k == 1:
                    pe.wait_ge(sm["xpad_ready"], NQ * r + 1)
                if k >= 2:
                    pe.wait_ge(sm["l_ready"], 32 * r + k - 1)
                c = cols(q)
                heads = sel[:, 8 * (g // 2) + g % 2:8 * (g // 2) + 8:2]
                nc.tensor.matmul(bank[:, :].rearrange("p (h l) -> p h l", h=4), a3n[:, c], rep(heads, P),
                                 start=True, stop=False, skip_group_check=True)
                nc.tensor.matmul(bank[:, :].rearrange("p (h l) -> p h l", h=4), ident_b[:],
                                 future[:].unsqueeze(1).broadcast_to([P, 4, P]),
                                 start=False, stop=False, skip_group_check=True)
                for j in range(4):
                    h = head(g, j)
                    last = nc.tensor.matmul(bank[:, j * P:(j + 1) * P], sel[:, h:h + 1].broadcast_to([R3, P]),
                                            a3[:, c], start=False, stop=True, skip_group_check=True)
                last.then_inc(sm["seg_psum"], 1)

            def yd(r, k):
                q, g = divmod(k, G)
                pe.wait_ge(sm["m_ready"], 32 * r + k + 1)
                if g == 0:
                    pe.wait_ge(sm["xpad_ready"], NQ * r + q + 1)
                    if q:
                        pe.wait_ge(sm["y_sum"], NQ * r + q)
                    else:
                        pe.wait_ge(sm["final_done"], r)
                for j in range(4):
                    last = nc.tensor.matmul(py[32 * j:32 * j + 32, (g // 2) * P:(g // 2 + 1) * P],
                                            xpad[:, q % 2, head(g, j), :], lm[:, k % 4, j * P:(j + 1) * P],
                                            start=(g % 2 == 0), stop=(g % 2 == 1), skip_group_check=True)
                last.then_inc(sm["m_used"], 1)

            def x_tok(q, bank):
                for j in range(XB):
                    last = nc.tensor.transpose(bank[:, j * P:(j + 1) * P], u[:, j, cols(q)], ident[:])
                last.then_inc(sm["xt_psum"], 1)

            def step(s, A, B, kind, j):
                r = s - 1
                if kind == "T":
                    pe.wait_ge(sm["xn_ready"], s * NQ + NQ)
                    for k in range(KT):
                        pj_free(s, B, "T", k)
                        for t in range(NQ):
                            last = nc.tensor.transpose(pj[k][:, t * P:(t + 1) * P],
                                                       xin[:, t, k * P:(k + 1) * P], ident[:])
                        last.then_inc(sm["pj_done"], 1)
                elif kind == "W":
                    weights(j)
                elif kind == "DT":
                    pe.wait_ge(sm["pj_dve"], pj_count(s, B, "T", KT - 1))
                    if not B:
                        pe.wait_ge(sm["in_low"], 1)
                    project(s, B, "DT", 0, win_h, win_l, INTER + CB * P, R3)
                elif kind == "X":
                    project(s, B, "X", j, win_h, win_l, INTER + j * P, P)
                elif kind == "Z":
                    project(s, B, "Z", j, win_h, win_l, j * P, P)
                elif kind == "GU":
                    if not B:
                        pe.wait_ge(sm["w_low"], W_FIRST["down"])
                    project(s, B, "GATE", j, wgu_h, wgu_l, j * P, P)
                    project(s, B, "UP", j, wgu_h, wgu_l, FFN + j * P, P)
                elif kind == "DN":
                    if j == 0:
                        if B:
                            pe.wait_ge(sm["evac_done"], s)
                        else:
                            pe.wait_ge(sm["w_low"], len(W_GROUPS))
                    down(s, A, B, "F", j, wdn_h, wdn_l, pd, FB, "f_used")
                elif kind == "OUT":
                    if j == 0:
                        pe.wait_ge(sm["y_sum"], NQ * r + NQ)
                        pe.wait_ge(sm["s_ready"], NQ * r + NQ)
                    down(s, A, B, "O", j, wo_h, wo_l, po, XB, "o_used")
                elif kind == "YD":
                    yd(r, NQ * G - 1)
                elif kind == "SS":
                    pe.wait_ge(sm["sqs_ready"], r + 1)
                    pe.wait_ge(sm["l_ready"], 32 * (r + 1))
                    if A:
                        pe.wait_ge(sm["tt_ready"], s + 1)
                    for t in range(NQ):
                        last = nc.tensor.matmul(pseg[0][:, t:t + 1], sqs[:, t * P:(t + 1) * P], ones[:, 0:1],
                                                start=True, stop=True)
                    last.then_inc(sm["ss_psum"], 1)
                elif kind == "CB":
                    pe.wait_ge(sm["u_ready"], u_made(s, XB + 1))
                    if B:
                        pe.wait_ge(sm["l_ready"], 32 * s)
                    for q in range(NQ):
                        last = nc.tensor.matmul(pseg[0][:, q * P:(q + 1) * P], u[:, XB, cols(q)],
                                                u[:, XB + 1, cols(q)], start=True, stop=True)
                    last.then_inc(sm["g_psum"], 1)
                elif kind == "BT":
                    for q in range(NQ):
                        last = nc.tensor.transpose(pseg[1][:, q * P:(q + 1) * P], u[:, XB, cols(q)], ident[:])
                    last.then_inc(sm["b_psum"], 1)
                elif kind == "DD":
                    pe.wait_ge(sm["gm_ready"], s + 1)
                    pe.wait_ge(sm["dt_ready"], s + 1)
                    pe.wait_ge(sm["decay_ready"], s + 1)
                    for q in range(NQ):
                        last = nc.tensor.matmul(pseg[0][:, q * 2 * HEADS:(q + 1) * 2 * HEADS], tt_f[:, cols(q)],
                                                ident[0:2 * HEADS, 0:2 * HEADS], start=True, stop=True)
                    last.then_inc(sm["tt_psum"], 1)
                elif kind == "ET":
                    pe.wait_ge(sm["b_ready"], s + 1)
                    pe.wait_ge(sm["e3_ready"], s + 1)
                    for q in range(NQ):
                        end = cols(q).stop
                        last = nc.tensor.matmul(pseg[1][:, q * HEADS:(q + 1) * HEADS],
                                                e3[:, end - 1:end].broadcast_to([R3, P]), sel[:, :],
                                                start=True, stop=True)
                    last.then_inc(sm["et_psum"], 1)
                elif kind == "XT":
                    pe.wait_ge(sm["et_ready"], s + 1)
                    pe.wait_ge(sm["u_ready"], CB * s + CB)
                    x_tok(0, pseg[1])

            def body(s, A, B):
                r = s - 1
                for k in range(SLOTS[B]):
                    q, g = divmod(k, G)
                    if B:
                        seg(r, k)
                    if A and k in FILL[B]:
                        step(s, A, B, *FILL[B][k])
                    if B:
                        if k:
                            yd(r, k - 1)
                        if g == 1:
                            pe.wait_ge(sm["xpad_ready"], NQ * r + q + 1)
                            if not q:
                                pe.wait_ge(sm["final_done"], r)
                            for j in range(XB):
                                last = nc.tensor.matmul(pm[:, j * P:(j + 1) * P], selq[:, j * P:(j + 1) * P],
                                                        e3[:, cols(q)], start=True, stop=True)
                            last.then_inc(sm["e_psum"], 1)
                        if g == 3:
                            pe.wait_ge(sm["e_ready"], NQ * r + q + 1)
                            if q >= 2:
                                pe.wait_ge(sm["s_ready"], NQ * r + q - 1)
                            for j in range(XB):
                                last = nc.tensor.matmul(pm[:, j * P:(j + 1) * P],
                                                        state[q % BATCH][:, j * P:(j + 1) * P],
                                                        u[:, XB + 1, cols(q)], start=True, stop=True)
                            last.then_inc(sm["o_psum"], 1)
                        if g == 5:
                            pe.wait_ge(sm["y_off"], NQ * r + q + 1)
                            pe.wait_ge(sm["xdec_ready"], NQ * r + q + 1)
                            nc.tensor.matmul(pm[:, :], b_tok[:, q, :], xdec[:, q % 2, :],
                                             start=True, stop=True).then_inc(sm["s_psum"], 1)
                        if g == 7 and q < NQ - 1:
                            pe.wait_ge(sm["s_ready"], NQ * r + q + 1)
                            x_tok(q + 1, pm)
                for kind, j in tail(PE_TAIL, A, B):
                    step(s, A, B, kind, j)

            body(0, True, False)
            with pe.Fori(1, NST) as s:
                body(s, True, True)
            body(NST, False, True)

        @block.scalar
        def _(act):
            st = Steps(act, sm["act_step"])
            act.wait_ge(sm["ld_const"], 16 * N_CONST)
            nc.scalar.activation(a_neg[:], alog[:], ACT.Exp).then_inc(sm["set_act"], 1)
            act.wait_ge(sm["ld_in"], 16)
            nc.scalar.activation(win_h[:], raw_in[:], ACT.Copy).then_inc(sm["in_high"], 1)
            act.wait_ge(sm["ld_out"], 16)
            for j in range(XB):
                nc.scalar.activation(wo_h[:, j, :], raw_out[:, j, :], ACT.Identity,
                                     scale=nw[:, j:j + 1]).then_inc(sm["out_high"], 1)

            def weights(kind):
                for n, (k, parts) in enumerate(W_GROUPS):
                    if k == kind:
                        act.wait_ge(sm["w_trans"], n + 1)
                        w_h, w_l, ps, scale = weight_parts(kind, parts, psum[W_BANKS[n % len(W_BANKS)]])
                        nc.scalar.activation(w_h, ps, ACT.Copy, scale=scale).then_inc(sm["w_high"], 1)

            def tanh_slot(s, B, kind, j):
                i = TANH[B].index((kind, j))
                before = TANH[B][i - 2] if i >= 2 else None
                if before is None:
                    if B:
                        act.wait_ge(sm["u_ready"], CB * s)
                        act.wait_ge(sm["pj_dve"], N_DVE * s)
                elif before[0] == "C":
                    act.wait_ge(sm["u_ready"], u_made(s, before[1]))
                else:
                    act.wait_ge(sm["pj_dve"], pj_count(s, B, *before))
                return th[:, i % 2, :]

            def operand_slot(s, A, B, kind, j):
                before = ring_before(A, B, kind, j)
                if before is None:
                    if B:
                        act.wait_ge(sm["f_used"], FB * s)
                        act.wait_ge(sm["o_used"], XB * (s - 1))
                elif before[0] == "F":
                    act.wait_ge(sm["f_used"], FB * s + before[1] + 1)
                else:
                    act.wait_ge(sm["o_used"], XB * (s - 1) + before[1] + 1)
                return opn_h[:, ring_slot(kind, j), :]

            def pj_tanh(s, B, kind, j):
                act.wait_ge(sm["pj_done"], pj_made(s, B, kind, j))
                slot = tanh_slot(s, B, kind, j)
                nc.scalar.activation(slot, pj[pj_bank(B, kind, j)][:], ACT.Tanh,
                                     scale=0.5).then_inc(sm["gate_tanh"], 1)

            def step(s, A, B, kind, j):
                r = s - 1
                if kind == "T":
                    for k in range(KT):
                        act.wait_ge(sm["pj_done"], pj_made(s, B, "T", k))
                        if B:
                            act.wait_ge(sm["pj_done"], NPJ * s)
                        nc.scalar.activation(xnt_h[:, k, :], pj[k][:], ACT.Copy).then_inc(sm["xnt_high"], 1)
                elif kind == "W":
                    weights(j)
                elif kind == "DT":
                    act.wait_ge(sm["pj_done"], pj_made(s, B, "DT", 0))
                    if B:
                        act.wait_ge(sm["a3_ready"], s)
                    nc.scalar.activation(dz[:], pj[pj_bank(B, "DT", 0)][0:R3, :], ACT.Identity,
                                         bias=dtb[:]).then_inc(sm["pj_act"], 1)
                elif kind == "X":
                    act.wait_ge(sm["pj_done"], pj_made(s, B, "X", j))
                    if j >= 2 or B:
                        act.wait_ge(sm["tap_done"], CB * s + j - 1)
                    if j == 0 and B:
                        act.wait_ge(sm["u_ready"], CB * s)
                    bank = pj[pj_bank(B, "X", j)]
                    batches = bank[:].rearrange("p (b t) -> p b t", b=BATCH)
                    n = st.did(nc.scalar.activation(pre[:, j % 2, :, 0:CONV_K - 1], halo[:, j], ACT.Copy))
                    nc.scalar.activation(pre[:, j % 2, :, CONV_K - 1:], batches, ACT.Copy)
                    nc.scalar.activation(acc[:, j, :], bank[:], ACT.Identity, bias=cb[:, j:j + 1],
                                         scale=cw[:, j, CONV_K - 1:CONV_K])
                    st.wait(n)
                    nc.scalar.activation(halo[:, j], batches[:, :, ST_B - CONV_K + 1:],
                                         ACT.Copy).then_inc(sm["pj_act"], 1)
                elif kind in ("GU", "GT"):
                    pj_tanh(s, B, "GATE", j)
                elif kind in ("Z", "ZT"):
                    pj_tanh(s, B, "Z", j)
                elif kind in ("C", "CT"):
                    act.wait_ge(sm["tap_done"], CB * s + j + 1)
                    slot = tanh_slot(s, B, "C", j)
                    nc.scalar.activation(slot, acc[:, j, :], ACT.Tanh, scale=0.5).then_inc(sm["silu_tanh"], 1)
                elif kind == "GH":
                    act.wait_ge(sm["pj_dve"], pj_count(s, B, "UP", j))
                    slot = operand_slot(s, A, B, "F", j)
                    nc.scalar.activation(slot, inter[:, j % 2, :], ACT.Copy).then_inc(sm["opn_high"], 1)
                elif kind == "YH":
                    act.wait_ge(sm["y_gated"], XB * r + j + 1)
                    slot = operand_slot(s, A, B, "O", j)
                    nc.scalar.activation(slot, y[:, j, :], ACT.Copy).then_inc(sm["opn_high"], 1)
                elif kind == "SQ":
                    if j < 2:
                        act.wait_ge(sm["s_psum"], NQ * r + NQ)
                    else:
                        act.wait_ge(sm["sq_used"], r + 1)
                    nc.scalar.activation(xdec[:, j % 2, :], y[:, j, :], ACT.Square,
                                         scale=0.5).then_inc(sm["sq_ready"], 1)
                elif kind == "SS":
                    act.wait_ge(sm["ss_psum"], r + 1)
                    nc.scalar.activation(ss_sb[:], pseg[0][:, 0:NQ], ACT.Copy).then_inc(sm["ss_ready"], 1)
                elif kind == "CB":
                    act.wait_ge(sm["g_psum"], s + 1)
                    nc.scalar.activation(gm[:].rearrange("p q l -> p (q l)"), pseg[0][:], ACT.Copy,
                                         scale=0.25).then_inc(sm["gm_ready"], 1)
                elif kind == "BT":
                    act.wait_ge(sm["b_psum"], s + 1)
                    nc.scalar.activation(b_tok[:].rearrange("p a b -> p (a b)"), pseg[1][:],
                                         ACT.Copy).then_inc(sm["b_ready"], 1)
                elif kind == "DD":
                    act.wait_ge(sm["tt_psum"], s + 1)
                    nc.scalar.activation(tt[:].rearrange("p a b -> p (a b)"), pseg[0][:, 0:NQ * 2 * HEADS],
                                         ACT.Copy).then_inc(sm["tt_ready"], 1)
                elif kind == "ET":
                    act.wait_ge(sm["et_psum"], s + 1)
                    nc.scalar.activation(etot[:].rearrange("p a b -> p (a b)"), pseg[1][:, 0:NQ * HEADS],
                                         ACT.Copy).then_inc(sm["et_ready"], 1)

            def body(s, A, B):
                r = s - 1
                for k in range(SLOTS[B] + 2):
                    q, g = divmod(k, G)
                    if B and k < NQ * G:
                        act.wait_ge(sm["seg_psum"], 32 * r + k + 1)
                        if k >= 4:
                            act.wait_ge(sm["m_used"], 32 * r + k - 3)
                        nc.scalar.activation(lm[:, k % 4, :], pseg[k % 2][:], ACT.Exp).then_inc(sm["l_ready"], 1)
                        if g == 2:
                            act.wait_ge(sm["e_psum"], NQ * r + q + 1)
                            if q:
                                act.wait_ge(sm["y_off"], NQ * r + q)
                            nc.scalar.activation(e_sb[:].rearrange("p a b -> p (a b)"), pm[:],
                                                 ACT.Copy).then_inc(sm["e_ready"], 1)
                    if A and FILL[B].get(k - 2, NOTHING)[0] == "GU":
                        step(s, A, B, "GH", FILL[B][k - 2][1])
                    if A and k in FILL[B]:
                        step(s, A, B, *FILL[B][k])
                    if A and k == DT_SLOT[B] + 1:
                        act.wait_ge(sm["pj_act"], pj_count(s, B, "DT", 0))
                        st.did(nc.scalar.activation(dw[:], dz[:], ACT.Abs))
                    if A and k == DT_SLOT[B] + 2:
                        st.wait()
                        st.did(nc.scalar.activation(de[:], dw[:], ACT.Exp, scale=-1.0))
                    if A and k == DT_SLOT[B] + 3:
                        st.wait()
                        nc.scalar.activation(dl[:], de[:], ACT.Ln, bias=1.0).then_inc(sm["dt_log"], 1)
                    if A and k == DECAY_SLOT[B]:
                        act.wait_ge(sm["scan_done"], s + 1)
                        for t in range(NQ):
                            c = slice(t * P, (t + 1) * P)
                            last = nc.scalar.activation(tt_f[HEADS:2 * HEADS, c], acum[HEADS:2 * HEADS, c], ACT.Exp,
                                                        scale=-1.0,
                                                        bias=acum[HEADS:2 * HEADS, c.stop - 1:c.stop])
                        last.then_inc(sm["decay_ready"], 1)
                        nc.scalar.activation(dl[:], acum[:], ACT.Exp).then_inc(sm["exp_acum"], 1)
                for kind, j in tail(ACT_TAIL, A, B):
                    step(s, A, B, kind, j)
                st.restart()

            body(0, True, False)
            with act.Fori(1, NST) as s:
                body(s, True, True)
            body(NST, False, True)

        @block.vector
        def _(dve):
            st = Steps(dve, sm["dve_step"])

            def link(ins):
                st.did(ins)
                st.wait()

            V = nc.vector
            V.memset(ones[:], 1.0).then_inc(sm["set_dve"], 1)
            V.memset(halo[:].rearrange("p a b c -> p (a b c)"), 0.0).then_inc(sm["set_dve"], 1)
            for b in range(BATCH):
                V.memset(state[b][:], 0.0).then_inc(sm["set_dve"], 1)
            for t, v in ((half_neg, -0.5), (eps_1, EPS), (eps_n, EPS * INTER)):
                V.memset(t[:], v).then_inc(sm["set_dve"], 1)

            def layer_norm(s):
                dve.wait_ge(sm["ld_x"], 32 * s + 32)
                for t in range(NQ):
                    st.did(V.bn_stats(stats[:, t, :], xin[:, t, :]))
                st.wait()
                for t in range(NQ):
                    last = V.bn_aggr(mv[:, t, :], stats[:, t, :])
                last.then_inc(sm["var_ready"], 1)

            def normalize(s):
                dve.wait_ge(sm["rstd_ready"], s + 1)
                for t in range(NQ):
                    V.tensor_scalar(xin[:, t, :], xin[:, t, :], mv[:, t, 0:1], rstd[:, t:t + 1],
                                    ALU.subtract, ALU.mult).then_inc(sm["xn_ready"], 1)

            layer_norm(0)
            dve.wait_ge(sm["ld_spline"], 16 * 5)
            p0, p1, p2, p3 = (cpw[:, :, k:k + RPP + 1] for k in range(4))
            c0, c1, c2, c3 = (coef[:, k] for k in range(4))
            tmp = ctmp[:]
            st.did(V.tensor_copy(c0, p1))
            link(V.tensor_tensor(tmp, p2, p0, ALU.subtract))
            link(V.tensor_scalar(c1, tmp, 0.5, None, ALU.mult))
            link(V.scalar_tensor_tensor(tmp, p0, 2.0, p3, ALU.mult, ALU.subtract))
            link(V.scalar_tensor_tensor(tmp, p1, -5.0, tmp, ALU.mult, ALU.add))
            link(V.scalar_tensor_tensor(tmp, p2, 4.0, tmp, ALU.mult, ALU.add))
            link(V.tensor_scalar(c2, tmp, 0.5, None, ALU.mult))
            link(V.tensor_tensor(tmp, p3, p0, ALU.subtract))
            link(V.scalar_tensor_tensor(tmp, p1, 3.0, tmp, ALU.mult, ALU.add))
            link(V.scalar_tensor_tensor(tmp, p2, -3.0, tmp, ALU.mult, ALU.add))
            V.tensor_scalar(c3, tmp, 0.5, None, ALU.mult).then_inc(sm["coef_ready"], 1)
            normalize(0)
            dve.wait_ge(sm["coef_ready"], 1)
            spline_rows(V, link, 0, wv[:], wp[:]).then_inc(sm["spline_gate"], 1)
            dve.wait_ge(sm["in_high"], 1)
            V.tensor_tensor(win_l[:], raw_in[:], win_h[:].bitcast(F32), ALU.subtract).then_inc(sm["in_low"], 1)

            def down_spline():
                dve.wait_ge(sm["st_gate"], 16)
                dve.wait_ge(sm["spline_gate"], 1)
                spline_rows(V, link, 2, wv[:], wp[:]).then_inc(sm["spline_down"], 1)
                dve.wait_ge(sm["out_high"], XB)
                for j in range(XB):
                    V.scalar_tensor_tensor(wo_l[:, j, :], raw_out[:, j, :], nw[:, j:j + 1],
                                           wo_h[:, j, :].bitcast(F32), ALU.mult, ALU.subtract)
                st.did(V.tensor_scalar(dsk[:], dsk[:], 0.5, None, ALU.mult))

            def weights(kind):
                for n, (k, parts) in enumerate(W_GROUPS):
                    if k == kind:
                        dve.wait_ge(sm["w_high"], n + 1)
                        w_h, w_l, ps, scale = weight_parts(kind, parts, psum[W_BANKS[n % len(W_BANKS)]])
                        V.scalar_tensor_tensor(w_l, ps, scale, w_h.bitcast(F32), ALU.mult,
                                               ALU.subtract).then_inc(sm["w_low"], 1)

            def pad_x(r, q, bank):
                dve.wait_ge(sm["xt_psum"], NQ * r + q + 1)
                if q == 0:
                    dve.wait_ge(sm["tt_ready"], r + 1)
                dst = bass.AP(xpad, (q % 2) * 2 * INTER,
                              [[4 * INTER, P], [4 * HDIM, HEADS // 2], [3 * HDIM, 2], [1, HDIM]])
                V.tensor_tensor(dst, bank[:].rearrange("p (a b c) -> p a b c", a=HEADS // 2, b=2),
                                rep(tt[:, q, 0:HEADS], HDIM).rearrange("p (a b) c -> p a b c", b=2),
                                ALU.mult).then_inc(sm["xpad_ready"], 1)

            def y_sum(r, q):
                dve.wait_ge(sm["m_used"], 32 * r + G * q + G)
                dve.wait_ge(sm["y_off"], NQ * r + q + 1)
                V.tensor_tensor(y[:, :, cols(q)], y[:, :, cols(q)], py[:].rearrange("p (a l) -> p a l", a=XB),
                                ALU.add).then_inc(sm["y_sum"], 1)

            def step(s, A, B, kind, j):
                r = s - 1
                if kind == "T":
                    for k in range(KT):
                        dve.wait_ge(sm["xnt_high"], KT * s + k + 1)
                        V.tensor_tensor(xnt_l[:, k, :], pj[k][:], xnt_h[:, k, :].bitcast(F32),
                                        ALU.subtract).then_inc(sm["pj_dve"], 1)
                elif kind == "W":
                    weights(j)
                elif kind == "X":
                    dve.wait_ge(sm["pj_act"], pj_count(s, B, "X", j))
                    sl = pre[:, j % 2]
                    a = acc[:, j, :].rearrange("p (b t) -> p b t", b=BATCH)
                    for k in range(CONV_K - 2, -1, -1):
                        ins = V.scalar_tensor_tensor(a, sl[:, :, k:k + ST_B], cw[:, j, k:k + 1], a, ALU.mult, ALU.add)
                        if k:
                            link(ins)
                        else:
                            ins.then_inc(sm["tap_done"], 1)
                elif kind in ("GU", "GM"):
                    dve.wait_ge(sm["gate_tanh"], tanh_made(s, B, "GATE", j))
                    if j >= 2:
                        dve.wait_ge(sm["opn_low"], ring_count(s, A, B, "F", j - 2))
                    V.scalar_tensor_tensor(inter[:, j % 2, :], th[:, TANH[B].index(("GATE", j)) % 2, :], 1.0,
                                           pj[pj_bank(B, "GATE", j)][:], ALU.add,
                                           ALU.mult).then_inc(sm["pj_dve"], 1)
                    dve.wait_ge(sm["pj_dve"], pj_count(s, B, "GATE", j))
                    dve.wait_ge(sm["pj_done"], pj_made(s, B, "UP", j))
                    V.tensor_tensor(inter[:, j % 2, :], inter[:, j % 2, :], pj[pj_bank(B, "UP", j)][:],
                                    ALU.mult).then_inc(sm["pj_dve"], 1)
                elif kind == "GL":
                    dve.wait_ge(sm["opn_high"], ring_count(s, A, B, "F", j))
                    i = ring_slot("F", j)
                    V.tensor_tensor(opn_l[:, i, :], inter[:, j % 2, :], opn_h[:, i, :].bitcast(F32),
                                    ALU.subtract).then_inc(sm["opn_low"], 1)
                elif kind == "YL":
                    dve.wait_ge(sm["opn_high"], ring_count(s, A, B, "O", j))
                    i = ring_slot("O", j)
                    V.tensor_tensor(opn_l[:, i, :], y[:, j, :], opn_h[:, i, :].bitcast(F32),
                                    ALU.subtract).then_inc(sm["opn_low"], 1)
                elif kind == "Z":
                    dve.wait_ge(sm["gate_tanh"], tanh_made(s, B, "Z", j))
                    if B:
                        dve.wait_ge(sm["y_gated"], XB * r + j + 1)
                    V.scalar_tensor_tensor(gz[:, j, :], th[:, TANH[B].index(("Z", j)) % 2, :], 1.0,
                                           pj[pj_bank(B, "Z", j)][:], ALU.add, ALU.mult).then_inc(sm["pj_dve"], 1)
                elif kind == "C":
                    dve.wait_ge(sm["silu_tanh"], u_made(s, j))
                    if B and j < XB:
                        dve.wait_ge(sm["y_gated"], XB * r + j + 1)
                    if not B:
                        dve.wait_ge(sm["st_up"], 16)
                    V.scalar_tensor_tensor(u[:, j, :], th[:, TANH[B].index(("C", j)) % 2, :], 1.0, acc[:, j, :],
                                           ALU.add, ALU.mult).then_inc(sm["u_ready"], 1)
                elif kind == "YS":
                    y_sum(r, NQ - 1)
                elif kind == "Y":
                    if j == 0:
                        dve.wait_ge(sm["y_sum"], NQ * r + NQ)
                    link(V.scalar_tensor_tensor(y[:, j, :], u[:, j, :], dsk[:, j:j + 1], y[:, j, :],
                                                ALU.mult, ALU.add))
                    V.tensor_tensor(y[:, j, :], y[:, j, :], gz[:, j, :], ALU.mult).then_inc(sm["y_gated"], 1)
                elif kind == "XT":
                    if not B:
                        dve.wait_ge(sm["w_trans"], len(W_GROUPS))
                        link(V.memset(xpad[:].rearrange("p a b c -> p (a b c)"), 0.0))
                    pad_x(s, 0, pseg[1])
                elif kind == "FIN":
                    dve.wait_ge(sm["evac_done"], r + 1)
                    dve.wait_ge(sm["rms_ready"], r + 1)
                    dve.wait_ge(sm["o_used"], XB * r + XB)
                    for t in range(NQ):
                        last = V.scalar_tensor_tensor(res[:, t, :], po[t // 2][:, t % 2, :], rms[:, t:t + 1],
                                                      res[:, t, :], ALU.mult, ALU.add)
                    last.then_inc(sm["final_done"], 1)

            def body(s, A, B, more=True):
                r = s - 1
                for k in range(SLOTS[B] + 3):
                    q, g = divmod(k, G)
                    if B and k < NQ * G:
                        dve.wait_ge(sm["l_ready"], 32 * r + k + 1)
                        slot = lm[:, k % 4, :].rearrange("p (h l) -> p h l", h=4)
                        V.tensor_tensor(slot, slot, gm[:, q, :].unsqueeze(1).broadcast_to([P, 4, P]),
                                        ALU.mult).then_inc(sm["m_ready"], 1)
                        if g == 0 and q:
                            y_sum(r, q - 1)
                        if g == 4:
                            dve.wait_ge(sm["o_psum"], NQ * r + q + 1)
                            dve.wait_ge(sm["e_ready"], NQ * r + q + 1)
                            V.tensor_tensor(y[:, :, cols(q)], pm[:].rearrange("p (a l) -> p a l", a=XB), e_sb[:],
                                            ALU.mult).then_inc(sm["y_off"], 1)
                        if g == 6:
                            dve.wait_ge(sm["s_psum"], NQ * r + q + 1)
                            dve.wait_ge(sm["s_decayed"], NQ * r + q + 1)
                            V.tensor_tensor(state[q % 2][:], state[q % 2][:], pm[:],
                                            ALU.add).then_inc(sm["s_ready"], 1)
                        if g == 7 and q < NQ - 1:
                            pad_x(r, q + 1, pm)
                        if k == RESIDUAL_SLOT:
                            dve.wait_ge(sm["ld_res"], 32 * r + 32)
                            dve.wait_ge(sm["f_used"], FB * r + FB)
                            for t in range(2):
                                last = V.tensor_tensor(res[:, 2 * t:2 * t + 2, :], res[:, 2 * t:2 * t + 2, :], pd[t],
                                                       ALU.add)
                            last.then_inc(sm["evac_done"], 1)
                    if A and FILL[B].get(k - 3, NOTHING)[0] == "GU":
                        step(s, A, B, "GL", FILL[B][k - 3][1])
                    if A and k - 1 in FILL[B]:
                        step(s, A, B, *FILL[B][k - 1])
                    if A and not B and k == DOWN_SPLINE_SLOT:
                        down_spline()
                    if A and more and k == STAT_SLOT[B]:
                        layer_norm(s + 1)
                    if A and more and k == NORM_SLOT[B]:
                        normalize(s + 1)
                    if A and k == SCAN_SLOT[B]:
                        dve.wait_ge(sm["ad_ready"], s + 1)
                        for t in range(NQ):
                            c = slice(t * P, (t + 1) * P)
                            last = V.tensor_tensor_scan(acum[:, c], ones[0:R3, :], de[:, c], 0.0, ALU.mult, ALU.add)
                        last.then_inc(sm["scan_done"], 1)
                for kind, j in tail(DVE_TAIL, A, B):
                    step(s, A, B, kind, j)
                st.restart()

            body(0, True, False)
            with dve.Fori(1, NST - 1) as s:
                body(s, True, True)
            body(NST - 1, True, True, more=False)
            body(NST, False, True)

        @block.gpsimd
        def _(pool):
            st = Steps(pool, sm["pool_step"])
            Gp = nc.gpsimd

            def link(ins):
                st.did(ins)
                st.wait()

            def layer_norm_scale(s):
                pool.wait_ge(sm["var_ready"], s + 1)
                link(Gp.tensor_tensor(rstd[:], mv[:, :, 1], eps_1[:], ALU.add))
                Gp.tensor_tensor(rstd[:], rstd[:], half_neg[:], ALU.pow).then_inc(sm["rstd_ready"], 1)

            pool.wait_ge(sm["set_dve"], 7)
            layer_norm_scale(0)
            pool.wait_ge(sm["coef_ready"], 1)
            spline_rows(Gp, link, 1, wv_up, wp_up).then_inc(sm["spline_up"], 1)
            pool.wait_ge(sm["set_act"], 1)
            minus_one = half_neg[0:R3, 0:1]
            link(Gp.tensor_tensor(a_neg[:], a_neg[:], minus_one, ALU.mult))
            link(Gp.tensor_scalar(a_neg[:], a_neg[:], 2.0, None, ALU.mult))

            def split3(dst, src, tmp):
                link(Gp.tensor_tensor(dst[:], src[:], ones[0:R3, 0:1].broadcast_to([R3, ST]), ALU.mult))
                m = 2 * HEADS
                link(Gp.tensor_tensor(tmp[0:m, :], src[0:m, :], dst[0:m, :], ALU.subtract))
                link(Gp.tensor_scalar(dst[0:m, :], tmp[0:m, :], 1.0, None, ALU.mult))
                m = HEADS
                link(Gp.tensor_tensor(tmp[0:m, :], tmp[0:m, :], dst[0:m, :], ALU.subtract))
                return Gp.tensor_scalar(dst[0:m, :], tmp[0:m, :], 1.0, None, ALU.mult)

            def ssd_tile(r, q):
                pool.wait_ge(sm["xpad_ready"], NQ * r + q + 1)
                if q >= 2:
                    pool.wait_ge(sm["s_psum"], NQ * r + q - 1)
                src = bass.AP(xpad, (q % 2) * 2 * INTER,
                              [[4 * INTER, P], [4 * HDIM, HEADS // 2], [3 * HDIM, 2], [1, HDIM]])
                Gp.tensor_tensor(xdec[:, q % 2, :].rearrange("p (a b c) -> p a b c", b=2, c=HDIM), src,
                                 rep(tt[:, q, HEADS:], HDIM).rearrange("p (a b) c -> p a b c", b=2),
                                 ALU.mult).then_inc(sm["xdec_ready"], 1)
                pool.wait_ge(sm["o_psum"], NQ * r + q + 1)
                b = q % BATCH
                Gp.tensor_tensor(state[b][:].rearrange("p (h c) -> p h c", c=HDIM),
                                 state[b][:].rearrange("p (h c) -> p h c", c=HDIM),
                                 rep(etot[:, q, :], HDIM), ALU.mult).then_inc(sm["s_decayed"], 1)

            def body(s, A, B, more=True):
                r = s - 1
                if B:
                    ssd_tile(r, 0)
                if A:
                    pool.wait_ge(sm["dt_log"], s + 1)
                    one = ones[0:R3, 0:1].broadcast_to([R3, ST])
                    link(Gp.tensor_tensor(dw[:], de[:], one, ALU.add))
                    link(Gp.tensor_scalar(dw[:], dw[:], 1.0, None, ALU.subtract))
                    link(Gp.tensor_tensor(dw[:], de[:], dw[:], ALU.subtract))
                    link(Gp.tensor_scalar(dz[:], dz[:], 0.0, None, ALU.max))
                    link(Gp.tensor_tensor(dw[:], dw[:], dl[:], ALU.add))
                    link(Gp.tensor_tensor(dz[:], dz[:], dw[:], ALU.add))
                    link(Gp.tensor_scalar(dz[:], dz[:], 0.0, DT_MAX, ALU.max, ALU.min))
                    Gp.tensor_scalar(de[:], dz[:], a_neg[:], None, ALU.mult).then_inc(sm["ad_ready"], 1)
                    Gp.tensor_scalar(tt_f[0:HEADS, :], dz[0:HEADS, :], 0.5, None, ALU.mult).then_inc(sm["dt_ready"], 1)
                if B:
                    ssd_tile(r, 1)
                if A and more:
                    layer_norm_scale(s + 1)
                if B:
                    for q in range(2, NQ):
                        ssd_tile(r, q)
                if A:
                    pool.wait_ge(sm["exp_acum"], s + 1)
                    if B:
                        pool.wait_ge(sm["e_psum"], NQ * s)
                    split3(e3, dl, dw).then_inc(sm["e3_ready"], 1)
                    pool.wait_ge(sm["e3_ready"], s + 1)
                    if B:
                        pool.wait_ge(sm["seg_psum"], 32 * s)
                    link(split3(a3, acum, dw))
                    Gp.tensor_scalar(a3n[:], a3[:], -1.0, None, ALU.mult).then_inc(sm["a3_ready"], 1)
                if B:
                    pool.wait_ge(sm["sq_ready"], XB * r + 2)
                    Gp.tensor_tensor(sqs[:], xdec[:, 0, :], xdec[:, 1, :], ALU.add).then_inc(sm["sq_used"], 1)
                    for j in range(2, XB):
                        pool.wait_ge(sm["sq_ready"], XB * r + j + 1)
                        if j == 2:
                            pool.wait_ge(sm["sq_used"], r + 1)
                            link(Gp.tensor_tensor(sqs[:], sqs[:], xdec[:, 0, :], ALU.add))
                        else:
                            Gp.tensor_tensor(sqs[:], sqs[:], xdec[:, 1, :], ALU.add).then_inc(sm["sqs_ready"], 1)
                    pool.wait_ge(sm["ss_ready"], r + 1)
                    link(Gp.tensor_tensor(rms[:], ss_sb[:], eps_n[:], ALU.add))
                    link(Gp.tensor_tensor(rms[:], rms[:], half_neg[:], ALU.pow))
                    Gp.tensor_scalar(rms[:], rms[:], 0.5 * INTER ** 0.5, None, ALU.mult).then_inc(sm["rms_ready"], 1)
                st.restart()

            body(0, True, False)
            with pool.Fori(1, NST - 1) as s:
                body(s, True, True)
            body(NST - 1, True, True, more=False)
            body(NST, False, True)


def _constants():
    import numpy as np

    t = np.linspace(0.0, NCP - 1.0, NSAMP, dtype=np.float64)
    seg = np.clip(np.floor(t).astype(np.int64), 0, NCP - 2)
    f = (t - seg).astype(np.float32)
    n = np.arange(P * WROW)
    row, r = n // SEG, n % SEG
    real = n < NSAMP
    n = np.minimum(n, NSAMP - 1)
    prev = row - seg[n]
    assert np.isin(prev[real], (0, 1)).all() and (r[real & (prev == 1)] < 16).all()
    frac = np.where(real, f[n], np.float32(0)).astype(np.float32).reshape(P, WROW)
    mask = (real & (prev == 1)).astype(np.float32).reshape(P, RPP, SEG)[:, :, :16].reshape(P, RPP * 16)
    ident = np.eye(P, dtype=np.float32)
    bf16 = np.dtype("bfloat16")
    future = np.tril(np.full((P, P), -1e38, np.float32), -1).astype(bf16)
    row_of = np.tile(np.eye(HEADS, dtype=np.float32), (REP, 1))
    feature = np.repeat(row_of * np.float32(0.25), HDIM, axis=1).astype(bf16)
    return {"frac": frac, "prev_mask": np.ascontiguousarray(mask), "ident": ident,
            "ident_b": ident.astype(bf16), "future": future,
            "head": row_of.astype(bf16), "feature": feature}


def _layouts(w):
    import numpy as np

    def by_block(v):
        return np.ascontiguousarray(v.reshape(-1, P).T)

    in_w = w["in_proj_w"].T
    dt_w = in_w[:, -HEADS:]
    return {
        "hidden_states": w["hidden_states"],
        "in_proj_w": np.ascontiguousarray(np.concatenate([in_w[:, :-HEADS]] + [dt_w] * REP, axis=1)),
        "conv_w": np.ascontiguousarray(w["conv_w"].reshape(-1, P, CONV_K).transpose(1, 0, 2).reshape(P, -1)),
        "conv_b": by_block(w["conv_b"]),
        "A_log": w["A_log"].reshape(-1, 1),
        "dt_bias": w["dt_bias"].reshape(-1, 1),
        "D": by_block(np.repeat(w["D"], HDIM)),
        "norm_w": by_block(w["norm_w"]),
        "out_proj_w": np.ascontiguousarray(w["out_proj_w"].T),
    }


_INS = ["hidden_states", "in_proj_w", "conv_w", "conv_b", "A_log", "dt_bias", "D", "norm_w", "out_proj_w"]


def kernel(**inputs):
    import numpy as np
    import concourse.bacc as bacc
    from concourse.bass_utils import run_bass_kernel_spmd as run

    nc = bacc.Bacc("TRN2", target_bir_lowering=False, num_devices=1)
    arrays = _layouts({n: np.asarray(inputs[f"L0_attn_{n}"]) for n in _INS})
    for n in ("gate_cp", "up_cp", "down_cp"):
        cp = np.asarray(inputs[f"L0_ffn_{n}"])
        arrays[n] = np.concatenate([cp[:1]] * 2 + [cp] + [cp[-1:]] * (RPP * P + 4 - 2 - NCP))
    arrays.update(_constants())
    args = [nc.dram_tensor(f"in_{n}", a.shape, mybir.dt.from_np(a.dtype), kind="ExternalInput").ap()
            for n, a in arrays.items()]
    out = nc.dram_tensor("out_0", (BATCH, SEQ, HID), F32, kind="ExternalOutput").ap()
    mamba_ffn_kernel(nc, *args, out)
    r = run(nc, [{f"in_{n}": a for n, a in arrays.items()}], core_ids=[0])
    return r.results[0]["out_0"]
```

```python
from contextlib import ExitStack

import concourse.bass as bass
from concourse import mybir

ALU = mybir.AluOpType
ACT = mybir.ActivationFunctionType
F32 = mybir.dt.float32
F32R = mybir.dt.float32r
BF16 = mybir.dt.bfloat16

P = 128
BATCH, SEQ, HID = 2, 2048, 256
INTER, STATE, HEADS, CONV_K = 512, 128, 32, 4
HDIM = INTER // HEADS
FFN = 1024
EPS = 1e-5
DT_MAX = 100.0

ST_B = 256
ST = BATCH * ST_B
NST = SEQ // ST_B
NQ = ST // P
KT = HID // P
ZB = INTER // P
XB = INTER // P
CB = XB + 2
FB = FFN // P
G = 8
REP = 3
R3 = REP * HEADS

NCP = int(FFN * HID / 128.9)
NSAMP = FFN * HID
SEG = (NSAMP - 1) // (NCP - 1)
RPP = -(-(-(-NSAMP // SEG)) // P)
WROW = RPP * SEG

FILL_SSD = {0: ("T", 0), 2: ("DT", 0), 3: ("X", 0), 4: ("GU", 0), 7: ("X", 1), 9: ("GU", 1), 11: ("DN", 0),
            12: ("X", 2), 14: ("GU", 2), 16: ("DN", 1), 17: ("X", 3), 19: ("GU", 3), 20: ("DN", 2), 22: ("X", 4),
            24: ("GU", 4), 26: ("DN", 3), 27: ("X", 5), 29: ("GU", 5), 31: ("DN", 4)}
FILL_ALONE = dict(enumerate([
    ("T", 0), ("DT", 0), ("X", 0), ("W", "gate"), ("W", "up"), ("X", 1), ("GU", 0), ("C", 0), ("GU", 1),
    ("W", "down"), ("X", 2), ("DN", 0), ("GU", 2), ("C", 1), ("X", 3), ("DN", 1), ("C", 2), ("GU", 3), ("X", 4),
    ("GU", 4), ("DN", 2), ("C", 3), ("X", 5), ("DN", 3), ("C", 4), ("GU", 5), ("C", 5), ("DN", 4), ("GU", 6),
    ("Z", 0), ("Z", 1), ("DN", 5), ("Z", 2), ("GU", 7), ("DN", 6), ("Z", 3), ("DN", 7)]))
FILL = {True: FILL_SSD, False: FILL_ALONE}
SLOTS = {b: max(f) + 1 for b, f in FILL.items()}
SLOTS[True] = NQ * G
NOTHING = (None, 0)
DT_SLOT = {True: 2, False: 1}
LOG_SLOT = {True: 5, False: 4}
SCAN_SLOT = {True: 13, False: 12}
DECAY_SLOT = {True: 15, False: 14}
STAT_SLOT = {True: 8, False: 24}
NORM_SLOT = {True: 15, False: 30}
RESIDUAL_SLOT = 5
POOL_M = (3, 9, 12, 15, 17, 23, 25)
YD_LAG = 2
SPLINE_STEPS = 15
DOWN_SPLINE_SLOT = 1
NORM_PARTS_SLOT = 20

PE_TAIL = [("YD", 30), ("GU", 6), ("YD", 31), ("DN", 5), ("Z", 0), ("GU", 7), ("CB", 0), ("BT", 0), ("OUT", 0),
           ("Z", 1), ("DN", 6), ("Z", 2), ("OUT", 1), ("OUT", 2), ("DN", 7), ("SS", 0), ("ET", 0), ("Z", 3),
           ("DD", 0), ("OUT", 3), ("XT", 0)]
ACT_TAIL = [("GT", 6), ("CT", 4), ("CT", 5), ("ZT", 0), ("YH", 0), ("CT", 0), ("GT", 7), ("SQ", 0), ("GH", 6),
            ("YH", 1), ("SQ", 1), ("CT", 1), ("BT", 0), ("ZT", 1), ("YH", 2), ("SQ", 2), ("GH", 7), ("ZT", 2),
            ("CT", 2), ("YH", 3), ("SQ", 3), ("ET", 0), ("SS", 0), ("ZT", 3), ("CT", 3), ("DD", 0)]
DVE_TAIL = [("GM", 6), ("YS", 0), ("C", 4), ("Y", 0), ("C", 5), ("Z", 0), ("C", 0), ("Y", 1), ("GM", 7),
            ("GL", 6), ("CB", 0), ("Y", 2), ("C", 1), ("Z", 1), ("Y", 3), ("Z", 2), ("GL", 7), ("C", 2),
            ("YL", 3), ("Z", 3), ("C", 3), ("FIN", 0), ("XT", 0)]
SSD_PART = ("YD", "YS", "Y", "YH", "YL", "SQ", "OUT", "SS", "FIN")
START_PART = ("CB", "BT", "DD", "ET", "XT")


def tail(steps, A, B):
    if A and B:
        return steps
    return [t for t in steps if t[0] in (SSD_PART if B else START_PART)]


def pj_order(B):
    out = []
    for kind, j in [FILL[B][k] for k in sorted(FILL[B])] + tail(PE_TAIL, True, B):
        out += {"T": [("T", 0), ("T", 1)], "GU": [("GATE", j), ("UP", j)], "DT": [("DT", 0)], "X": [("X", j)],
                "Z": [("Z", j)]}.get(kind, [])
    return out


def tanh_order(B):
    names = {"GU": "GATE", "GT": "GATE", "Z": "Z", "ZT": "Z", "C": "C", "CT": "C"}
    steps = [FILL[B][k] for k in sorted(FILL[B])] + tail(ACT_TAIL, True, B)
    return [(names[kind], j) for kind, j in steps if kind in names]


PJ = {b: pj_order(b) for b in FILL}
TANH = {b: tanh_order(b) for b in FILL}
NPJ = len(PJ[True])
PJ_BANKS = {True: 2, False: 4}
assert NPJ == len(PJ[False])
BY_ACT = ("DT", "X")


def m_by_dve(k):
    return sum(i not in POOL_M for i in range(k + 1))


def pj_index(B, kind, j):
    return PJ[B].index((kind, j))


def pj_bank(B, kind, j):
    return pj_index(B, kind, j) % PJ_BANKS[B]


def pj_freed(B, upto, by_act):
    return sum((k in BY_ACT) == by_act for k, _ in PJ[B][:upto + 1])


N_ACT, N_DVE = pj_freed(True, NPJ - 1, True), pj_freed(True, NPJ - 1, False)


def pj_count(s, B, kind, j):
    by_act = kind in BY_ACT
    return (N_ACT if by_act else N_DVE) * s + pj_freed(B, pj_index(B, kind, j), by_act)


def pj_made(s, B, kind, j):
    return NPJ * s + pj_index(B, kind, j) + 1


def tanh_made(s, B, kind, j):
    order = [t for t in TANH[B] if t[0] != "C"]
    return len(order) * s + order.index((kind, j)) + 1


def u_made(s, B, j):
    return CB * s + [i for kind, i in TANH[B] if kind == "C"].index(j) + 1


def cols(q):
    c = (q % BATCH) * ST_B + (q // BATCH) * P
    return slice(c, c + P)


def head(g, j):
    return 8 * (g // 2) + 2 * j + g % 2


def w_groups():
    out = []
    for kind in ("gate", "up"):
        for k in range(KT):
            for a in range(0, FB, 4):
                out.append((kind, [(a + i, k) for i in range(4)]))
    for a in range(0, FB, 2):
        out.append(("down", [(a + i, b) for i in range(2) for b in range(KT)]))
    return out


W_GROUPS = w_groups()
W_FIRST = {k: [g[0] for g in W_GROUPS].index(k) for k in ("gate", "up", "down")}
N_CONST = 8 + 2 * REP


class Steps:

    def __init__(self, eng, sem):
        self.eng, self.sem, self.n, self.seen = eng, sem, 0, 0

    def did(self, ins):
        self.n += 1
        ins.then_inc(self.sem, 1)
        return self.n

    def wait(self, n=None):
        n = self.n if n is None else n
        if n > self.seen:
            self.eng.wait_ge(self.sem, n)
            self.seen = n

    def restart(self):
        self.wait()
        if self.n:
            self.eng.sem_clear(self.sem)
        self.n = self.seen = 0


def mamba_ffn_kernel(nc, x, in_w, conv_w, conv_b, a_log, dt_bias, d_skip, norm_w, out_w, gate_cp, up_cp, down_cp,
                     frac, prev_mask, ident_c, causal_c, head_c, feature_c, out):
    with ExitStack() as ctx:
        def sb(name, shape, dt=F32, c=ctx):
            return c.enter_context(nc.sbuf_tensor(name, shape, dt))

        def sem(name):
            return ctx.enter_context(nc.semaphore(name))

        NIN = INTER + CB * P + R3
        win_h, win_l = sb("win_h", [P, KT, NIN], F32R), sb("win_l", [P, KT, NIN], F32R)
        wgu_h, wgu_l = sb("wgu_h", [P, KT, 2 * FFN], F32R), sb("wgu_l", [P, KT, 2 * FFN], F32R)
        wdn_h, wdn_l = sb("wdn_h", [P, FB, HID], F32R), sb("wdn_l", [P, FB, HID], F32R)
        wo_h, wo_l = sb("wo_h", [P, XB, HID], F32R), sb("wo_l", [P, XB, HID], F32R)
        ident = sb("ident", [P, P])
        causal = sb("causal", [P, P])
        sel = sb("sel", [R3, HEADS], BF16)
        selq = sb("selq", [R3, INTER], BF16)
        ones = sb("ones", [P, P])
        half_neg = sb("half_neg", [P, NQ])
        eps_1 = sb("eps_1", [P, NQ])
        eps_n = sb("eps_n", [P, NQ])
        cw = sb("cw", [P, CB, CONV_K])
        cb = sb("cb", [P, CB])
        dtb = sb("dtb", [R3, 1])
        alog = sb("alog", [R3, 1])
        a_neg = sb("a_neg", [R3, 1])
        dsk = sb("dsk", [P, XB])
        nw = sb("nw", [P, XB])
        xin = sb("xin", [P, NQ, HID])
        stats = sb("stats", [P, NQ, 6])
        mv = sb("mv", [P, NQ, 2])
        rstd = sb("rstd", [P, NQ])
        xnt_h, xnt_l = sb("xnt_h", [P, KT, ST], F32R), sb("xnt_l", [P, KT, ST], F32R)
        pre = sb("pre", [P, 2, BATCH, CONV_K - 1 + ST_B])
        halo = sb("halo", [P, CB, BATCH, CONV_K - 1])
        acc = sb("acc", [P, CB, ST])
        u = sb("u", [P, CB, ST])
        th = sb("th", [P, 2, ST])
        gz = sb("gz", [P, ZB, ST])
        dz = sb("dz", [R3, ST])
        de = sb("de", [R3, ST])
        dl = sb("dl", [R3, ST])
        dw = sb("dw", [R3, ST])
        acum = sb("acum", [R3, ST])
        a3 = sb("a3", [R3, ST], BF16)
        a3n = sb("a3n", [R3, ST], BF16)
        e3 = sb("e3", [R3, ST], BF16)
        tt_f = sb("tt_f", [2 * HEADS, ST])
        res = sb("res", [P, NQ, HID])
        opn_h, opn_l = sb("opn_h", [P, 2, ST], F32R), sb("opn_l", [P, 2, ST], F32R)
        inter = sb("inter", [P, 2, ST])
        state = [sb(f"state{b}", [P, INTER]) for b in range(BATCH)]
        with ExitStack() as over:
            out_high = sb("out_high", [P, XB, ST], F32R, c=over)
            out_low = sb("out_low", [P, XB, ST], F32R, c=over)
        with ExitStack() as early:
            raw_in = sb("raw_in", [P, KT, NIN], c=early)
            raw_out = sb("raw_out", [P, XB, HID], c=early)
            fr = sb("fr", [P, RPP, SEG], c=early)
            mk = sb("mk", [P, RPP, 16], c=early)
            cpw = sb("cpw", [P, 3, RPP + 4], c=early)
            coef = sb("coef", [P, 4, 3, RPP + 1], c=early)
            ctmp = sb("ctmp", [P, 3, RPP + 1], c=early)
            wv = sb("wv", [P, RPP, SEG], c=early)
            wp = sb("wp", [P, RPP, 16], c=early)
        lm = sb("lm", [P, XB, 4 * P])
        y = sb("y", [P, XB, ST])
        tt = sb("tt", [P, NQ, 2 * HEADS])
        gm = sb("gm", [P, NQ, P])
        e_sb = sb("e_sb", [P, XB, P])
        xpad = sb("xpad", [P, 2, HEADS, 2 * HDIM])
        xdec = sb("xdec", [P, 2, INTER])
        b_tok = sb("b_tok", [P, NQ, STATE])
        etot = sb("etot", [P, NQ, HEADS])
        sqs = sb("sqs", [P, ST])
        ss_sb = sb("ss_sb", [P, NQ])
        rms = sb("rms", [P, NQ])
        u_flat = u[:, :, :].rearrange("p a b -> p (a b)")
        wv_up = u_flat[:, 0:WROW].rearrange("p (j r) -> p j r", r=SEG)
        wp_up = u_flat[:, WROW:WROW + RPP * 16].rearrange("p (j r) -> p j r", r=16)
        def square(j):
            return xdec[:, j, :] if j < 2 else acc[:, XB + j - 2, :]

        raw_w = {"gate": gz[:, :, :].rearrange("p a b -> p (a b)"),
                 "up": raw_in[:, :, :].rearrange("p a b -> p (a b)")[:, 0:NSAMP // P],
                 "down": fr[:, :, :].rearrange("p a b -> p (a b)")[:, 0:NSAMP // P]}
        KINDS = ("gate", "up", "down")
        W_BANKS = (6, 7, 0, 1)

        def weight_parts(kind, parts, ps):
            a0, b0 = parts[0]
            n = len(parts) * P
            if kind == "down":
                w = slice(a0, a0 + 2)
                return wdn_h[:, w, :], wdn_l[:, w, :], ps[:, :].rearrange("p (a h) -> p a h", a=2), 0.5
            o = (kind == "up") * FFN
            c = slice(o + a0 * P, o + a0 * P + n)
            return wgu_h[:, b0, c], wgu_l[:, b0, c], ps[:, 0:n], 1.0

        w_dram = [nc.dram_tensor(f"spline_w{i}", [P * WROW], F32, kind="Internal").ap() for i in range(3)]

        psum = [ctx.enter_context(nc.psum_tensor(f"ps{i}", [P, 512], F32)) for i in range(8)]
        pd = [psum[0][:].rearrange("p (t h) -> p t h", t=2), psum[1][:].rearrange("p (t h) -> p t h", t=2)]
        pj = [psum[2], psum[3], psum[4], psum[5]]
        pseg = [psum[4], psum[5]]
        py = psum[6]
        pm = psum[7]
        po = [psum[6][:].rearrange("p (t h) -> p t h", t=2), psum[7][:].rearrange("p (t h) -> p t h", t=2)]

        names = """ld_const ld_spline ld_in ld_out ld_x ld_res st_out
        st_gate st_up st_down ld_gate ld_up ld_down
        set_dve set_act pad_zero in_high in_low out_high w_trans w_high w_low
        coef_ready spline_gate spline_up first_down spline_down
        xn_ready var_ready rstd_ready xnt_high pj_done pj_act pj_dve
        tap_done silu_tanh u_ready gate_tanh f_high f_low o_high o_low o_low_last f_used o_used
        dt_exp dt_log ad_ready scan_done dt_ready decay_ready exp_acum a3_ready e3_ready
        tt_psum tt_ready g_psum gm_ready b_psum b_ready et_psum et_ready
        xt_psum xpad_ready xdec_ready seg_psum seg_read l_ready m_dve m_pool m_used
        e_psum e_ready o_psum y_off s_psum s_decayed s_ready y_sum
        y_gated sq_ready sqs_ready ss_psum ss_ready rms_ready evac_done po_free
        act_step dve_step pool_step""".split()
        sm = {n: sem(n) for n in names}

        def rep(ap, n):
            return ap.unsqueeze(len(ap.shape)).broadcast_to(list(ap.shape) + [n])

        x_st = x.rearrange("b (s h p) c -> b s p h c", p=P, h=ST_B // P)
        out_st = out.rearrange("b (s h p) c -> b s p h c", p=P, h=ST_B // P)
        HB = ST_B // P

        block = ctx.enter_context(nc.Block())

        def low_part(eng, j):
            return eng.tensor_tensor(out_low[:, j, :], y[:, j, :], out_high[:, j, :].bitcast(F32), ALU.subtract)

        def times_cb(eng, k):
            slot = lm[:, k % 4, :].rearrange("p (h l) -> p h l", h=4)
            return eng.tensor_tensor(slot, slot, gm[:, k // G, :].unsqueeze(1).broadcast_to([P, 4, P]), ALU.mult)

        def spline_step(eng, n, i, dst, first):
            if n < 6:
                out, f, m0, width = dst, fr[:], 1, SEG
            else:
                out, f, m0, width = first, fr[:, :, 0:16], 0, 16
            if n < 12:
                h = n % 6
                c = rep(coef[:, 3 - (h + 1) // 2, i, m0:m0 + RPP], width)
                if h % 2:
                    return eng.tensor_tensor(out, out, c, ALU.add)
                return eng.tensor_tensor(out, out if h else c, f, ALU.mult)
            if n == 12:
                return eng.tensor_tensor(first, first, dst[:, :, 0:16], ALU.subtract)
            if n == 13:
                return eng.tensor_tensor(first, first, mk[:], ALU.mult)
            return eng.tensor_tensor(dst[:, :, 0:16], dst[:, :, 0:16], first, ALU.add)

        @block.sync
        def _(sp):
            for b in range(BATCH):
                sp.dma_start(xin[:, b * HB:(b + 1) * HB, :], x_st[b, 0]).then_inc(sm["ld_x"], 16)
            for i, cp in enumerate((gate_cp, up_cp, down_cp)):
                window = bass.AP(cp.tensor, 0, [[RPP, P], [1, RPP + 4]])
                sp.dma_start(cpw[:, i, :], window).then_inc(sm["ld_spline"], 16)
            sp.dma_start(fr[:], frac.rearrange("p (j r) -> p j r", r=SEG)).then_inc(sm["ld_spline"], 16)
            sp.dma_start(mk[:], prev_mask.rearrange("p (j r) -> p j r", r=16)).then_inc(sm["ld_spline"], 16)
            sp.dma_start(raw_in[:], in_w.rearrange("(k p) f -> p k f", p=P)).then_inc(sm["ld_in"], 16)
            n = 0
            for dst, src in ((ident[:], ident_c), (causal[:], causal_c), (sel[:], head_c), (selq[:], feature_c),
                             (cw[:], conv_w.rearrange("p (j k) -> p j k", k=CONV_K)),
                             (cb[:], conv_b), (nw[:], norm_w), (dsk[:], d_skip)):
                sp.dma_start(dst, src).then_inc(sm["ld_const"], 16)
                n += 1
            for c in range(REP):
                rr = slice(c * HEADS, (c + 1) * HEADS)
                sp.dma_start(dtb[rr, :], dt_bias).then_inc(sm["ld_const"], 16)
                sp.dma_start(alog[rr, :], a_log).then_inc(sm["ld_const"], 16)
                n += 2
            assert n == N_CONST
            sp.dma_start(raw_out[:], out_w.rearrange("(j p) h -> p j h", p=P)).then_inc(sm["ld_out"], 16)
            for b in range(BATCH):
                sp.dma_start(res[:, b * HB:(b + 1) * HB, :], x_st[b, 0]).then_inc(sm["ld_res"], 16)
            for i, kind in enumerate(KINDS):
                sp.wait_ge(sm[f"spline_{kind}"], 1)
                src = wv_up if kind == "up" else wv[:]
                sp.dma_start(w_dram[i].rearrange("(p j r) -> p j r", p=P, r=SEG), src).then_inc(sm[f"st_{kind}"], 16)
                sp.wait_ge(sm[f"st_{kind}"], 16)
                if kind == "up":
                    sp.wait_ge(sm["in_low"], 1)
                wide = FFN if kind == "down" else HID
                rows = w_dram[i][0:NSAMP].rearrange("(b p h) -> p b h", p=P, h=wide)
                sp.dma_start(raw_w[kind].rearrange("p (n h) -> p n h", h=wide), rows).then_inc(sm[f"ld_{kind}"], 16)

            def load_x(s):
                sp.wait_ge(sm["pj_done"], NPJ * (s - 1) + KT)
                for b in range(BATCH):
                    sp.dma_start(xin[:, b * HB:(b + 1) * HB, :], x_st[b, s]).then_inc(sm["ld_x"], 16)

            def store(r):
                sp.wait_ge(sm["po_free"], r + 2)
                for b in range(BATCH):
                    sp.dma_start(out_st[b, r], res[:, b * HB:(b + 1) * HB, :]).then_inc(sm["st_out"], 16)
                sp.wait_ge(sm["st_out"], 32 * (r + 1))

            def load_res(s):
                for b in range(BATCH):
                    sp.dma_start(res[:, b * HB:(b + 1) * HB, :], x_st[b, s]).then_inc(sm["ld_res"], 16)

            load_x(1)
            with sp.Fori(1, NST - 1) as s:
                load_x(s + 1)
                store(s - 1)
                load_res(s)
            store(NST - 2)
            load_res(NST - 1)
            store(NST - 1)

        @block.tensor
        def _(pe):
            pe.wait_ge(sm["ld_const"], 16 * N_CONST)

            def weights(kind):
                pe.wait_ge(sm[f"ld_{kind}"], 16)
                raw = raw_w[kind]
                for n, (k, parts) in enumerate(W_GROUPS):
                    if k != kind:
                        continue
                    nb = len(W_BANKS)
                    if n >= nb:
                        pe.wait_ge(sm["w_low"], n - nb + 1)
                    for i, (a, b) in enumerate(parts):
                        c = b * FFN + a * P if kind == "down" else a * HID + b * P
                        last = nc.tensor.transpose(psum[W_BANKS[n % nb]][:, i * P:(i + 1) * P], raw[:, c:c + P],
                                                   ident[:])
                    last.then_inc(sm["w_trans"], 1)

            def pj_free(s, B, kind, j):
                n = pj_index(B, kind, j)
                if n >= PJ_BANKS[B]:
                    before = PJ[B][n - PJ_BANKS[B]]
                    pe.wait_ge(sm["pj_act" if before[0] in BY_ACT else "pj_dve"], pj_count(s, B, *before))
                elif B:
                    pe.wait_ge(sm["pj_dve"], N_DVE * s)

            def project(s, B, kind, j, w_h, w_l, c0, m):
                pj_free(s, B, kind, j)
                bank = pj[pj_bank(B, kind, j)]
                n = 0
                for k in range(KT):
                    for w, a in ((w_h, xnt_h), (w_h, xnt_l), (w_l, xnt_h)):
                        last = nc.tensor.matmul(bank[0:m, :], w[:, k, c0:c0 + m], a[:, k, :],
                                                start=(n == 0), stop=(n == 3 * KT - 1))
                        n += 1
                last.then_inc(sm["pj_done"], 1)

            def down(high, low, j, w_h, w_l, banks, n_blocks, used):
                for t in range(NQ):
                    tc = slice(t * P, (t + 1) * P)
                    for n, (a, w) in enumerate(((high, w_h), (high, w_l), (low, w_h))):
                        last = nc.tensor.matmul(banks[t // 2][:, t % 2, :], a[:, tc], w[:, j, :],
                                                start=(j == 0 and t % 2 == 0 and n == 0),
                                                stop=(j == n_blocks - 1 and n == 2), skip_group_check=True)
                last.then_inc(sm[used], 1)

            def seg(r, k):
                q, g = divmod(k, G)
                bank = pseg[k % 2]
                if k == 0:
                    pe.wait_ge(sm["a3_ready"], r + 1)
                    pe.wait_ge(sm["ss_ready"], r + 1)
                    pe.wait_ge(sm["tt_ready"], r + 1)
                if k == 1:
                    pe.wait_ge(sm["xpad_ready"], NQ * r + 1)
                if k >= 2:
                    pe.wait_ge(sm["seg_read"], 32 * r + k - 1)
                c = cols(q)
                heads = sel[:, 8 * (g // 2) + g % 2:8 * (g // 2) + 8:2]
                nc.tensor.matmul(bank[:, :].rearrange("p (h l) -> p h l", h=4), a3n[:, c], rep(heads, P),
                                 start=True, stop=False, skip_group_check=True)
                for j in range(4):
                    h = head(g, j)
                    last = nc.tensor.matmul(bank[:, j * P:(j + 1) * P], sel[:, h:h + 1].broadcast_to([R3, P]),
                                            a3[:, c], start=False, stop=True, skip_group_check=True)
                last.then_inc(sm["seg_psum"], 1)

            def yd(r, k):
                q, g = divmod(k, G)
                if k in POOL_M:
                    pe.wait_ge(sm["m_pool"], len(POOL_M) * r + POOL_M.index(k) + 1)
                else:
                    pe.wait_ge(sm["m_dve"], m_by_dve(NQ * G - 1) * r + m_by_dve(k))
                if g == 0:
                    pe.wait_ge(sm["xpad_ready"], NQ * r + q + 1)
                    if q:
                        pe.wait_ge(sm["y_sum"], NQ * r + q)
                    else:
                        pe.wait_ge(sm["po_free"], r + 1)
                for j in range(4):
                    last = nc.tensor.matmul(py[32 * j:32 * j + 32, (g // 2) * P:(g // 2 + 1) * P],
                                            xpad[:, q % 2, head(g, j), :], lm[:, k % 4, j * P:(j + 1) * P],
                                            start=(g % 2 == 0), stop=(g % 2 == 1), skip_group_check=True)
                last.then_inc(sm["m_used"], 1)

            def x_tok(q, bank):
                for j in range(XB):
                    last = nc.tensor.transpose(bank[:, j * P:(j + 1) * P], u[:, j, cols(q)], ident[:])
                last.then_inc(sm["xt_psum"], 1)

            def step(s, A, B, kind, j):
                r = s - 1
                if kind == "T":
                    pe.wait_ge(sm["xn_ready"], s * NQ + NQ)
                    for k in range(KT):
                        pj_free(s, B, "T", k)
                        for t in range(NQ):
                            last = nc.tensor.transpose(pj[k][:, t * P:(t + 1) * P],
                                                       xin[:, t, k * P:(k + 1) * P], ident[:])
                        last.then_inc(sm["pj_done"], 1)
                elif kind == "W":
                    weights(j)
                elif kind == "DT":
                    pe.wait_ge(sm["pj_dve"], pj_count(s, B, "T", KT - 1))
                    if not B:
                        pe.wait_ge(sm["in_low"], 1)
                    project(s, B, "DT", 0, win_h, win_l, INTER + CB * P, R3)
                elif kind == "X":
                    project(s, B, "X", j, win_h, win_l, INTER + j * P, P)
                elif kind == "Z":
                    project(s, B, "Z", j, win_h, win_l, j * P, P)
                elif kind == "GU":
                    if not B:
                        pe.wait_ge(sm["w_low"], W_FIRST["down"])
                    project(s, B, "GATE", j, wgu_h, wgu_l, j * P, P)
                    project(s, B, "UP", j, wgu_h, wgu_l, FFN + j * P, P)
                elif kind == "DN":
                    if j == 0:
                        if B:
                            pe.wait_ge(sm["evac_done"], s)
                        else:
                            pe.wait_ge(sm["w_low"], len(W_GROUPS))
                    pe.wait_ge(sm["f_low"], FB * s + j + 1)
                    down(opn_h[:, j % 2, :], opn_l[:, j % 2, :], j, wdn_h, wdn_l, pd, FB, "f_used")
                elif kind == "OUT":
                    if j == 0:
                        pe.wait_ge(sm["y_sum"], NQ * r + NQ)
                        pe.wait_ge(sm["s_ready"], NQ * r + NQ)
                    if j < XB - 1:
                        pe.wait_ge(sm["o_low"], (XB - 1) * r + j + 1)
                    else:
                        pe.wait_ge(sm["o_low_last"], r + 1)
                    down(out_high[:, j, :], out_low[:, j, :], j, wo_h, wo_l, po, XB, "o_used")
                elif kind == "YD":
                    yd(r, j)
                elif kind == "SS":
                    pe.wait_ge(sm["sqs_ready"], r + 1)
                    pe.wait_ge(sm["seg_read"], 32 * (r + 1))
                    if A:
                        pe.wait_ge(sm["gm_ready"], s + 1)
                    for t in range(NQ):
                        last = nc.tensor.matmul(pseg[0][:, t:t + 1], sqs[:, t * P:(t + 1) * P], ones[:, 0:1],
                                                start=True, stop=True)
                    last.then_inc(sm["ss_psum"], 1)
                elif kind == "CB":
                    pe.wait_ge(sm["u_ready"], u_made(s, B, XB + 1))
                    if B:
                        pe.wait_ge(sm["seg_read"], 32 * s)
                    else:
                        pe.wait_ge(sm["pj_dve"], N_DVE)
                        pe.wait_ge(sm["pj_act"], N_ACT)
                    for q in range(NQ):
                        last = nc.tensor.matmul(pseg[0][:, q * P:(q + 1) * P], u[:, XB, cols(q)],
                                                u[:, XB + 1, cols(q)], start=True, stop=True)
                    last.then_inc(sm["g_psum"], 1)
                elif kind == "BT":
                    for q in range(NQ):
                        last = nc.tensor.transpose(pseg[1][:, q * P:(q + 1) * P], u[:, XB, cols(q)], ident[:])
                    last.then_inc(sm["b_psum"], 1)
                elif kind == "DD":
                    if B:
                        pe.wait_ge(sm["ss_ready"], s + 1)
                    pe.wait_ge(sm["gm_ready"], s + 1)
                    pe.wait_ge(sm["dt_ready"], s + 1)
                    pe.wait_ge(sm["decay_ready"], NQ * s + NQ)
                    for q in range(NQ):
                        last = nc.tensor.matmul(pseg[0][:, q * 2 * HEADS:(q + 1) * 2 * HEADS], tt_f[:, cols(q)],
                                                ident[0:2 * HEADS, 0:2 * HEADS], start=True, stop=True)
                    last.then_inc(sm["tt_psum"], 1)
                elif kind == "ET":
                    pe.wait_ge(sm["b_ready"], s + 1)
                    pe.wait_ge(sm["e3_ready"], s + 1)
                    for q in range(NQ):
                        end = cols(q).stop
                        last = nc.tensor.matmul(pseg[1][:, q * HEADS:(q + 1) * HEADS],
                                                e3[:, end - 1:end].broadcast_to([R3, P]), sel[:, :],
                                                start=True, stop=True)
                    last.then_inc(sm["et_psum"], 1)
                elif kind == "XT":
                    pe.wait_ge(sm["et_ready"], s + 1)
                    pe.wait_ge(sm["u_ready"], CB * s + CB)
                    x_tok(0, pseg[1])

            def body(s, A, B):
                r = s - 1
                for k in range(SLOTS[B]):
                    q, g = divmod(k, G)
                    if B:
                        seg(r, k)
                    if A and k in FILL[B]:
                        step(s, A, B, *FILL[B][k])
                    if B:
                        if k >= YD_LAG:
                            yd(r, k - YD_LAG)
                        if g == 1:
                            pe.wait_ge(sm["xpad_ready"], NQ * r + q + 1)
                            if not q:
                                pe.wait_ge(sm["po_free"], r + 1)
                            for j in range(XB):
                                last = nc.tensor.matmul(pm[:, j * P:(j + 1) * P], selq[:, j * P:(j + 1) * P],
                                                        e3[:, cols(q)], start=True, stop=True)
                            last.then_inc(sm["e_psum"], 1)
                        if g == 3:
                            pe.wait_ge(sm["e_ready"], NQ * r + q + 1)
                            if q >= 2:
                                pe.wait_ge(sm["s_ready"], NQ * r + q - 1)
                            for j in range(XB):
                                last = nc.tensor.matmul(pm[:, j * P:(j + 1) * P],
                                                        state[q % BATCH][:, j * P:(j + 1) * P],
                                                        u[:, XB + 1, cols(q)], start=True, stop=True)
                            last.then_inc(sm["o_psum"], 1)
                        if g == 5:
                            pe.wait_ge(sm["y_off"], NQ * r + q + 1)
                            pe.wait_ge(sm["xdec_ready"], NQ * r + q + 1)
                            nc.tensor.matmul(pm[:, :], b_tok[:, q, :], xdec[:, q % 2, :],
                                             start=True, stop=True).then_inc(sm["s_psum"], 1)
                        if g == 7 and q < NQ - 1:
                            pe.wait_ge(sm["s_ready"], NQ * r + q + 1)
                            x_tok(q + 1, pm)
                for kind, j in tail(PE_TAIL, A, B):
                    step(s, A, B, kind, j)

            body(0, True, False)
            with pe.Fori(1, NST) as s:
                body(s, True, True)
            body(NST, False, True)

        @block.scalar
        def _(act):
            st = Steps(act, sm["act_step"])
            act.wait_ge(sm["ld_const"], 16 * N_CONST)
            nc.scalar.activation(ss_sb[:], ident[:, 0:NQ], ACT.Copy).then_inc(sm["ss_ready"], 1)
            nc.scalar.activation(a_neg[:], alog[:], ACT.Exp).then_inc(sm["set_act"], 1)
            act.wait_ge(sm["ld_in"], 16)
            nc.scalar.activation(win_h[:], raw_in[:], ACT.Copy).then_inc(sm["in_high"], 1)
            act.wait_ge(sm["ld_out"], 16)
            for j in range(XB):
                nc.scalar.activation(wo_h[:, j, :], raw_out[:, j, :], ACT.Identity,
                                     scale=nw[:, j:j + 1]).then_inc(sm["out_high"], 1)

            def weights(kind):
                for n, (k, parts) in enumerate(W_GROUPS):
                    if k == kind:
                        act.wait_ge(sm["w_trans"], n + 1)
                        w_h, w_l, ps, scale = weight_parts(kind, parts, psum[W_BANKS[n % len(W_BANKS)]])
                        nc.scalar.activation(w_h, ps, ACT.Copy, scale=scale).then_inc(sm["w_high"], 1)

            def tanh_slot(s, B, kind, j):
                i = TANH[B].index((kind, j))
                before = TANH[B][i - 2] if i >= 2 else None
                if before is None:
                    if B:
                        act.wait_ge(sm["u_ready"], CB * s)
                        act.wait_ge(sm["pj_dve"], N_DVE * s)
                elif before[0] == "C":
                    act.wait_ge(sm["u_ready"], u_made(s, B, before[1]))
                else:
                    act.wait_ge(sm["pj_dve"], pj_count(s, B, *before))
                return th[:, i % 2, :]

            def pj_tanh(s, B, kind, j):
                act.wait_ge(sm["pj_done"], pj_made(s, B, kind, j))
                slot = tanh_slot(s, B, kind, j)
                nc.scalar.activation(slot, pj[pj_bank(B, kind, j)][:], ACT.Tanh,
                                     scale=0.5).then_inc(sm["gate_tanh"], 1)

            def step(s, A, B, kind, j):
                r = s - 1
                if kind == "T":
                    for k in range(KT):
                        act.wait_ge(sm["pj_done"], pj_made(s, B, "T", k))
                        if B:
                            act.wait_ge(sm["pj_done"], NPJ * s)
                        nc.scalar.activation(xnt_h[:, k, :], pj[k][:], ACT.Copy).then_inc(sm["xnt_high"], 1)
                elif kind == "W":
                    weights(j)
                elif kind == "DT":
                    act.wait_ge(sm["pj_done"], pj_made(s, B, "DT", 0))
                    if B:
                        act.wait_ge(sm["a3_ready"], s)
                    nc.scalar.activation(dz[:], pj[pj_bank(B, "DT", 0)][0:R3, :], ACT.Identity,
                                         bias=dtb[:]).then_inc(sm["pj_act"], 1)
                elif kind == "X":
                    act.wait_ge(sm["pj_done"], pj_made(s, B, "X", j))
                    if j >= 2 or B:
                        act.wait_ge(sm["tap_done"], CB * s + j - 1)
                    if j == 0 and B:
                        act.wait_ge(sm["u_ready"], CB * s)
                    bank = pj[pj_bank(B, "X", j)]
                    batches = bank[:].rearrange("p (b t) -> p b t", b=BATCH)
                    n = st.did(nc.scalar.activation(pre[:, j % 2, :, 0:CONV_K - 1], halo[:, j], ACT.Copy))
                    nc.scalar.activation(pre[:, j % 2, :, CONV_K - 1:], batches, ACT.Copy)
                    nc.scalar.activation(acc[:, j, :], bank[:], ACT.Identity, bias=cb[:, j:j + 1],
                                         scale=cw[:, j, CONV_K - 1:CONV_K])
                    st.wait(n)
                    nc.scalar.activation(halo[:, j], batches[:, :, ST_B - CONV_K + 1:],
                                         ACT.Copy).then_inc(sm["pj_act"], 1)
                elif kind in ("GU", "GT"):
                    pj_tanh(s, B, "GATE", j)
                elif kind in ("Z", "ZT"):
                    pj_tanh(s, B, "Z", j)
                elif kind in ("C", "CT"):
                    act.wait_ge(sm["tap_done"], CB * s + j + 1)
                    slot = tanh_slot(s, B, "C", j)
                    nc.scalar.activation(slot, acc[:, j, :], ACT.Tanh, scale=0.5).then_inc(sm["silu_tanh"], 1)
                elif kind == "GH":
                    act.wait_ge(sm["pj_dve"], pj_count(s, B, "UP", j))
                    if j >= 2 or B:
                        act.wait_ge(sm["f_used"], FB * s + j - 1)
                    nc.scalar.activation(opn_h[:, j % 2, :], inter[:, j % 2, :], ACT.Copy).then_inc(sm["f_high"], 1)
                elif kind == "YH":
                    act.wait_ge(sm["y_gated"], XB * r + j + 1)
                    act.wait_ge(sm["m_used"], 32 * r + 29 + j)
                    nc.scalar.activation(out_high[:, j, :], y[:, j, :], ACT.Copy).then_inc(sm["o_high"], 1)
                elif kind == "SQ":
                    if j < 2:
                        act.wait_ge(sm["s_psum"], NQ * r + NQ)
                    elif A:
                        act.wait_ge(sm["u_ready"], u_made(s, B, XB + j - 2))
                    nc.scalar.activation(square(j), y[:, j, :], ACT.Square, scale=0.5).then_inc(sm["sq_ready"], 1)
                elif kind == "SS":
                    act.wait_ge(sm["ss_psum"], r + 1)
                    nc.scalar.activation(ss_sb[:], pseg[0][:, 0:NQ], ACT.Copy).then_inc(sm["ss_ready"], 1)
                elif kind == "BT":
                    act.wait_ge(sm["b_psum"], s + 1)
                    nc.scalar.activation(b_tok[:].rearrange("p a b -> p (a b)"), pseg[1][:],
                                         ACT.Copy).then_inc(sm["b_ready"], 1)
                elif kind == "DD":
                    act.wait_ge(sm["tt_psum"], s + 1)
                    nc.scalar.activation(tt[:].rearrange("p a b -> p (a b)"), pseg[0][:, 0:NQ * 2 * HEADS],
                                         ACT.Copy).then_inc(sm["tt_ready"], 1)
                elif kind == "ET":
                    act.wait_ge(sm["et_psum"], s + 1)
                    nc.scalar.activation(etot[:].rearrange("p a b -> p (a b)"), pseg[1][:, 0:NQ * HEADS],
                                         ACT.Copy).then_inc(sm["et_ready"], 1)

            def body(s, A, B):
                r = s - 1
                for k in range(SLOTS[B] + 2):
                    q, g = divmod(k, G)
                    if B and k < NQ * G:
                        act.wait_ge(sm["seg_psum"], 32 * r + k + 1)
                        if k >= 4:
                            act.wait_ge(sm["m_used"], 32 * r + k - 3)
                        slot = lm[:, k % 4, :]
                        nc.scalar.activation(slot, pseg[k % 2][:], ACT.Relu, scale=-1.0).then_inc(sm["seg_read"], 1)
                        act.wait_ge(sm["seg_read"], 32 * r + k + 1)
                        nc.scalar.activation(slot, slot, ACT.Exp, scale=-1.0).then_inc(sm["l_ready"], 1)
                        if g == 2:
                            act.wait_ge(sm["e_psum"], NQ * r + q + 1)
                            if q:
                                act.wait_ge(sm["y_off"], NQ * r + q)
                            nc.scalar.activation(e_sb[:].rearrange("p a b -> p (a b)"), pm[:],
                                                 ACT.Copy).then_inc(sm["e_ready"], 1)
                    if A and FILL[B].get(k - 2, NOTHING)[0] == "GU":
                        step(s, A, B, "GH", FILL[B][k - 2][1])
                    if A and k in FILL[B]:
                        step(s, A, B, *FILL[B][k])
                    if A and k == DT_SLOT[B] + 1:
                        act.wait_ge(sm["pj_act"], pj_count(s, B, "DT", 0))
                        st.did(nc.scalar.activation(dw[:], dz[:], ACT.Abs))
                    if A and k == DT_SLOT[B] + 2:
                        st.wait()
                        nc.scalar.activation(de[:], dw[:], ACT.Exp, scale=-1.0).then_inc(sm["dt_exp"], 1)
                    if A and k == LOG_SLOT[B]:
                        act.wait_ge(sm["dt_exp"], s + 1)
                        nc.scalar.activation(dl[:], de[:], ACT.Ln, bias=1.0).then_inc(sm["dt_log"], 1)
                    t = k - DECAY_SLOT[B]
                    if A and t == 0:
                        act.wait_ge(sm["scan_done"], s + 1)
                    if A and 0 <= t < NQ:
                        c = slice(t * P, (t + 1) * P)
                        nc.scalar.activation(tt_f[HEADS:2 * HEADS, c], acum[HEADS:2 * HEADS, c], ACT.Exp, scale=-1.0,
                                             bias=acum[HEADS:2 * HEADS, c.stop - 1:c.stop]).then_inc(
                                                 sm["decay_ready"], 1)
                    if A and t == NQ:
                        nc.scalar.activation(dl[:], acum[:], ACT.Exp).then_inc(sm["exp_acum"], 1)
                for kind, j in tail(ACT_TAIL, A, B):
                    step(s, A, B, kind, j)
                st.restart()

            body(0, True, False)
            with act.Fori(1, NST) as s:
                body(s, True, True)
            body(NST, False, True)

        @block.vector
        def _(dve):
            st = Steps(dve, sm["dve_step"])

            def link(ins):
                st.did(ins)
                st.wait()

            V = nc.vector
            V.memset(ones[:], 1.0).then_inc(sm["set_dve"], 1)
            V.memset(halo[:].rearrange("p a b c -> p (a b c)"), 0.0).then_inc(sm["set_dve"], 1)
            V.memset(state[0][:], 0.0).then_inc(sm["set_dve"], 1)
            V.memset(state[1][:], 0.0).then_inc(sm["po_free"], 1)
            for t, v in ((half_neg, -0.5), (eps_1, EPS), (eps_n, EPS * INTER)):
                V.memset(t[:], v).then_inc(sm["set_dve"], 1)

            def token_stats(s, t):
                if t == 0:
                    dve.wait_ge(sm["ld_x"], 32 * s + 32)
                st.did(V.bn_stats(stats[:, t, :], xin[:, t, :]))
                if t == NQ - 1:
                    st.wait()
                    for i in range(NQ):
                        last = V.bn_aggr(mv[:, i, :], stats[:, i, :])
                    last.then_inc(sm["var_ready"], 1)

            def normalize(s, t):
                if t == 0:
                    dve.wait_ge(sm["rstd_ready"], s + 1)
                V.tensor_scalar(xin[:, t, :], xin[:, t, :], mv[:, t, 0:1], rstd[:, t:t + 1],
                                ALU.subtract, ALU.mult).then_inc(sm["xn_ready"], 1)

            for t in range(NQ):
                token_stats(0, t)
            dve.wait_ge(sm["ld_spline"], 16 * 5)
            p0, p1, p2, p3 = (cpw[:, :, k:k + RPP + 1] for k in range(4))
            c0, c1, c2, c3 = (coef[:, k] for k in range(4))
            tmp = ctmp[:]
            st.did(V.tensor_copy(c0, p1))
            link(V.tensor_tensor(tmp, p2, p0, ALU.subtract))
            link(V.tensor_scalar(c1, tmp, 0.5, None, ALU.mult))
            link(V.scalar_tensor_tensor(tmp, p0, 2.0, p3, ALU.mult, ALU.subtract))
            link(V.scalar_tensor_tensor(tmp, p1, -5.0, tmp, ALU.mult, ALU.add))
            link(V.scalar_tensor_tensor(tmp, p2, 4.0, tmp, ALU.mult, ALU.add))
            link(V.tensor_scalar(c2, tmp, 0.5, None, ALU.mult))
            link(V.tensor_tensor(tmp, p3, p0, ALU.subtract))
            link(V.scalar_tensor_tensor(tmp, p1, 3.0, tmp, ALU.mult, ALU.add))
            link(V.scalar_tensor_tensor(tmp, p2, -3.0, tmp, ALU.mult, ALU.add))
            V.tensor_scalar(c3, tmp, 0.5, None, ALU.mult).then_inc(sm["coef_ready"], 1)
            for t in range(NQ):
                normalize(0, t)
            dve.wait_ge(sm["coef_ready"], 1)
            for n in range(SPLINE_STEPS - 1):
                link(spline_step(V, n, 0, wv[:], wp[:]))
            spline_step(V, SPLINE_STEPS - 1, 0, wv[:], wp[:]).then_inc(sm["spline_gate"], 1)
            dve.wait_ge(sm["in_high"], 1)
            V.tensor_tensor(win_l[:], raw_in[:], win_h[:].bitcast(F32), ALU.subtract).then_inc(sm["in_low"], 1)

            def down_spline():
                dve.wait_ge(sm["st_gate"], 16)
                dve.wait_ge(sm["spline_gate"], 1)
                for n in range(6):
                    link(spline_step(V, n, 2, wv[:], wp_up))
                dve.wait_ge(sm["first_down"], 1)
                for n in range(12, SPLINE_STEPS - 1):
                    link(spline_step(V, n, 2, wv[:], wp_up))
                spline_step(V, SPLINE_STEPS - 1, 2, wv[:], wp_up).then_inc(sm["spline_down"], 1)

            def norm_parts():
                dve.wait_ge(sm["out_high"], XB)
                for j in range(XB):
                    V.scalar_tensor_tensor(wo_l[:, j, :], raw_out[:, j, :], nw[:, j:j + 1],
                                           wo_h[:, j, :].bitcast(F32), ALU.mult, ALU.subtract)
                st.did(V.tensor_scalar(dsk[:], dsk[:], 0.5, None, ALU.mult))

            def weights(kind):
                for n, (k, parts) in enumerate(W_GROUPS):
                    if k == kind:
                        dve.wait_ge(sm["w_high"], n + 1)
                        w_h, w_l, ps, scale = weight_parts(kind, parts, psum[W_BANKS[n % len(W_BANKS)]])
                        V.scalar_tensor_tensor(w_l, ps, scale, w_h.bitcast(F32), ALU.mult,
                                               ALU.subtract).then_inc(sm["w_low"], 1)

            def pad_x(r, q, bank):
                dve.wait_ge(sm["xt_psum"], NQ * r + q + 1)
                if q == 0:
                    dve.wait_ge(sm["tt_ready"], r + 1)
                dst = bass.AP(xpad, (q % 2) * 2 * INTER,
                              [[4 * INTER, P], [4 * HDIM, HEADS // 2], [3 * HDIM, 2], [1, HDIM]])
                V.tensor_tensor(dst, bank[:].rearrange("p (a b c) -> p a b c", a=HEADS // 2, b=2),
                                rep(tt[:, q, 0:HEADS], HDIM).rearrange("p (a b) c -> p a b c", b=2),
                                ALU.mult).then_inc(sm["xpad_ready"], 1)

            def y_sum(r, q):
                dve.wait_ge(sm["m_used"], 32 * r + G * q + G)
                dve.wait_ge(sm["y_off"], NQ * r + q + 1)
                V.tensor_tensor(y[:, :, cols(q)], y[:, :, cols(q)], py[:].rearrange("p (a l) -> p a l", a=XB),
                                ALU.add).then_inc(sm["y_sum"], 1)

            tapped = {}

            def tap(s, B, j, k):
                if k == CONV_K - 2:
                    dve.wait_ge(sm["pj_act"], pj_count(s, B, "X", j))
                else:
                    st.wait(tapped[j])
                a = acc[:, j, :].rearrange("p (b t) -> p b t", b=BATCH)
                ins = V.scalar_tensor_tensor(a, pre[:, j % 2, :, k:k + ST_B], cw[:, j, k:k + 1], a, ALU.mult, ALU.add)
                if k:
                    tapped[j] = st.did(ins)
                else:
                    ins.then_inc(sm["tap_done"], 1)

            def step(s, A, B, kind, j):
                r = s - 1
                if kind == "T":
                    for k in range(KT):
                        dve.wait_ge(sm["xnt_high"], KT * s + k + 1)
                        V.tensor_tensor(xnt_l[:, k, :], pj[k][:], xnt_h[:, k, :].bitcast(F32),
                                        ALU.subtract).then_inc(sm["pj_dve"], 1)
                elif kind == "W":
                    weights(j)
                elif kind in ("GU", "GM"):
                    dve.wait_ge(sm["gate_tanh"], tanh_made(s, B, "GATE", j))
                    if j >= 2:
                        dve.wait_ge(sm["f_low"], FB * s + j - 1)
                    V.scalar_tensor_tensor(inter[:, j % 2, :], th[:, TANH[B].index(("GATE", j)) % 2, :], 1.0,
                                           pj[pj_bank(B, "GATE", j)][:], ALU.add,
                                           ALU.mult).then_inc(sm["pj_dve"], 1)
                    dve.wait_ge(sm["pj_dve"], pj_count(s, B, "GATE", j))
                    dve.wait_ge(sm["pj_done"], pj_made(s, B, "UP", j))
                    V.tensor_tensor(inter[:, j % 2, :], inter[:, j % 2, :], pj[pj_bank(B, "UP", j)][:],
                                    ALU.mult).then_inc(sm["pj_dve"], 1)
                elif kind == "GL":
                    dve.wait_ge(sm["f_high"], FB * s + j + 1)
                    i = j % 2
                    V.tensor_tensor(opn_l[:, i, :], inter[:, i, :], opn_h[:, i, :].bitcast(F32),
                                    ALU.subtract).then_inc(sm["f_low"], 1)
                elif kind == "YL":
                    dve.wait_ge(sm["o_high"], XB * r + j + 1)
                    dve.wait_ge(sm["sq_ready"], XB * r + j + 1)
                    low_part(V, j).then_inc(sm["o_low_last"], 1)
                elif kind == "CB":
                    dve.wait_ge(sm["g_psum"], s + 1)
                    V.scalar_tensor_tensor(gm[:], pseg[0][:].rearrange("p (q l) -> p q l", q=NQ), 0.25,
                                           causal[:].unsqueeze(1).broadcast_to([P, NQ, P]),
                                           ALU.mult, ALU.mult).then_inc(sm["gm_ready"], 1)
                elif kind == "Z":
                    dve.wait_ge(sm["gate_tanh"], tanh_made(s, B, "Z", j))
                    if B:
                        dve.wait_ge(sm["y_gated"], XB * r + j + 1)
                    V.scalar_tensor_tensor(gz[:, j, :], th[:, TANH[B].index(("Z", j)) % 2, :], 1.0,
                                           pj[pj_bank(B, "Z", j)][:], ALU.add, ALU.mult).then_inc(sm["pj_dve"], 1)
                elif kind == "C":
                    dve.wait_ge(sm["silu_tanh"], u_made(s, B, j))
                    if B and j < XB:
                        dve.wait_ge(sm["y_gated"], XB * r + j + 1)
                    if not B:
                        dve.wait_ge(sm["st_up"], 16)
                        dve.wait_ge(sm["spline_down"], 1)
                    V.scalar_tensor_tensor(u[:, j, :], th[:, TANH[B].index(("C", j)) % 2, :], 1.0, acc[:, j, :],
                                           ALU.add, ALU.mult).then_inc(sm["u_ready"], 1)
                elif kind == "YS":
                    y_sum(r, NQ - 1)
                elif kind == "Y":
                    if j == 0:
                        dve.wait_ge(sm["y_sum"], NQ * r + NQ)
                    link(V.scalar_tensor_tensor(y[:, j, :], u[:, j, :], dsk[:, j:j + 1], y[:, j, :],
                                                ALU.mult, ALU.add))
                    V.tensor_tensor(y[:, j, :], y[:, j, :], gz[:, j, :], ALU.mult).then_inc(sm["y_gated"], 1)
                elif kind == "XT":
                    if not B:
                        dve.wait_ge(sm["pad_zero"], 1)
                    pad_x(s, 0, pseg[1])
                elif kind == "FIN":
                    dve.wait_ge(sm["evac_done"], r + 1)
                    dve.wait_ge(sm["rms_ready"], r + 1)
                    dve.wait_ge(sm["o_used"], XB * r + XB)
                    for t in range(NQ):
                        last = V.scalar_tensor_tensor(res[:, t, :], po[t // 2][:, t % 2, :], rms[:, t:t + 1],
                                                      res[:, t, :], ALU.mult, ALU.add)
                    last.then_inc(sm["po_free"], 1)

            def body(s, A, B, more=True):
                r = s - 1
                for k in range(SLOTS[B] + 3):
                    q, g = divmod(k, G)
                    if A and k == 0:
                        step(s, A, B, "T", 0)
                    if B and k < NQ * G:
                        if g == 4:
                            dve.wait_ge(sm["o_psum"], NQ * r + q + 1)
                            dve.wait_ge(sm["e_ready"], NQ * r + q + 1)
                            V.tensor_tensor(y[:, :, cols(q)], pm[:].rearrange("p (a l) -> p a l", a=XB), e_sb[:],
                                            ALU.mult).then_inc(sm["y_off"], 1)
                        if g == 6:
                            dve.wait_ge(sm["s_psum"], NQ * r + q + 1)
                            dve.wait_ge(sm["s_decayed"], NQ * r + q + 1)
                            V.tensor_tensor(state[q % 2][:], state[q % 2][:], pm[:],
                                            ALU.add).then_inc(sm["s_ready"], 1)
                        if k not in POOL_M:
                            dve.wait_ge(sm["l_ready"], 32 * r + k + 1)
                            times_cb(V, k).then_inc(sm["m_dve"], 1)
                        if g == YD_LAG - 1 and q:
                            y_sum(r, q - 1)
                        if g == 7 and q < NQ - 1:
                            pad_x(r, q + 1, pm)
                        if k == RESIDUAL_SLOT:
                            dve.wait_ge(sm["ld_res"], 32 * r + 32)
                            dve.wait_ge(sm["f_used"], FB * r + FB)
                            for t in range(2):
                                last = V.tensor_tensor(res[:, 2 * t:2 * t + 2, :], res[:, 2 * t:2 * t + 2, :], pd[t],
                                                       ALU.add)
                            last.then_inc(sm["evac_done"], 1)
                    if A and FILL[B].get(k - 3, NOTHING)[0] == "GU":
                        step(s, A, B, "GL", FILL[B][k - 3][1])
                    if A and k > 1 and FILL[B].get(k - 1, NOTHING)[0] not in (None, "X"):
                        step(s, A, B, *FILL[B][k - 1])
                    for k_tap in range(CONV_K - 1):
                        item = FILL[B].get(k - 1 - (CONV_K - 2 - k_tap), NOTHING)
                        if A and item[0] == "X":
                            tap(s, B, item[1], k_tap)
                    if not B:
                        if k == DOWN_SPLINE_SLOT:
                            down_spline()
                        if k == NORM_PARTS_SLOT:
                            norm_parts()
                    if A and more and 0 <= k - STAT_SLOT[B] < NQ:
                        token_stats(s + 1, k - STAT_SLOT[B])
                    if A and more and 0 <= k - NORM_SLOT[B] < NQ:
                        normalize(s + 1, k - NORM_SLOT[B])
                    if A and k == SCAN_SLOT[B]:
                        dve.wait_ge(sm["ad_ready"], s + 1)
                        for t in range(NQ):
                            c = slice(t * P, (t + 1) * P)
                            last = V.tensor_tensor_scan(acum[:, c], ones[0:R3, :], de[:, c], 0.0, ALU.mult, ALU.add)
                        last.then_inc(sm["scan_done"], 1)
                for kind, j in tail(DVE_TAIL, A, B):
                    step(s, A, B, kind, j)
                st.restart()

            body(0, True, False)
            with dve.Fori(1, NST - 1) as s:
                body(s, True, True)
            body(NST - 1, True, True, more=False)
            body(NST, False, True)

        @block.gpsimd
        def _(pool):
            st = Steps(pool, sm["pool_step"])
            Gp = nc.gpsimd

            def link(ins):
                st.did(ins)
                st.wait()

            def layer_norm_scale(s):
                pool.wait_ge(sm["var_ready"], s + 1)
                link(Gp.tensor_tensor(rstd[:], mv[:, :, 1], eps_1[:], ALU.add))
                Gp.tensor_tensor(rstd[:], rstd[:], half_neg[:], ALU.pow).then_inc(sm["rstd_ready"], 1)

            pool.wait_ge(sm["set_dve"], 6)
            layer_norm_scale(0)
            pool.wait_ge(sm["coef_ready"], 1)
            for n in range(SPLINE_STEPS - 1):
                link(spline_step(Gp, n, 1, wv_up, wp_up))
            spline_step(Gp, SPLINE_STEPS - 1, 1, wv_up, wp_up).then_inc(sm["spline_up"], 1)
            pool.wait_ge(sm["spline_up"], 1)
            for n in range(6, 11):
                link(spline_step(Gp, n, 2, wv[:], wp_up))
            spline_step(Gp, 11, 2, wv[:], wp_up).then_inc(sm["first_down"], 1)
            pool.wait_ge(sm["set_act"], 1)
            link(Gp.tensor_tensor(a_neg[:], a_neg[:], half_neg[0:R3, 0:1], ALU.mult))
            link(Gp.tensor_scalar(a_neg[:], a_neg[:], 2.0, None, ALU.mult))

            def split3(dst, src, tmp):
                def rounded(m, a):
                    return Gp.tensor_tensor(dst[0:m, :], a[0:m, :], ones[0:m, 0:1].broadcast_to([m, ST]), ALU.mult)

                link(rounded(R3, src))
                m = 2 * HEADS
                link(Gp.tensor_tensor(tmp[0:m, :], src[0:m, :], dst[0:m, :], ALU.subtract))
                link(rounded(m, tmp))
                m = HEADS
                link(Gp.tensor_tensor(tmp[0:m, :], tmp[0:m, :], dst[0:m, :], ALU.subtract))
                return rounded(m, tmp)

            def decayed_x(r, q):
                pool.wait_ge(sm["xpad_ready"], NQ * r + q + 1)
                if q >= 2:
                    pool.wait_ge(sm["s_psum"], NQ * r + q - 1)
                src = bass.AP(xpad, (q % 2) * 2 * INTER,
                              [[4 * INTER, P], [4 * HDIM, HEADS // 2], [3 * HDIM, 2], [1, HDIM]])
                Gp.tensor_tensor(xdec[:, q % 2, :].rearrange("p (a b c) -> p a b c", b=2, c=HDIM), src,
                                 rep(tt[:, q, HEADS:], HDIM).rearrange("p (a b) c -> p a b c", b=2),
                                 ALU.mult).then_inc(sm["xdec_ready"], 1)

            def decay_state(r, q):
                pool.wait_ge(sm["o_psum"], NQ * r + q + 1)
                b = q % BATCH
                Gp.tensor_tensor(state[b][:].rearrange("p (h c) -> p h c", c=HDIM),
                                 state[b][:].rearrange("p (h c) -> p h c", c=HDIM),
                                 rep(etot[:, q, :], HDIM), ALU.mult).then_inc(sm["s_decayed"], 1)

            def log_correction(s):
                pool.wait_ge(sm["dt_exp"], s + 1)
                one = ones[0:R3, 0:1].broadcast_to([R3, ST])
                link(Gp.tensor_tensor(dw[:], de[:], one, ALU.add))
                link(Gp.tensor_tensor(dw[:], dw[:], one, ALU.subtract))
                link(Gp.tensor_tensor(dw[:], de[:], dw[:], ALU.subtract))
                link(Gp.tensor_scalar(dz[:], dz[:], 0.0, None, ALU.max))
                link(Gp.tensor_tensor(dz[:], dz[:], dw[:], ALU.add))

            def time_steps(s):
                pool.wait_ge(sm["dt_log"], s + 1)
                link(Gp.tensor_tensor(dz[:], dz[:], dl[:], ALU.add))
                link(Gp.tensor_scalar(dz[:], dz[:], 0.0, DT_MAX, ALU.max, ALU.min))
                Gp.tensor_tensor(de[:], dz[:], a_neg[:, 0:1].broadcast_to([R3, ST]),
                                 ALU.mult).then_inc(sm["ad_ready"], 1)
                Gp.tensor_scalar(tt_f[0:HEADS, :], dz[0:HEADS, :], 0.5, None, ALU.mult).then_inc(sm["dt_ready"], 1)

            def body(s, A, B, more=True):
                r = s - 1
                for k in range(NQ * G):
                    q, g = divmod(k, G)
                    if B and k in POOL_M:
                        pool.wait_ge(sm["l_ready"], 32 * r + k + 1)
                        times_cb(Gp, k).then_inc(sm["m_pool"], 1)
                    if B and g == 0:
                        decayed_x(r, q)
                    if B and g == 3:
                        decay_state(r, q)
                    if A and k == DT_SLOT[True] + 2:
                        log_correction(s)
                    if A and k == LOG_SLOT[True]:
                        time_steps(s)
                    if A and more and k == STAT_SLOT[True] + NQ:
                        layer_norm_scale(s + 1)
                if A:
                    pool.wait_ge(sm["exp_acum"], s + 1)
                    if B:
                        pool.wait_ge(sm["e_psum"], NQ * s)
                    split3(e3, dl, dw).then_inc(sm["e3_ready"], 1)
                    pool.wait_ge(sm["e3_ready"], s + 1)
                    if B:
                        pool.wait_ge(sm["seg_psum"], 32 * s)
                    link(split3(a3, acum, dw))
                    Gp.tensor_scalar(a3n[:], a3[:], -1.0, None, ALU.mult).then_inc(sm["a3_ready"], 1)
                if not B:
                    pool.wait_ge(sm["w_trans"], len(W_GROUPS))
                    Gp.memset(xpad[:].rearrange("p a b c -> p (a b c)"), 0.0).then_inc(sm["pad_zero"], 1)
                if B:
                    def y_low(j):
                        pool.wait_ge(sm["o_high"], XB * r + j + 1)
                        pool.wait_ge(sm["sq_ready"], XB * r + j + 1)
                        low_part(Gp, j).then_inc(sm["o_low"], 1)

                    y_low(0)
                    y_low(1)
                    link(Gp.tensor_tensor(sqs[:], square(0), square(1), ALU.add))
                    y_low(2)
                    link(Gp.tensor_tensor(sqs[:], sqs[:], square(2), ALU.add))
                    pool.wait_ge(sm["sq_ready"], XB * r + 4)
                    Gp.tensor_tensor(sqs[:], sqs[:], square(3), ALU.add).then_inc(sm["sqs_ready"], 1)
                    pool.wait_ge(sm["ss_ready"], r + 2)
                    link(Gp.tensor_tensor(rms[:], ss_sb[:], eps_n[:], ALU.add))
                    link(Gp.tensor_tensor(rms[:], rms[:], half_neg[:], ALU.pow))
                    Gp.tensor_scalar(rms[:], rms[:], 0.5 * INTER ** 0.5, None, ALU.mult).then_inc(sm["rms_ready"], 1)
                st.restart()

            body(0, True, False)
            with pool.Fori(1, NST - 1) as s:
                body(s, True, True)
            body(NST - 1, True, True, more=False)
            body(NST, False, True)


def _constants():
    import numpy as np

    t = np.linspace(0.0, NCP - 1.0, NSAMP, dtype=np.float64)
    seg = np.clip(np.floor(t).astype(np.int64), 0, NCP - 2)
    f = (t - seg).astype(np.float32)
    n = np.arange(P * WROW)
    row, r = n // SEG, n % SEG
    real = n < NSAMP
    n = np.minimum(n, NSAMP - 1)
    prev = row - seg[n]
    assert np.isin(prev[real], (0, 1)).all() and (r[real & (prev == 1)] < 16).all()
    frac = np.where(real, f[n], np.float32(0)).astype(np.float32).reshape(P, WROW)
    mask = (real & (prev == 1)).astype(np.float32).reshape(P, RPP, SEG)[:, :, :16].reshape(P, RPP * 16)
    ident = np.eye(P, dtype=np.float32)
    bf16 = np.dtype("bfloat16")
    causal = np.triu(np.ones((P, P), np.float32))
    row_of = np.tile(np.eye(HEADS, dtype=np.float32), (REP, 1))
    feature = np.repeat(row_of * np.float32(0.25), HDIM, axis=1).astype(bf16)
    return {"frac": frac, "prev_mask": np.ascontiguousarray(mask), "ident": ident,
            "causal": causal, "head": row_of.astype(bf16), "feature": feature}


def _layouts(w):
    import numpy as np

    def by_block(v):
        return np.ascontiguousarray(v.reshape(-1, P).T)

    in_w = w["in_proj_w"].T
    dt_w = in_w[:, -HEADS:]
    return {
        "hidden_states": w["hidden_states"],
        "in_proj_w": np.ascontiguousarray(np.concatenate([in_w[:, :-HEADS]] + [dt_w] * REP, axis=1)),
        "conv_w": np.ascontiguousarray(w["conv_w"].reshape(-1, P, CONV_K).transpose(1, 0, 2).reshape(P, -1)),
        "conv_b": by_block(w["conv_b"]),
        "A_log": w["A_log"].reshape(-1, 1),
        "dt_bias": w["dt_bias"].reshape(-1, 1),
        "D": by_block(np.repeat(w["D"], HDIM)),
        "norm_w": by_block(w["norm_w"]),
        "out_proj_w": np.ascontiguousarray(w["out_proj_w"].T),
    }


_INS = ["hidden_states", "in_proj_w", "conv_w", "conv_b", "A_log", "dt_bias", "D", "norm_w", "out_proj_w"]


def kernel(**inputs):
    import numpy as np
    import concourse.bacc as bacc
    from concourse.bass_utils import run_bass_kernel_spmd as run

    nc = bacc.Bacc("TRN2", target_bir_lowering=False, num_devices=1)
    arrays = _layouts({n: np.asarray(inputs[f"L0_attn_{n}"]) for n in _INS})
    for n in ("gate_cp", "up_cp", "down_cp"):
        cp = np.asarray(inputs[f"L0_ffn_{n}"])
        arrays[n] = np.concatenate([cp[:1]] * 2 + [cp] + [cp[-1:]] * (RPP * P + 4 - 2 - NCP))
    arrays.update(_constants())
    args = [nc.dram_tensor(f"in_{n}", a.shape, mybir.dt.from_np(a.dtype), kind="ExternalInput").ap()
            for n, a in arrays.items()]
    out = nc.dram_tensor("out_0", (BATCH, SEQ, HID), F32, kind="ExternalOutput").ap()
    mamba_ffn_kernel(nc, *args, out)
    r = run(nc, [{f"in_{n}": a for n, a in arrays.items()}], core_ids=[0])
    return r.results[0]["out_0"]
```
